# Optimizing a Trainium2 kernel written in Bass

```python
import numpy as np
import jax
import jax.numpy as jnp

def _softmax(x, axis=-1):
    return jax.nn.softmax(x, axis=axis)

def _gelu(x):
    return jax.nn.gelu(x, approximate=True)

def _silu(x):
    return jax.nn.silu(x)

def _sigmoid(x):
    return jax.nn.sigmoid(x)

def _layernorm(x, axis=-1, eps=1e-05):
    m = jnp.mean(x, axis=axis, keepdims=True)
    v = jnp.var(x, axis=axis, keepdims=True)
    return (x - m) / jnp.sqrt(v + eps)

def _scatter_add(tgt, idx, src, axis=0):
    return tgt.at[idx].add(src)

def _segment_sum(src, seg, n):
    return jax.ops.segment_sum(src, seg, n)
kernel_name = 'mk_seq_preln_d1_jaxref_r8_75e587'

def setup_inputs(seed: int=0):
    np.random.seed(seed)
    _w = jnp.asarray

    def _L0_attn_setup():
        import jax, jax.numpy as jnp
        import numpy as np
        NUM_STEPS = 3
        NUM_HEADS = 8
        HEAD_DIM = 128
        EPS = 1e-05

        def layernorm(x, g, b):
            mu = jnp.mean(x, -1, keepdims=True)
            var = jnp.mean(jnp.square(x - mu), -1, keepdims=True)
            return (x - mu) * jax.lax.rsqrt(var + EPS) * g + b

        def entmax15(x):
            x = (x - jnp.max(x, -1, keepdims=True)) / 2.0
            xs = jnp.flip(jnp.sort(x, -1), -1)
            rho = jnp.arange(1, x.shape[-1] + 1, dtype=x.dtype)
            mean = jnp.cumsum(xs, -1) / rho
            meansq = jnp.cumsum(xs * xs, -1) / rho
            ss = rho * (meansq - jnp.square(mean))
            tau = mean - jnp.sqrt(jnp.clip((1.0 - ss) / rho, 0.0, None))
            support = jnp.sum(tau <= xs, -1, keepdims=True)
            tau_star = jnp.take_along_axis(tau, support - 1, -1)
            return jnp.square(jnp.clip(x - tau_star, 0.0, None))
        key = jax.random.key(seed)
        ks = jax.random.split(key, 6)
        B, S, Hd, Md, N = (2, 128, 256, 128, 256)
        THD = NUM_HEADS * HEAD_DIM
        return {'hidden': jax.random.normal(ks[0], (B, S, Hd), jnp.float32), 'memory': jax.random.normal(ks[1], (N, Md), jnp.float32), 'Wq': jax.random.normal(ks[2], (THD, Hd), jnp.float32) / np.float32(np.sqrt(Hd)), 'Wk': jax.random.normal(ks[3], (THD, Md), jnp.float32) / np.float32(np.sqrt(Md)), 'Wv': jax.random.normal(ks[4], (THD, Md), jnp.float32) / np.float32(np.sqrt(Md)), 'Wo': jax.random.normal(ks[5], (Hd, THD), jnp.float32) / np.float32(np.sqrt(THD)), 'log_beta': jnp.full((NUM_HEADS,), float(np.log(1.0 / np.sqrt(HEAD_DIM))), jnp.float32), 'g_state': jnp.ones((Hd,), jnp.float32), 'b_state': jnp.zeros((Hd,), jnp.float32), 'g_mem': jnp.ones((Md,), jnp.float32), 'b_mem': jnp.zeros((Md,), jnp.float32)}
    _L0_attn_in = _L0_attn_setup()

    def _L0_ffn_setup():
        import jax, jax.numpy as jnp
        import numpy as np
        B, S, D = (2, 256, 256)
        H, HD = (16, 128)
        E, K, I = (16, 6, 176)
        SI = 352
        EPS = 1e-06

        def rmsnorm(x, w):
            v = jnp.mean(jnp.square(x), axis=-1, keepdims=True)
            return x * jax.lax.rsqrt(v + EPS) * w
        key = jax.random.key(seed)
        ks = jax.random.split(key, 14)
        s = 0.02
        return {'hidden_states': jax.random.normal(ks[0], (B, S, D), jnp.float32), 'ln1_w': jnp.ones((D,), jnp.float32), 'ln2_w': jnp.ones((D,), jnp.float32), 'wq': jax.random.normal(ks[1], (D, H * HD), jnp.float32) * s, 'wk': jax.random.normal(ks[2], (D, H * HD), jnp.float32) * s, 'wv': jax.random.normal(ks[3], (D, H * HD), jnp.float32) * s, 'wo': jax.random.normal(ks[4], (H * HD, D), jnp.float32) * s, 'gate_w': jax.random.normal(ks[5], (E, D), jnp.float32) * s, 'eg_w': jax.random.normal(ks[6], (E, I, D), jnp.float32) * s, 'eu_w': jax.random.normal(ks[7], (E, I, D), jnp.float32) * s, 'ed_w': jax.random.normal(ks[8], (E, D, I), jnp.float32) * s, 'sg_w': jax.random.normal(ks[9], (SI, D), jnp.float32) * s, 'su_w': jax.random.normal(ks[10], (SI, D), jnp.float32) * s, 'sd_w': jax.random.normal(ks[11], (D, SI), jnp.float32) * s}
    _L0_ffn_in = _L0_ffn_setup()
    _d = {'L0_attn_hidden': _L0_attn_in['hidden'], 'L0_attn_memory': _L0_attn_in['memory'], 'L0_attn_Wq': _L0_attn_in['Wq'], 'L0_attn_Wk': _L0_attn_in['Wk'], 'L0_attn_Wv': _L0_attn_in['Wv'], 'L0_attn_Wo': _L0_attn_in['Wo'], 'L0_attn_log_beta': _L0_attn_in['log_beta'], 'L0_attn_g_state': _L0_attn_in['g_state'], 'L0_attn_b_state': _L0_attn_in['b_state'], 'L0_attn_g_mem': _L0_attn_in['g_mem'], 'L0_attn_b_mem': _L0_attn_in['b_mem'], 'L0_ffn_ln1_w': _L0_ffn_in['ln1_w'], 'L0_ffn_ln2_w': _L0_ffn_in['ln2_w'], 'L0_ffn_wq': _L0_ffn_in['wq'], 'L0_ffn_wk': _L0_ffn_in['wk'], 'L0_ffn_wv': _L0_ffn_in['wv'], 'L0_ffn_wo': _L0_ffn_in['wo'], 'L0_ffn_gate_w': _L0_ffn_in['gate_w'], 'L0_ffn_eg_w': _L0_ffn_in['eg_w'], 'L0_ffn_eu_w': _L0_ffn_in['eu_w'], 'L0_ffn_ed_w': _L0_ffn_in['ed_w'], 'L0_ffn_sg_w': _L0_ffn_in['sg_w'], 'L0_ffn_su_w': _L0_ffn_in['su_w'], 'L0_ffn_sd_w': _L0_ffn_in['sd_w']}
    _x0 = _d['L0_attn_hidden']
    _d['L0_attn_hidden'] = jax.random.normal(jax.random.fold_in(jax.random.key(seed), 1), (4, 512, 256), dtype=_x0.dtype)
    del _x0
    return _d

def reference(L0_attn_hidden, L0_attn_memory, L0_attn_Wq, L0_attn_Wk, L0_attn_Wv, L0_attn_Wo, L0_attn_log_beta, L0_attn_g_state, L0_attn_b_state, L0_attn_g_mem, L0_attn_b_mem, L0_ffn_ln1_w, L0_ffn_ln2_w, L0_ffn_wq, L0_ffn_wk, L0_ffn_wv, L0_ffn_wo, L0_ffn_gate_w, L0_ffn_eg_w, L0_ffn_eu_w, L0_ffn_ed_w, L0_ffn_sg_w, L0_ffn_su_w, L0_ffn_sd_w):

    def _L0_attn_ref(hidden, memory, Wq, Wk, Wv, Wo, log_beta, g_state, b_state, g_mem, b_mem):
        import jax, jax.numpy as jnp
        import numpy as np
        NUM_STEPS = 3
        NUM_HEADS = 8
        HEAD_DIM = 128
        EPS = 1e-05

        def layernorm(x, g, b):
            mu = jnp.mean(x, -1, keepdims=True)
            var = jnp.mean(jnp.square(x - mu), -1, keepdims=True)
            return (x - mu) * jax.lax.rsqrt(var + EPS) * g + b

        def entmax15(x):
            x = (x - jnp.max(x, -1, keepdims=True)) / 2.0
            xs = jnp.flip(jnp.sort(x, -1), -1)
            rho = jnp.arange(1, x.shape[-1] + 1, dtype=x.dtype)
            mean = jnp.cumsum(xs, -1) / rho
            meansq = jnp.cumsum(xs * xs, -1) / rho
            ss = rho * (meansq - jnp.square(mean))
            tau = mean - jnp.sqrt(jnp.clip((1.0 - ss) / rho, 0.0, None))
            support = jnp.sum(tau <= xs, -1, keepdims=True)
            tau_star = jnp.take_along_axis(tau, support - 1, -1)
            return jnp.square(jnp.clip(x - tau_star, 0.0, None))
        B, S, _ = hidden.shape
        N = memory.shape[0]
        H, hd = (NUM_HEADS, HEAD_DIM)
        Q = layernorm(hidden, g_state, b_state) @ Wq.T
        mn = layernorm(memory, g_mem, b_mem)
        K = (mn @ Wk.T).reshape(N, H, hd).transpose(1, 0, 2)
        V = (mn @ Wv.T).reshape(N, H, hd).transpose(1, 0, 2)
        xi = Q.reshape(B, S, H, hd).transpose(0, 2, 1, 3)
        beta = jnp.exp(log_beta)[None, :, None, None]
        for _ in range(NUM_STEPS):
            scores = jnp.einsum('bhsd,hnd->bhsn', xi, K) * beta
            w = entmax15(scores)
            xi = jnp.einsum('bhsn,hnd->bhsd', w, V)
        out = xi.transpose(0, 2, 1, 3).reshape(B, S, H * hd) @ Wo.T
        return out

    def _L0_ffn_ref(hidden_states, ln1_w, ln2_w, wq, wk, wv, wo, gate_w, eg_w, eu_w, ed_w, sg_w, su_w, sd_w):
        import jax, jax.numpy as jnp
        import numpy as np
        B, S, D = (2, 256, 256)
        H, HD = (16, 128)
        E, K, I = (16, 6, 176)
        SI = 352
        EPS = 1e-06

        def rmsnorm(x, w):
            v = jnp.mean(jnp.square(x), axis=-1, keepdims=True)
            return x * jax.lax.rsqrt(v + EPS) * w
        b, s, d = hidden_states.shape
        x = hidden_states
        h = rmsnorm(x, ln1_w)
        q = (h @ wq).reshape(b, s, H, HD)
        k = (h @ wk).reshape(b, s, H, HD)
        v = (h @ wv).reshape(b, s, H, HD)
        scores = jnp.einsum('bqhd,bkhd->bhqk', q, k) / np.sqrt(HD).astype(np.float32)
        causal = jnp.tril(jnp.ones((s, s), bool))
        scores = jnp.where(causal, scores, jnp.float32(-1000000000.0))
        attn = jax.nn.softmax(scores, axis=-1)
        ao = jnp.einsum('bhqk,bkhd->bqhd', attn, v).reshape(b, s, H * HD) @ wo
        x = x + ao
        h = rmsnorm(x, ln2_w)
        t = h.reshape(-1, d)
        T = t.shape[0]
        logits = t @ gate_w.T
        probs = jax.nn.softmax(logits, axis=-1)
        topv, topi = jax.lax.top_k(probs, K)
        topv = topv / jnp.sum(topv, axis=-1, keepdims=True)
        cw = jnp.zeros((T, E), t.dtype).at[jnp.arange(T)[:, None], topi].add(topv)
        g = jnp.einsum('td,eid->eti', t, eg_w)
        u = jnp.einsum('td,eid->eti', t, eu_w)
        hh = jax.nn.silu(g) * u
        routed = jnp.einsum('eti,edi,te->td', hh, ed_w, cw)
        shared = jax.nn.silu(t @ sg_w.T) * (t @ su_w.T) @ sd_w.T
        out = x + (routed + shared).reshape(b, s, d)
        return out
    x = L0_attn_hidden
    x = x + _L0_attn_ref(_layernorm(x, axis=-1), L0_attn_memory, L0_attn_Wq, L0_attn_Wk, L0_attn_Wv, L0_attn_Wo, L0_attn_log_beta, L0_attn_g_state, L0_attn_b_state, L0_attn_g_mem, L0_attn_b_mem)
    x = x + _L0_ffn_ref(_layernorm(x, axis=-1), L0_ffn_ln1_w, L0_ffn_ln2_w, L0_ffn_wq, L0_ffn_wk, L0_ffn_wv, L0_ffn_wo, L0_ffn_gate_w, L0_ffn_eg_w, L0_ffn_eu_w, L0_ffn_ed_w, L0_ffn_sg_w, L0_ffn_su_w, L0_ffn_sd_w)
    return x

_drawn_inputs = setup_inputs


def setup_inputs(seed=0):
    import zlib

    import numpy as np

    out = dict(_drawn_inputs(seed))
    spreads = {'L0_attn_log_beta': (-2.4260151386260986, 0.2),
     'L0_attn_g_state': (1.0, 0.2),
     'L0_attn_b_state': (0.0, 0.1),
     'L0_attn_g_mem': (1.0, 0.2),
     'L0_attn_b_mem': (0.0, 0.1),
     'L0_ffn_ln1_w': (1.0, 0.6),
     'L0_ffn_ln2_w': (1.0, 0.6)}
    factors = {'L0_ffn_wq': 8.0,
     'L0_ffn_wk': 8.0,
     'L0_ffn_gate_w': 8.0,
     'L0_ffn_eg_w': 8.0,
     'L0_ffn_eu_w': 8.0,
     'L0_ffn_ed_w': 8.0,
     'L0_ffn_sg_w': 5.381,
     'L0_ffn_su_w': 5.304,
     'L0_ffn_sd_w': 5.248}
    for name, (base, spread) in spreads.items():
        noise = np.random.default_rng([zlib.crc32(name.encode()), seed]).standard_normal(out[name].shape)
        drawn = base * np.exp(spread * noise) if base else spread * noise
        out[name] = jnp.asarray(drawn.astype(out[name].dtype))
    for name, factor in factors.items():
        out[name] = (out[name] * factor).astype(out[name].dtype)
    return out
```

```python
import concourse.bass as bass
from concourse import mybir
from contextlib import ExitStack

F32 = mybir.dt.float32
BF16 = mybir.dt.bfloat16
I32 = mybir.dt.int32
ALU = mybir.AluOpType
ACT = mybir.ActivationFunctionType
AX = mybir.AxisListType

P = 128
B, S, D = 4, 512, 256
DC = D // P
TB = S // P
NT = B * TB
MH, MD, MN = 8, 128, 256
NC = MN // P
STEPS = 3
LN_EPS = 1e-5
NEWTON = 5
ACT_HEADS = 3
DVE_HEADS = MH - ACT_HEADS
H, HD = 16, 128
RMS_EPS = 1e-6
E, TOPK, EI = 16, 6, 176
ITEM = 2 * EI
CHUNKS = (P, P, ITEM - 2 * P)
NCH = len(CHUNKS)
ITEMS = 1 + E // 2
GUARD = 3e38
DVE_STEPS = 74


class Tally:

    def __init__(self, per_body=0, before=0):
        self.per_body, self.before, self.n = per_body, before, 0

    def more(self):
        self.n += 1
        return self.n

    def value(self, i, n):
        return i * self.per_body + (self.before + n) if self.per_body else self.before + n

    def check(self):
        assert self.n == self.per_body, (self.n, self.per_body)


def inverse_root(dve, y, arg, half, term, step_done, steps, i=0):
    dve.tensor_scalar(half.bitcast(I32), arg.bitcast(I32), 1, None, ALU.arith_shift_right).then_inc(step_done, 1)
    dve.wait_ge(step_done, steps.value(i, steps.more()))
    dve.tensor_scalar(y.bitcast(I32), half.bitcast(I32), -1.0, float(0x5F3759DF), ALU.mult, ALU.add).then_inc(step_done, 1)
    dve.wait_ge(step_done, steps.value(i, steps.more()))
    dve.tensor_scalar(half, arg, -0.5, None, ALU.mult).then_inc(step_done, 1)
    dve.wait_ge(step_done, steps.value(i, steps.more()))
    for _ in range(4):
        dve.tensor_tensor(term, half, y, ALU.mult).then_inc(step_done, 1)
        dve.wait_ge(step_done, steps.value(i, steps.more()))
        dve.tensor_tensor(term, term, y, ALU.mult).then_inc(step_done, 1)
        dve.wait_ge(step_done, steps.value(i, steps.more()))
        dve.scalar_tensor_tensor(y, term, 1.5, y, ALU.add, ALU.mult).then_inc(step_done, 1)
        dve.wait_ge(step_done, steps.value(i, steps.more()))


def setup(nc, io, sb, ps, x_all, fold, stats, consts):
    ctx = ExitStack()
    with ctx:
        tile = lambda n, s, d=F32: ctx.enter_context(nc.sbuf_tensor(n, s, d))
        sem = lambda n: ctx.enter_context(nc.semaphore(n))
        memory = tile("memory", [P, NC, MD])
        memory_n = tile("memory_n", [P, NC, MD])
        memory_nT = tile("memory_nT", [P, MN])
        wq = tile("wq_m", [P, MH, D])
        wkT = tile("wkT", [P, MH * P])
        wvT = tile("wvT", [P, MH * P])
        woT = tile("woT", [P, MH, D])
        g_mem = tile("g_mem", [P, 1])
        b_mem = tile("b_mem", [P, 1])
        half_beta = tile("half_beta", [P, MH])
        kT = tile("kT_m", [P, 2, MN])
        vT = tile("vT_m", [P, 2, MN])
        bn = tile("bn_setup", [P, NT + NC, 6])
        mv = tile("mv_setup", [P, NT + NC, 2])
        arg = tile("arg_setup", [P, NT + NC])
        tmp = [tile(f"tmp_setup{k}", [P, NT + NC]) for k in range(2)]
        ident, mask_bias, ident_bf, mask_bf = consts

        memory_in, small_in, kv_w_in, q_w_in, o_w_in = (sem(n) for n in ("memory_in", "small_in", "kv_w_in", "q_w_in", "o_w_in"))
        tokens_in = [sem(f"tokens_in{b}") for b in range(B)]
        const_step, stats_done, root_done, memory_done = (sem(n) for n in ("const_step", "stats_done", "root_done", "memory_done"))
        memT_done, memT_ready, beta_ready = sem("memT_done"), sem("memT_ready"), sem("beta_ready")
        kv_done, fold_done = sem("kv_done"), sem("fold_done")
        kT_ready, vT_ready, g_saved, ap_saved = (sem(n) for n in ("kT_ready", "vT_ready", "g_saved", "ap_saved"))
        block = ctx.enter_context(nc.Block())

        @block.sync
        def _(sp):
            sp.dma_start(memory[:, :, :], io["memory"].rearrange("(c p) d -> p c d", p=P)).then_inc(memory_in, 16)
            for dst, name in ((g_mem, "g_mem"), (b_mem, "b_mem")):
                sp.dma_start(dst[:, :], io[name].rearrange("(p a) -> p a", a=1)).then_inc(small_in, 16)
            sp.dma_start(half_beta[:, :], io["log_beta"].rearrange("(a h) -> a h", a=1).to_broadcast([P, MH])).then_inc(small_in, 16)
            sp.dma_start(stats["gains"][:, :, :], io["gains"]).then_inc(small_in, 16)
            sp.dma_start(wkT[:, :], io["wkT"]).then_inc(kv_w_in, 16)
            sp.dma_start(wvT[:, :], io["wvT"]).then_inc(kv_w_in, 16)
            sp.dma_start(wq[:, :, :], io["wq_m"].rearrange("(h p) d -> p h d", p=P)).then_inc(q_w_in, 16)
            sp.dma_start(woT[:, :, :], io["woT"].rearrange("(h p) d -> p h d", p=P)).then_inc(o_w_in, 16)

        @block.gpsimd
        def _(pool):
            pool.memset(ident[:, :], 0.0).then_inc(const_step, 1)
            pool.memset(mask_bias[:, :], 0.0).then_inc(const_step, 1)
            pool.wait_ge(const_step, 2)
            pool.affine_select(out=ident[:, :], in_=ident[:, :], compare_op=ALU.not_equal, fill=1.0,
                               base=0, pattern=[[-1, P]], channel_multiplier=1).then_inc(const_step, 1)
            pool.affine_select(out=mask_bias[:, :], in_=mask_bias[:, :], compare_op=ALU.is_ge, fill=-1e30,
                               base=0, pattern=[[-1, P]], channel_multiplier=1).then_inc(const_step, 1)
            pool.wait_ge(const_step, 4)
            pool.tensor_copy(ident_bf[:, :], ident[:, :]).then_inc(const_step, 1)
            pool.tensor_copy(mask_bf[:, :], mask_bias[:, :]).then_inc(const_step, 1)

        @block.scalar
        def _(act):
            for b in range(B):
                act.dma_start(x_all[:, b * TB:(b + 1) * TB, :],
                              io["hidden"][b].rearrange("(t p) d -> p t d", p=P)).then_inc(tokens_in[b], 16)
            act.wait_ge(small_in, 4 * 16)
            act.activation(half_beta[:, :], half_beta[:, :], ACT.Exp).then_inc(beta_ready, 1)
            act.wait_ge(beta_ready, 1)
            act.activation(half_beta[:, :], half_beta[:, :], ACT.Copy, scale=0.5).then_inc(beta_ready, 1)
            act.wait_ge(memT_done, 1)
            act.activation(memory_nT[:, :], ps[0][:, 0:MN], ACT.Identity, bias=b_mem[:, :], scale=g_mem[:, :]).then_inc(memT_ready, 1)
            act.wait_ge(beta_ready, 2)

            def save_k(h):
                act.wait_ge(kv_done, h + 1)
                if h >= 2:
                    act.wait_ge(fold_done, h - 1)
                act.activation(kT[:, h % 2, :], ps[h % 2][:, 0:MN], ACT.Copy, scale=half_beta[:, h:h + 1]).then_inc(kT_ready, 1)

            save_k(0)
            for h in range(MH):
                if h + 1 < MH:
                    save_k(h + 1)
                act.wait_ge(fold_done, h + 1)
                act.activation(fold["G"][:, h, :, :], ps[4 + h % 2][:, :].rearrange("p (c n) -> p c n", c=NC), ACT.Copy).then_inc(g_saved, 1)

        @block.vector
        def _(dve):
            dve.wait_ge(memory_in, 16)
            for c in range(NC):
                dve.bn_stats(bn[:, NT + c, :], memory[:, c, :]).then_inc(stats_done, 1)
            for b in range(B):
                dve.wait_ge(tokens_in[b], 16)
                for t in range(b * TB, (b + 1) * TB):
                    dve.bn_stats(bn[:, t, :], x_all[:, t, :]).then_inc(stats_done, 1)
            dve.wait_ge(stats_done, NT + NC)
            for t in range(NT + NC):
                dve.bn_aggr(mv[:, t, :], bn[:, t, :]).then_inc(stats_done, 1)
            dve.wait_ge(stats_done, 2 * (NT + NC))
            dve.tensor_scalar(arg[:, 0:NT], mv[:, 0:NT, 1], 1.0 + LN_EPS, LN_EPS * LN_EPS, ALU.mult, ALU.add).then_inc(root_done, 1)
            dve.tensor_scalar(arg[:, NT:NT + NC], mv[:, NT:NT + NC, 1], LN_EPS, None, ALU.add).then_inc(root_done, 1)
            dve.wait_ge(root_done, 2)
            inverse_root(dve, stats["scale"][:, :], arg[:, :], tmp[0][:, :], tmp[1][:, :], root_done, Tally(before=2))
            dve.tensor_copy(stats["mean"][:, :], mv[:, 0:NT, 0])
            for c in range(NC):
                dve.tensor_scalar(memory_n[:, c, :], memory[:, c, :], mv[:, NT + c, 0:1], stats["scale"][:, NT + c:NT + c + 1],
                                  ALU.subtract, ALU.mult).then_inc(memory_done, 1)

            def save_v(h):
                dve.wait_ge(kT_ready, h + 1)
                if h >= 2:
                    dve.wait_ge(fold_done, h - 1)
                dve.tensor_copy(vT[:, h % 2, :], ps[h % 2][:, MN:2 * MN]).then_inc(vT_ready, 1)

            save_v(0)
            for h in range(MH):
                if h + 1 < MH:
                    save_v(h + 1)
                dve.wait_ge(fold_done, h + 1)
                dve.tensor_copy(fold["A"][:, h, :, :], ps[2 + h % 2][:, :].rearrange("p (c n) -> p c n", c=DC)).then_inc(ap_saved, 1)
                dve.tensor_copy(fold["O"][:, h, :, :], ps[6 + h % 2][:, :].rearrange("p (c n) -> p c n", c=NC)).then_inc(ap_saved, 1)

        @block.tensor
        def _(pe):
            pe.wait_ge(const_step, 3)
            for c in range(NC):
                pe.wait_ge(memory_done, c + 1)
                last = pe.transpose(ps[0][:, c * P:(c + 1) * P], memory_n[:, c, :], ident[:, :])
            last.then_inc(memT_done, 1)
            pe.wait_ge(memT_ready, 1)
            pe.wait_ge(kv_w_in, 32)

            def keys_values(h):
                if h >= 2:
                    pe.wait_ge(kT_ready, h - 1)
                    pe.wait_ge(vT_ready, h - 1)
                pe.matmul(ps[h % 2][:, 0:MN], wkT[:, h * P:(h + 1) * P], memory_nT[:, :], start=True, stop=True)
                pe.matmul(ps[h % 2][:, MN:2 * MN], wvT[:, h * P:(h + 1) * P], memory_nT[:, :], start=True, stop=True).then_inc(kv_done, 1)

            keys_values(0)
            pe.wait_ge(q_w_in, 16)
            pe.wait_ge(o_w_in, 16)
            for h in range(MH):
                if h + 1 < MH:
                    keys_values(h + 1)
                pe.wait_ge(kT_ready, h + 1)
                pe.wait_ge(vT_ready, h + 1)
                if h >= 2:
                    pe.wait_ge(ap_saved, 2 * (h - 1))
                    pe.wait_ge(g_saved, h - 1)
                k, v = kT[:, h % 2, :], vT[:, h % 2, :]
                for c in range(DC):
                    pe.matmul(ps[2 + h % 2][:, c * MN:(c + 1) * MN], wq[:, h, c * P:(c + 1) * P], k, start=True, stop=True)
                for c in range(NC):
                    pe.matmul(ps[4 + h % 2][:, c * MN:(c + 1) * MN], v[:, c * P:(c + 1) * P], k, start=True, stop=True)
                for c in range(NC):
                    last = pe.matmul(ps[6 + h % 2][:, c * D:(c + 1) * D], v[:, c * P:(c + 1) * P], woT[:, h, :], start=True, stop=True)
                last.then_inc(fold_done, 1)


def memory_attention(nc, io, ps, x_all, fold, stats, consts):
    PAIRS = ((0, 1), (2, 3))
    ctx = ExitStack()
    with ctx:
        tile = lambda n, s, d=F32: ctx.enter_context(nc.sbuf_tensor(n, s, d))
        sem = lambda n: ctx.enter_context(nc.semaphore(n))
        xn = tile("xn", [P, TB, D])
        hT = tile("hT_m", [P, TB, DC, P])
        R = tile("R", [P, TB, MH, MN])
        r = tile("r", [P, TB, MH, MN])
        wT = tile("wT", [P, TB, MH, NC, P])
        mx = tile("mx", [P, TB, MH])
        one_less_max = tile("one_less_max", [P, TB, MH])
        neg_tau = tile("neg_tau", [P, TB, MH])
        bn = tile("bn", [P, TB, MH, 6])
        squares = tile("squares", [P, TB, MH, 2])
        s1 = tile("s1", [P, TB, MH])
        s2 = tile("s2", [P, TB, MH])
        den = tile("den", [P, TB, MH])
        num = tile("num", [P, TB, MH])
        junk = tile("junk", [P, ACT_HEADS, MN])
        ident = consts[0]

        xn_ready, xnT_done, hT_ready = sem("xn_ready"), sem("xnT_done"), sem("hT_ready")
        scores_done, max_ready, R_ready = sem("scores_done"), sem("max_ready"), sem("R_ready")
        tau_ready, act_sums, r_final = sem("tau_ready"), sem("act_sums"), sem("r_final")
        rT_done, wT_ready, out_done, x_ready = sem("rT_done"), sem("wT_ready"), sem("out_done"), sem("x_ready")
        relu_done, stats_done, small_done, max_done = sem("relu_done"), sem("stats_done_m"), sem("small_done"), sem("max_done")
        act_relu = sem("act_relu")
        block = ctx.enter_context(nc.Block())
        BANKS = 4
        NS = STEPS * TB
        nth = lambda s, t: s * TB + t

        @block.tensor
        def _(pe):
            with pe.Fori(0, B) as b:
                for t in range(TB):
                    pe.wait_ge(xn_ready, b * TB + (t + 1))
                    pe.wait_ge(hT_ready, b * TB + (t + 1))
                    if t < 2:
                        pe.wait_ge(wT_ready, b * (NS * 4) + 1 + t)
                    for c in range(DC):
                        last = pe.transpose(ps[4 + t % 2][:, c * P:(c + 1) * P], xn[:, t, c * P:(c + 1) * P], ident[:, :])
                    last.then_inc(xnT_done, 1)

                def scores(t, s):
                    n = nth(s, t)
                    if s == 0:
                        pe.wait_ge(hT_ready, b * TB + (2 + t + 1))
                    else:
                        pe.wait_ge(wT_ready, b * (NS * 4) + (2 + 4 * nth(s - 1, t) + 4))
                    for u in range(MH):
                        bank, at = ps[u // 2], (u % 2) * MN
                        if u % 2 == 0:
                            pe.wait_ge(R_ready, b * (NS * 4) + (4 * n + u // 2 + 1))
                        for c in range(NC):
                            lhsT, rhs = (hT[:, t, c, :], fold["A"][:, u, c, :]) if s == 0 else (wT[:, t, u, c, :], fold["G"][:, u, c, :])
                            last = pe.matmul(bank[:, at:at + MN], lhsT, rhs, start=(c == 0), stop=(c == NC - 1))
                        if u % 2:
                            last.then_inc(scores_done, 1)

                def transpose_r(t, s):
                    n = nth(s, t)
                    pe.wait_ge(r_final, b * NS + (n + 1))
                    for u in range(MH):
                        bank, at = ps[4 + (u // 2) % 2], (u % 2) * MN
                        if u % 2 == 0:
                            if n == 0 and u < 4:
                                pe.wait_ge(hT_ready, b * TB + (2 + 4))
                            else:
                                pe.wait_ge(wT_ready, b * (NS * 4) + (2 + 4 * n + u // 2 - 1))
                        for c in range(NC):
                            last = pe.transpose(bank[:, at + c * P:at + (c + 1) * P], r[:, t, u, c * P:(c + 1) * P], ident[:, :])
                        if u % 2:
                            last.then_inc(rT_done, 1)

                def project(t):
                    pe.wait_ge(wT_ready, b * (NS * 4) + (2 + 4 * nth(STEPS - 1, t) + 4))
                    pe.wait_ge(x_ready, b * TB + (t + 1))
                    for u in range(MH):
                        for c in range(NC):
                            last = pe.matmul(ps[6 + t % 2][:, 0:D], wT[:, t, u, c, :], fold["O"][:, u, c, :],
                                             start=(u == 0 and c == 0), stop=(u == MH - 1 and c == NC - 1))
                    last.then_inc(out_done, 1)

                for pair in PAIRS:
                    for t in pair:
                        scores(t, 0)
                for s in range(STEPS):
                    for pair in PAIRS:
                        for t in pair:
                            transpose_r(t, s)
                        for t in pair:
                            if s + 1 < STEPS:
                                scores(t, s + 1)
                            else:
                                project(t)

        @block.scalar
        def _(act):
            act.sem_inc(hT_ready, 2)
            act.sem_inc(wT_ready, 2)
            act.sem_inc(R_ready, BANKS)
            relus = Tally(per_body=STEPS * TB * (NEWTON - 1) * ACT_HEADS)
            with act.Fori(0, B) as b:
                for t in range(TB):
                    act.wait_ge(xnT_done, b * TB + (t + 1))
                    for c in range(DC):
                        last = act.activation(hT[:, t, c, :], ps[4 + t % 2][:, c * P:(c + 1) * P], ACT.Identity,
                                              bias=stats["gains"][:, 1, c:c + 1], scale=stats["gains"][:, 0, c:c + 1])
                    last.then_inc(hT_ready, 1)

                def save_scores(t, s):
                    n = nth(s, t)
                    act.wait_ge(max_ready, b * NS + (n + 1))
                    for u in range(MH):
                        last = act.activation(R[:, t, u, :], ps[u // 2][:, (u % 2) * MN:(u % 2 + 1) * MN], ACT.Relu,
                                              bias=one_less_max[:, t, u:u + 1])
                        if u % 2:
                            last.then_inc(R_ready, 1)

                def share(k, pair, s):
                    for i, t in enumerate(pair):
                        act.wait_ge(tau_ready, b * (NS * NEWTON) + (s * TB * NEWTON + pair[0] * NEWTON + 2 * (k - 1) + i + 1))
                        for j in range(ACT_HEADS):
                            u = DVE_HEADS + j
                            act.activation(r[:, t, u, :], R[:, t, u, :], ACT.Relu, bias=neg_tau[:, t, u:u + 1],
                                                        accum_out=s1[:, t, u:u + 1]).then_inc(act_relu, 1)
                            relus.more()
                        for j in range(ACT_HEADS):
                            u = DVE_HEADS + j
                            act.wait_ge(act_relu, relus.value(b, relus.n - ACT_HEADS + j + 1))
                            last = act.activation(junk[:, j, :], r[:, t, u, :], ACT.Square, accum_out=s2[:, t, u:u + 1])
                        last.then_inc(act_sums, 1)

                def save_weights(t, s):
                    n = nth(s, t)
                    for u in range(0, MH, 2):
                        act.wait_ge(rT_done, b * (NS * 4) + (4 * n + u // 2 + 1))
                        act.activation(wT[:, t, u:u + 2, :, :], ps[4 + (u // 2) % 2][:, :], ACT.Square).then_inc(wT_ready, 1)

                for t in range(TB):
                    save_scores(t, 0)
                for s in range(STEPS):
                    for pair, other in (PAIRS, PAIRS[::-1]):
                        coming = s if pair == PAIRS[0] else s + 1
                        for k in range(1, NEWTON):
                            share(k, pair, s)
                            if k in (2, 4) and 1 <= coming < STEPS:
                                save_scores(other[k // 2 - 1], coming)
                        for t in pair:
                            save_weights(t, s)
            relus.check()

        @block.vector
        def _(dve):
            dve.sem_inc(x_ready, 2)
            relu_n = Tally(per_body=NS * (NEWTON - 1) * DVE_HEADS)
            stats_n = Tally(per_body=NS * (MH + (NEWTON - 1) * DVE_HEADS))
            small_n = Tally(per_body=NS * (8 + (NEWTON - 1) * 9))
            max_n = Tally(per_body=NS * BANKS)
            with dve.Fori(0, B) as b:
                for t in range(TB):
                    dve.tensor_scalar(xn[:, t, :], x_all[:, b * TB + t, :], stats["mean"][:, bass.ds(b * TB + t, 1)],
                                      stats["scale"][:, bass.ds(b * TB + t, 1)], ALU.subtract, ALU.mult).then_inc(xn_ready, 1)

                def maxima(t, s):
                    for j in range(BANKS):
                        dve.wait_ge(scores_done, b * (NS * BANKS) + (BANKS * nth(s, t) + j + 1))
                        dve.tensor_reduce(mx[:, t, 2 * j:2 * j + 2], ps[j][:, :].rearrange("p (u n) -> p u n", u=2),
                                                       op=ALU.max, axis=AX.X).then_inc(max_done, 1)
                        max_n.more()
                    dve.wait_ge(max_done, max_n.value(b, max_n.n))
                    dve.tensor_scalar(one_less_max[:, t, :], mx[:, t, :], -1.0, 1.0, ALU.mult, ALU.add).then_inc(max_ready, 1)

                sums_end = {}
                small_at = {}

                def taus(t, k, s):
                    return b * (NS * NEWTON) + (nth(s, t - t % 2) * NEWTON + 2 * k + t % 2 + 1)

                def update(t, k, s, i):
                    w = MH if k == 0 else DVE_HEADS
                    bnv = bn[:, t, 0:w, :].rearrange("p u (e q) -> p u e q", e=2)
                    if i == 0:
                        dve.wait_ge(stats_done, stats_n.value(b, sums_end[t]))
                        dve.tensor_tensor(squares[:, t, 0:w, :], bnv[:, :, :, 1], bnv[:, :, :, 1], ALU.mult).then_inc(small_done, 1)
                        small_at[t] = small_n.more()
                    elif i == 1:
                        dve.tensor_tensor(s1[:, t, 0:w], bnv[:, :, 0, 1], bnv[:, :, 1, 1], ALU.add).then_inc(small_done, 1)
                        small_n.more()
                        dve.wait_ge(small_done, small_n.value(b, small_at[t]))
                        dve.scalar_tensor_tensor(squares[:, t, 0:w, :], squares[:, t, 0:w, :], MN / 2.0,
                                                                              bnv[:, :, :, 2], ALU.mult, ALU.add).then_inc(small_done, 1)
                        small_at[t] = small_n.more()
                    elif i == 2:
                        dve.wait_ge(small_done, small_n.value(b, small_at[t]))
                        dve.tensor_tensor(s2[:, t, 0:w], squares[:, t, 0:w, 0], squares[:, t, 0:w, 1], ALU.add).then_inc(small_done, 1)
                        small_at[t] = small_n.more()
                    elif i == 3:
                        if k > 0:
                            dve.wait_ge(act_sums, b * (NS * (NEWTON - 1)) + (nth(s, t - t % 2) * (NEWTON - 1) + 2 * (k - 1) + t % 2 + 1))
                            dve.tensor_scalar(s1[:, t, w:MH], s1[:, t, w:MH], 2.0 / MN, None, ALU.mult).then_inc(small_done, 1)
                            small_at[t] = small_n.more()
                    elif i == 4:
                        dve.wait_ge(small_done, small_n.value(b, small_at[t]))
                        dve.scalar_tensor_tensor(den[:, t, :], s2[:, t, :], 3.0, s1[:, t, :], ALU.add, ALU.mult).then_inc(small_done, 1)
                        small_at[t] = small_n.more()
                        dve.tensor_tensor(num[:, t, :], s2[:, t, :], s2[:, t, :], ALU.mult).then_inc(small_done, 1)
                        small_n.more()
                    elif i == 5:
                        dve.wait_ge(small_done, small_n.value(b, small_at[t]))
                        dve.reciprocal(den[:, t, :], den[:, t, :]).then_inc(small_done, 1)
                        small_at[t] = small_n.more()
                    elif i == 6:
                        dve.wait_ge(small_done, small_n.value(b, small_at[t]))
                        dve.scalar_tensor_tensor(num[:, t, :], num[:, t, :], -1.0, den[:, t, :], ALU.add, ALU.mult).then_inc(small_done, 1)
                        small_at[t] = small_n.more()
                    elif i == 7:
                        dve.wait_ge(small_done, small_n.value(b, small_at[t]))
                        if k == 0:
                            dve.tensor_scalar(neg_tau[:, t, :], num[:, t, :], -2.0 / MN, None, ALU.mult).then_inc(tau_ready, 1)
                        else:
                            dve.scalar_tensor_tensor(neg_tau[:, t, :], num[:, t, :], -2.0 / MN, neg_tau[:, t, :],
                                                     ALU.mult, ALU.add).then_inc(tau_ready, 1)

                def first_sweep(t, s, between):
                    for u in range(MH):
                        dve.wait_ge(R_ready, b * (NS * BANKS) + (BANKS + BANKS * nth(s, t) + u // 2 + 1))
                        dve.bn_stats(bn[:, t, u, :], R[:, t, u, :]).then_inc(stats_done, 1)
                        n = stats_n.more()
                        if between:
                            update(*between, u)
                    sums_end[t] = n

                def sweep(t, k, s, between):
                    dve.wait_ge(tau_ready, taus(t, k - 1, s))
                    first = relu_n.n
                    part = 0
                    for u in range(DVE_HEADS + 1):
                        if u < DVE_HEADS:
                            dve.tensor_scalar(r[:, t, u, :], R[:, t, u, :], neg_tau[:, t, u:u + 1], 0.0, ALU.add, ALU.max).then_inc(relu_done, 1)
                            relu_n.more()
                            if part < 8:
                                update(*between, part)
                                part += 1
                        if u >= 1:
                            dve.wait_ge(relu_done, relu_n.value(b, first + u))
                            dve.bn_stats(bn[:, t, u - 1, :], r[:, t, u - 1, :]).then_inc(stats_done, 1)
                            sums_end[t] = stats_n.more()
                            if part < 8:
                                update(*between, part)
                                part += 1

                def final(t, s, between):
                    dve.wait_ge(tau_ready, taus(t, NEWTON - 1, s))
                    for u in range(MH):
                        last = dve.tensor_scalar(r[:, t, u, :], R[:, t, u, :], neg_tau[:, t, u:u + 1], 0.0, ALU.add, ALU.max)
                        if between:
                            update(*between, u)
                    last.then_inc(r_final, 1)

                for t in range(TB):
                    maxima(t, 0)
                for s in range(STEPS):
                    for pair, other in (PAIRS, PAIRS[::-1]):
                        coming = s if pair == PAIRS[0] else s + 1
                        a, z = pair
                        first_sweep(a, s, None)
                        first_sweep(z, s, (a, 0, s))
                        for k in range(1, NEWTON):
                            sweep(a, k, s, (z, k - 1, s))
                            sweep(z, k, s, (a, k, s))
                            if k in (1, 3) and 1 <= coming < STEPS:
                                maxima(other[k // 2], coming)
                        final(a, s, (z, NEWTON - 1, s))
                        final(z, s, None)
                for t in range(TB):
                    dve.wait_ge(out_done, b * TB + (t + 1))
                    dve.tensor_tensor(x_all[:, b * TB + t, :], x_all[:, b * TB + t, :], ps[6 + t % 2][:, 0:D], ALU.add).then_inc(x_ready, 1)
            for tally in (relu_n, stats_n, small_n, max_n):
                tally.check()


def decoder(nc, io, ps, x_all, stats, consts, out):
    ctx = ExitStack()
    with ctx:
        tile = lambda n, s, d=F32: ctx.enter_context(nc.sbuf_tensor(n, s, d))
        sem = lambda n: ctx.enter_context(nc.semaphore(n))
        ident, _, ident_bf, mask_bf = consts
        wv = tile("wv", [P, DC, H * HD])
        wo = tile("wo", [P, H, D])
        wd = tile("wd", [P, ITEMS * NCH, D])
        gate = tile("gate", [P, DC, E])
        wqk = tile("wqk", [P, 2, 2, DC, HD])
        wgu = tile("wgu", [P, 2, 2, DC, ITEM])
        cwB = tile("cwB", [P, 2, NCH, S])
        y = tile("y", [P, TB, D])
        hn = tile("hn", [P, TB, D])
        hT = tile("hT", [P, DC, S])
        qT = tile("qT", [P, S])
        kT = tile("kT", [P, S])
        v = tile("v", [P, 2, TB, HD])
        prob = tile("prob", [P, TB, S])
        probT = tile("probT", [P, TB, S])
        oT = tile("oT", [P, H, S])
        tT = tile("tT", [P, DC, S])
        act_g = tile("act_g", [P, 2, S])
        weighted = tile("weighted", [P, 2, S])
        hidden = tile("hidden", [P, 2, S])
        result = tile("result", [P, TB, D])
        bn = tile("bn_d", [P, 2 * TB, 6])
        mv = tile("mv_d", [P, 2 * TB, 2])
        arg, root, half, term = (tile(n, [P, 2 * TB]) for n in ("arg", "root", "half", "term"))
        nmax, rowsum, rinv = tile("nmax", [P, TB]), tile("rowsum", [P, TB]), tile("rinv", [P, TB])
        logits = tile("logits", [P, TB, E + 2])
        marked = tile("marked", [P, TB, E + 2])
        top = tile("top", [P, TB, 8])
        cw = tile("cw", [P, TB, E])
        cw_sum = tile("cw_sum", [P, TB])
        cwT = tile("cwT", [E, S])
        cw_dram = nc.dram_tensor("cw_dram", (E, S), F32, kind="Internal").ap()

        wv_in, wo_in, wd_in, gate_in = sem("wv_in"), sem("wo_in"), sem("wd_in"), sem("gate_in")
        wqk_in = [sem("wqk_in0"), sem("wqk_in1")]
        wgu_in = [sem("wgu_in0"), sem("wgu_in1")]
        cwB_in = [sem("cwB_in0"), sem("cwB_in1")]
        cw_stored, out_stored = sem("cw_stored"), sem("out_stored")
        dve_step, norm_ready, normT_done, normT_ready = sem("dve_step"), sem("norm_ready"), sem("normT_done"), sem("normT_ready")
        qkv_done, qk_saved, v_saved = sem("qkv_done"), sem("qk_saved"), sem("v_saved")
        scores_done, max_ready, exp_done, rinv_ready, prob_ready = (sem(n) for n in ("scores_done_d", "max_ready_d", "exp_done", "rinv_ready", "prob_ready"))
        pT_done, pT_act_saved, pT_dve_saved = sem("pT_done"), sem("pT_act_saved"), sem("pT_dve_saved")
        o_done, o_saved, ao_done = sem("o_done"), sem("o_saved"), sem("ao_done")
        gate_done, shifted_ready, e_ready, cw_ready, cwT_done, cwT_ready = (
            sem(n) for n in ("gate_done", "shifted_ready", "e_ready", "cw_ready", "cwT_done", "cwT_ready"))
        gu_done, silu_done, weighted_ready, hidden_ready = sem("gu_done"), sem("silu_done"), sem("weighted_ready"), sem("hidden_ready")
        down_done, result_ready = sem("down_done"), sem("result_ready")
        block = ctx.enter_context(nc.Block())
        T_GROUPS = ((6, (0,)), (7, (1, 3)), (6, (2,)))
        G_CHUNKS = ITEMS * NCH

        @block.sync
        def _(sp):
            sp.dma_start(wv[:, :, :], io["wv"].rearrange("(c p) n -> p c n", p=P)).then_inc(wv_in, 16)
            sp.dma_start(gate[:, :, :], io["gate"].rearrange("(c p) n -> p c n", p=P)).then_inc(gate_in, 16)
            sp.sem_inc(out_stored, 16)
            sp.sem_inc(cw_stored, 16)

            def load_item(b, i, j1, gu):
                e = j1 % 2
                sp.wait_ge(weighted_ready, b * (NCH * (ITEMS - 1)) + (i * (2 * NCH) + NCH * j1))
                for lo, hi, c, w in ((0, P, 0, 0), (0, EI - P, 1, 0), (EI - P, P, 1, 1), (0, CHUNKS[2], 2, 1)):
                    sp.dma_start(cwB[lo:hi, e, c, :], cw_dram[bass.ds(i * 4 + (2 * (j1 - 1) + w), 1), :].to_broadcast([hi - lo, S])).then_inc(cwB_in[e], 16)
                if gu:
                    sp.wait_ge(gu_done, b * G_CHUNKS + (i * (2 * NCH) + NCH * (j1 + 1)))
                    sp.dma_start(wgu[:, 1 - e, :, :, :], io["wgu"][i * 2 + (j1 + 1)]).then_inc(wgu_in[1 - e], 16)

            with sp.Fori(0, B) as b:
                with sp.Fori(0, H // 2) as i:
                    for e in range(2):
                        sp.wait_ge(qkv_done, b * (3 * H) + (i * 6 + (3 * e + 2)))
                        sp.dma_start(wqk[:, e, :, :, :], io["wqk"][i * 2 + e]).then_inc(wqk_in[e], 16)
                sp.wait_ge(gu_done, b * G_CHUNKS + NCH)
                for e in range(2):
                    sp.dma_start(wgu[:, e, :, :, :], io["wgu"][e]).then_inc(wgu_in[e], 16)
                sp.wait_ge(cwT_ready, b + 1)
                sp.wait_ge(weighted_ready, b * (NCH * (ITEMS - 1)) + 2 * NCH)
                sp.dma_start(cw_dram, cwT[:, :]).then_inc(cw_stored, 16)
                sp.wait_ge(cw_stored, b * 16 + 32)
                sp.nop(nofuse=True)
                with sp.Fori(0, ITEMS // 2 - 1) as i:
                    load_item(b, i, 1, True)
                    load_item(b, i, 2, True)
                load_item(b, ITEMS // 2 - 1, 1, True)
                load_item(b, ITEMS // 2 - 1, 2, False)
                sp.wait_ge(result_ready, b * TB + 2 * TB)
                sp.dma_start(out[b].rearrange("(t p) d -> p t d", p=P), result[:, :, :]).then_inc(out_stored, 16)
            sp.wait_ge(out_stored, 16 * (B + 1))

        @block.gpsimd
        def _(pool):
            pool.sem_inc(weighted_ready, 2 * NCH)
            with pool.Fori(0, B) as b:
                with pool.Fori(0, H) as h:
                    pool.wait_ge(rinv_ready, b * H + (h + 1))
                    pool.nop(nofuse=True)
                    for t in range(TB):
                        w = (t + 1) * P
                        pool.tensor_scalar(prob[:, t, 0:w], prob[:, t, 0:w], rinv[:, t:t + 1], 1.0, ALU.mult, ALU.mult).then_inc(prob_ready, 1)
                with pool.Fori(0, (ITEMS - 1) // 2) as i:
                    for j1 in (1, 2):
                        pool.wait_ge(cwB_in[j1 % 2], b * (64 * (ITEMS // 2)) + (i * 64 + 64))
                        for c, m in enumerate(CHUNKS):
                            k = NCH * j1 + c
                            pool.wait_ge(silu_done, b * G_CHUNKS + (i * (2 * NCH) + k + 1))
                            pool.tensor_tensor(weighted[0:m, k % 2, :], act_g[0:m, k % 2, :], cwB[0:m, j1 % 2, c, :], ALU.mult).then_inc(weighted_ready, 1)

        @block.tensor
        def _(pe):
            pe.sem_inc(qkv_done, 6)
            pe.sem_inc(gu_done, NCH)

            def transpose_norm(b, part):
                for t in range(TB):
                    pe.wait_ge(norm_ready, b * (2 * TB) + (part * TB + t + 1))
                    for c in range(DC):
                        ins = pe.transpose(ps[4 + c][:, t * P:(t + 1) * P], hn[:, t, c * P:(c + 1) * P], ident[:, :])
                        if t == TB - 1:
                            ins.then_inc(normT_done, 1)

            def qkv(b, h, e, idx):
                g = b * H + h
                pe.wait_ge(wqk_in[e], b * (8 * H) + (idx * 16 + 16))
                pe.wait_ge(v_saved, g + 1)
                for which in range(2):
                    if which == 1:
                        pe.wait_ge(o_saved, g + 1)
                    for c in range(DC):
                        last = pe.matmul(ps[4 + which][:, :], wqk[:, e, which, c, :], hT[:, c, :], start=(c == 0), stop=(c == DC - 1))
                    last.then_inc(qkv_done, 1)
                pe.wait_ge(qk_saved, g * 2 + 1)
                for t in range(TB):
                    for c in range(DC):
                        last = pe.matmul(ps[4][:, t * HD:(t + 1) * HD], hT[:, c, t * P:(t + 1) * P], wv[:, c, bass.ds(h * HD, HD)],
                                         start=(c == 0), stop=(c == DC - 1))
                last.then_inc(qkv_done, 1)

            def scores(b, h):
                g = b * H + h
                pe.wait_ge(qk_saved, g * 2 + 2)
                for t in range(TB):
                    pe.wait_ge(exp_done, g * TB + (t + 1))
                    pe.matmul(ps[t][:, 0:(t + 1) * P], qT[:, t * P:(t + 1) * P], kT[:, 0:(t + 1) * P], start=True, stop=False)
                    pe.matmul(ps[t][:, t * P:(t + 1) * P], ident_bf[:, :], mask_bf[:, :], start=False, stop=True).then_inc(scores_done, 1)

            def transpose_prob(b, h):
                g = b * H + h
                pe.wait_ge(prob_ready, g * TB + TB)
                for k, (bank, tiles) in enumerate(T_GROUPS):
                    if k == 0:
                        pe.wait_ge(pT_act_saved, g * 2 + 1)
                    elif k == 1:
                        pe.wait_ge(pT_dve_saved, g + 1)
                    else:
                        pe.wait_ge(pT_act_saved, g * 2 + 2)
                    at = 0
                    for j in tiles:
                        for t in range(j, TB):
                            last = pe.transpose(ps[bank][:, at:at + P], prob[:, t, j * P:(j + 1) * P], ident[:, :])
                            at += P
                    last.then_inc(pT_done, 1)

            def attend(b, h, e):
                g = b * H + h
                pe.wait_ge(v_saved, g + 2)
                pe.wait_ge(pT_act_saved, g * 2 + 3)
                pe.wait_ge(pT_dve_saved, g + 2)
                for j, (row, at) in enumerate(((0, 0), (1, 0), (2, 0), (1, 3 * P))):
                    last = pe.matmul(ps[5][:, j * P:S], v[:, e, j, :], probT[:, row, at:at + S - j * P], start=(j == 0), stop=(j == TB - 1))
                last.then_inc(o_done, 1)

            def head(b, h, e, idx, first=False):
                qkv(b, h, e, idx)
                if not first:
                    transpose_prob(b, h - 1)
                scores(b, h)
                if not first:
                    attend(b, h - 1, 1 - e)

            def gate_up(b, n, c, j_even, idx, par):
                m, lo = CHUNKS[c], c * P
                if c == 0:
                    pe.wait_ge(wgu_in[j_even], b * (16 * (5 - j_even)) + (idx * 16 + 16))
                pe.wait_ge(hidden_ready, b * G_CHUNKS + (n + 1))
                for which in range(2):
                    for k in range(DC):
                        last = pe.matmul(ps[2 * par + which][0:m, :], wgu[:, j_even, which, k, lo:lo + m], tT[:, k, :],
                                         start=(k == 0), stop=(k == DC - 1))
                last.then_inc(gu_done, 1)

            def down(b, n, m, par, start=False, stop=False):
                pe.wait_ge(hidden_ready, b * G_CHUNKS + (n + 3))
                for t in range(TB):
                    last = pe.matmul(ps[4 + t // 2][:, (t % 2) * D:(t % 2 + 1) * D], hidden[0:m, par, t * P:(t + 1) * P], wd[0:m, n, :],
                                     start=start and t % 2 == 0, stop=stop and t % 2 == 1)
                if stop:
                    last.then_inc(down_done, 1)

            pe.wait_ge(wv_in, 16)
            with pe.Fori(0, B) as b:
                pe.wait_ge(result_ready, b * TB + TB)
                transpose_norm(b, 0)
                pe.wait_ge(normT_ready, b * (2 * DC) + DC)
                head(b, 0, 0, 0, first=True)
                with pe.Fori(0, H // 2 - 1) as i:
                    head(b, i * 2 + 1, 1, i)
                    head(b, i * 2 + 2, 0, i + 1)
                head(b, H - 1, 1, H // 2 - 1)
                transpose_prob(b, H - 1)
                attend(b, H - 1, 1)
                pe.wait_ge(wo_in, 16)
                pe.wait_ge(exp_done, b * (H * TB) + (H * TB + TB))
                pe.wait_ge(o_saved, b * H + (H + 2))
                for t in range(TB):
                    for h in range(H):
                        last = pe.matmul(ps[t][:, 0:D], oT[:, h, t * P:(t + 1) * P], wo[:, h, :], start=(h == 0), stop=(h == H - 1))
                    last.then_inc(ao_done, 1)
                transpose_norm(b, 1)
                pe.wait_ge(normT_ready, b * (2 * DC) + 2 * DC)
                pe.wait_ge(gate_in, 16)
                for t in range(TB):
                    for c in range(DC):
                        last = pe.matmul(ps[6][:, t * E:(t + 1) * E], tT[:, c, t * P:(t + 1) * P], gate[:, c, :], start=(c == 0), stop=(c == DC - 1))
                last.then_inc(gate_done, 1)
                pe.wait_ge(wd_in, 16 * NCH)
                gate_up(b, 0, 0, 0, 0, 0)
                gate_up(b, 1, 1, 0, 0, 1)
                down(b, 0, P, 0, start=True)
                gate_up(b, 2, 2, 0, 0, 0)
                down(b, 1, P, 1)
                for t in range(TB):
                    pe.wait_ge(cw_ready, b + 1)
                    last = pe.transpose(ps[7][0:E, t * P:(t + 1) * P], cw[:, t, :], ident[:, :])
                last.then_inc(cwT_done, 1)
                with pe.Fori(0, (ITEMS - 1) // 2) as i:
                    for j1 in (1, 2):
                        for c in range(NCH):
                            k = NCH * j1 + c
                            gate_up(b, i * (2 * NCH) + k, c, j1 % 2, i if j1 == 1 else i + 1, k % 2)
                            down(b, i * (2 * NCH) + (k - 1), CHUNKS[c - 1], (k - 1) % 2)
                down(b, G_CHUNKS - 1, CHUNKS[-1], (G_CHUNKS - 1) % 2, stop=True)

        @block.scalar
        def _(act):
            act.dma_start(wo[:, :, :], io["wo"].rearrange("(h p) d -> p h d", p=P)).then_inc(wo_in, 16)
            for c, m in enumerate(CHUNKS):
                act.dma_start(wd[:, :, :].rearrange("p (j c) n -> p j c n", c=NCH)[0:m, :, c, :],
                              io["wd"][:, c * P:c * P + m, :].rearrange("j p n -> p j n")).then_inc(wd_in, 16)
            act.sem_inc(exp_done, TB)
            act.sem_inc(pT_act_saved, 1)
            act.sem_inc(o_saved, 2)

            def save_norm(b, part, dst, gain):
                for c in range(DC):
                    act.wait_ge(normT_done, b * (2 * DC) + (part * DC + c + 1))
                    act.activation(dst[:, c, :], ps[4 + c][:, :], ACT.Copy, scale=stats["gains"][:, gain, c:c + 1]).then_inc(normT_ready, 1)

            def save_prob(b, h):
                g = b * H + h
                act.wait_ge(pT_done, g * 3 + 1)
                act.activation(probT[:, 0, :], ps[6][:, :], ACT.Copy).then_inc(pT_act_saved, 1)
                act.wait_ge(pT_done, g * 3 + 3)
                act.activation(probT[:, 2, 0:2 * P], ps[6][:, 0:2 * P], ACT.Copy).then_inc(pT_act_saved, 1)

            def save_o(b, h):
                act.wait_ge(o_done, b * H + (h + 1))
                act.activation(oT[:, h, :], ps[5][:, :], ACT.Copy).then_inc(o_saved, 1)

            def head(b, h, first=False):
                g = b * H + h
                for which, (dst, scale) in enumerate(((qT, HD ** -0.5), (kT, 1.0))):
                    act.wait_ge(qkv_done, g * 3 + (6 + which + 1))
                    act.activation(dst[:, :], ps[4 + which][:, :], ACT.Copy, scale=scale).then_inc(qk_saved, 1)
                if not first:
                    save_prob(b, h - 1)
                for t in range(TB):
                    w = (t + 1) * P
                    act.wait_ge(max_ready, g * TB + (t + 1))
                    act.activation(prob[:, t, 0:w], ps[t][:, 0:w], ACT.Exp, bias=nmax[:, t:t + 1], accum_out=rowsum[:, t:t + 1]).then_inc(exp_done, 1)
                if not first:
                    save_o(b, h - 1)

            def silu(b, n, m, par):
                act.wait_ge(gu_done, b * G_CHUNKS + (n + (NCH + 1)))
                act.activation(act_g[0:m, par, :], ps[2 * par][0:m, :], ACT.Silu).then_inc(silu_done, 1)

            with act.Fori(0, B) as b:
                save_norm(b, 0, hT, 2)
                head(b, 0, first=True)
                with act.Fori(0, H - 1) as i:
                    head(b, i + 1)
                save_prob(b, H - 1)
                save_o(b, H - 1)
                save_norm(b, 1, tT, 3)
                act.wait_ge(shifted_ready, b + 1)
                act.activation(cw[:, :, :], logits[:, :, 0:E], ACT.Exp).then_inc(e_ready, 1)
                for c, m in enumerate(CHUNKS):
                    silu(b, c, m, c % 2)
                with act.Fori(0, (ITEMS - 1) // 2) as i:
                    for j1 in (1, 2):
                        for c, m in enumerate(CHUNKS):
                            silu(b, i * (2 * NCH) + (NCH * j1 + c), m, (NCH * j1 + c) % 2)

        @block.vector
        def _(dve):
            dve.sem_inc(v_saved, 1)
            dve.sem_inc(pT_dve_saved, 1)
            dve.sem_inc(hidden_ready, 2)
            dve.sem_inc(result_ready, TB)
            dve.memset(logits[:, :, E:E + 2], GUARD).then_inc(dve_step, 1)
            steps = Tally(per_body=DVE_STEPS, before=1)

            def head(b, h, e, first=False):
                g = b * H + h
                dve.wait_ge(qkv_done, g * 3 + (6 + 3))
                dve.tensor_copy(v[:, e, :, :], ps[4][:, :].rearrange("p (t d) -> p t d", t=TB)).then_inc(v_saved, 1)
                if not first:
                    save_prob(b, h - 1)
                for t in range(TB):
                    dve.wait_ge(scores_done, g * TB + (t + 1))
                    dve.tensor_reduce(nmax[:, t:t + 1], ps[t][:, 0:(t + 1) * P], op=ALU.max, axis=AX.X, negate=True).then_inc(max_ready, 1)
                dve.wait_ge(exp_done, g * TB + 2 * TB)
                dve.reciprocal(rinv[:, :], rowsum[:, :]).then_inc(rinv_ready, 1)

            def save_prob(b, h):
                dve.wait_ge(pT_done, (b * H + h) * 3 + 2)
                dve.tensor_copy(probT[:, 1, :], ps[7][:, :]).then_inc(pT_dve_saved, 1)

            def hidden_rows(b, n, m, par, routed):
                if routed:
                    dve.wait_ge(weighted_ready, b * (NCH * (ITEMS - 1)) + (n + (2 * NCH - NCH + 1)))
                else:
                    dve.wait_ge(silu_done, b * G_CHUNKS + (n + 1))
                src = weighted if routed else act_g
                dve.tensor_tensor(hidden[0:m, par, :], src[0:m, par, :], ps[2 * par + 1][0:m, :], ALU.mult).then_inc(hidden_ready, 1)

            with dve.Fori(0, B) as b:
                steps.n = 0

                for t in range(TB):
                    dve.bn_stats(bn[:, t, :], x_all[:, b * TB + t, :]).then_inc(dve_step, 1)
                    steps.more()
                dve.wait_ge(dve_step, steps.value(b, steps.n))
                dve.nop(nofuse=True)
                for t in range(TB):
                    dve.bn_aggr(mv[:, t, :], bn[:, t, :]).then_inc(dve_step, 1)
                    steps.more()
                dve.wait_ge(dve_step, steps.value(b, steps.n))
                dve.tensor_scalar(arg[:, 0:TB], mv[:, 0:TB, 1], LN_EPS, None, ALU.add).then_inc(dve_step, 1)
                steps.more()
                dve.tensor_scalar(arg[:, TB:2 * TB], mv[:, 0:TB, 1], 1.0 + RMS_EPS, RMS_EPS * LN_EPS, ALU.mult, ALU.add).then_inc(dve_step, 1)
                steps.more()
                dve.wait_ge(dve_step, steps.value(b, steps.n))
                inverse_root(dve, root[:, :], arg[:, :], half[:, :], term[:, :], dve_step, steps, b)
                for t in range(TB):
                    dve.tensor_scalar(hn[:, t, :], x_all[:, b * TB + t, :], mv[:, t, 0:1], root[:, TB + t:TB + t + 1],
                                      ALU.subtract, ALU.mult).then_inc(norm_ready, 1)
                for t in range(TB):
                    dve.tensor_scalar(y[:, t, :], x_all[:, b * TB + t, :], mv[:, t, 0:1], root[:, t:t + 1], ALU.subtract, ALU.mult).then_inc(dve_step, 1)
                    steps.more()
                y_at = steps.n

                head(b, 0, 0, first=True)
                with dve.Fori(0, H // 2 - 1) as i:
                    head(b, i * 2 + 1, 1)
                    head(b, i * 2 + 2, 0)
                head(b, H - 1, 1)
                save_prob(b, H - 1)

                dve.wait_ge(dve_step, steps.value(b, y_at))
                for t in range(TB):
                    dve.wait_ge(ao_done, b * TB + (t + 1))
                    dve.tensor_tensor(y[:, t, :], y[:, t, :], ps[t][:, 0:D], ALU.add).then_inc(dve_step, 1)
                    steps.more()
                for t in range(TB):
                    dve.wait_ge(dve_step, steps.value(b, y_at + t + 1))
                    dve.bn_stats(bn[:, TB + t, :], y[:, t, :]).then_inc(dve_step, 1)
                    steps.more()
                dve.wait_ge(dve_step, steps.value(b, steps.n))
                dve.nop(nofuse=True)
                for t in range(TB):
                    dve.bn_aggr(mv[:, TB + t, :], bn[:, TB + t, :]).then_inc(dve_step, 1)
                    steps.more()
                dve.wait_ge(dve_step, steps.value(b, steps.n))
                dve.tensor_tensor(arg[:, 0:TB], mv[:, TB:2 * TB, 0], mv[:, TB:2 * TB, 0], ALU.mult).then_inc(dve_step, 1)
                steps.more()
                dve.wait_ge(dve_step, steps.value(b, steps.n))
                dve.scalar_tensor_tensor(arg[:, 0:TB], arg[:, 0:TB], RMS_EPS, mv[:, TB:2 * TB, 1], ALU.add, ALU.add).then_inc(dve_step, 1)
                steps.more()
                dve.wait_ge(dve_step, steps.value(b, steps.n))
                inverse_root(dve, root[:, 0:TB], arg[:, 0:TB], half[:, 0:TB], term[:, 0:TB], dve_step, steps, b)
                for t in range(TB):
                    dve.tensor_scalar(hn[:, t, :], y[:, t, :], root[:, t:t + 1], None, ALU.mult).then_inc(norm_ready, 1)
                for t in range(TB):
                    dve.tensor_tensor(y[:, t, :], y[:, t, :], x_all[:, b * TB + t, :], ALU.add).then_inc(dve_step, 1)
                    steps.more()

                dve.wait_ge(gate_done, b + 1)
                dve.tensor_copy(logits[:, :, 0:E], ps[6][:, 0:TB * E].rearrange("p (t e) -> p t e", t=TB)).then_inc(dve_step, 1)
                steps.more()
                dve.wait_ge(dve_step, steps.value(b, steps.n))
                dve.nop(nofuse=True)
                for t in range(TB):
                    dve.max(top[:, t, :], logits[:, t, :]).then_inc(dve_step, 1)
                    steps.more()
                dve.wait_ge(dve_step, steps.value(b, steps.n))
                dve.nop(nofuse=True)
                for t in range(TB):
                    dve.match_replace(marked[:, t, :], top[:, t, :], logits[:, t, :], -GUARD).then_inc(dve_step, 1)
                    steps.more()
                dve.wait_ge(dve_step, steps.value(b, steps.n))
                dve.tensor_tensor(logits[:, :, 0:E], logits[:, :, 0:E], top[:, :, 2:3].to_broadcast([P, TB, E]), ALU.subtract).then_inc(shifted_ready, 1)
                dve.wait_ge(e_ready, b + 1)
                dve.scalar_tensor_tensor(cw[:, :, :], marked[:, :, 0:E], -GUARD, cw[:, :, :], ALU.is_le, ALU.mult).then_inc(dve_step, 1)
                steps.more()
                dve.wait_ge(dve_step, steps.value(b, steps.n))
                dve.tensor_reduce(cw_sum[:, :], cw[:, :, :], op=ALU.add, axis=AX.X).then_inc(dve_step, 1)
                steps.more()
                dve.wait_ge(dve_step, steps.value(b, steps.n))
                dve.reciprocal(cw_sum[:, :], cw_sum[:, :]).then_inc(dve_step, 1)
                steps.more()
                dve.wait_ge(dve_step, steps.value(b, steps.n))
                dve.tensor_tensor(cw[:, :, :], cw[:, :, :], cw_sum[:, :].rearrange("p (t a) -> p t a", a=1).to_broadcast([P, TB, E]), ALU.mult).then_inc(cw_ready, 1)

                hidden_rows(b, 0, P, 0, False)
                hidden_rows(b, 1, P, 1, False)
                dve.wait_ge(cwT_done, b + 1)
                dve.wait_ge(cw_stored, b * 16 + 16)
                dve.tensor_copy(cwT[:, :], ps[7][0:E, :]).then_inc(cwT_ready, 1)
                hidden_rows(b, 2, CHUNKS[2], 0, False)
                with dve.Fori(0, (ITEMS - 1) // 2) as i:
                    for j1 in (1, 2):
                        for c, m in enumerate(CHUNKS):
                            hidden_rows(b, i * (2 * NCH) + (NCH * j1 + c), m, (NCH * j1 + c) % 2, True)
                dve.wait_ge(down_done, b + 1)
                dve.wait_ge(out_stored, b * 16 + 16)
                dve.wait_ge(dve_step, steps.value(b, steps.n))
                for t in range(TB):
                    dve.tensor_tensor(result[:, t, :], y[:, t, :], ps[4 + t // 2][:, (t % 2) * D:(t % 2 + 1) * D], ALU.add).then_inc(result_ready, 1)
            steps.check()


def program(nc, io, out):
    ctx = ExitStack()
    with ctx:
        tile = lambda n, s, d=F32: ctx.enter_context(nc.sbuf_tensor(n, s, d))
        ps = [ctx.enter_context(nc.psum_tensor(f"bank{k}", [P, 512], F32)) for k in range(8)]
        x_all = tile("x_all", [P, NT, D])
        consts = (tile("ident", [P, P]), tile("mask_bias", [P, P]), tile("ident_bf", [P, P], BF16), tile("mask_bf", [P, P], BF16))
        stats = {"mean": tile("mean", [P, NT]), "scale": tile("scale", [P, NT + NC]), "gains": tile("gains", [P, 4, DC])}
        with nc.sbuf_tensor("fold_A", [P, MH, DC, MN], F32) as A, nc.sbuf_tensor("fold_G", [P, MH, NC, MN], F32) as G, \
                nc.sbuf_tensor("fold_O", [P, MH, NC, D], F32) as O:
            fold = {"A": A, "G": G, "O": O}
            setup(nc, io, tile, ps, x_all, fold, stats, consts)
            memory_attention(nc, io, ps, x_all, fold, stats, consts)
        decoder(nc, io, ps, x_all, stats, consts, out)


def kernel(**inputs):
    import numpy as np
    import concourse.bacc as bacc
    from concourse.bass_utils import run_bass_kernel_spmd as run

    at = {k: np.asarray(v) for k, v in inputs.items()}
    a, f = "L0_attn_", "L0_ffn_"
    laid = {
        "hidden": at[a + "hidden"], "memory": at[a + "memory"],
        "wq_m": at[a + "Wq"], "wkT": at[a + "Wk"].T, "wvT": at[a + "Wv"].T, "woT": at[a + "Wo"].T,
        "log_beta": at[a + "log_beta"], "g_mem": at[a + "g_mem"], "b_mem": at[a + "b_mem"],
        "gains": np.stack([at[n].reshape(DC, P).T for n in (a + "g_state", a + "b_state", f + "ln1_w", f + "ln2_w")], axis=1),
    }
    by_head = [at[f + n].reshape(DC, P, H, HD).transpose(2, 1, 0, 3) for n in ("wq", "wk")]
    rows = [np.concatenate([at[f + s_w], at[f + e_w].reshape(E * EI, D)]) for s_w, e_w in (("sg_w", "eg_w"), ("su_w", "eu_w"))]
    by_item = [r.reshape(ITEMS, ITEM, DC, P).transpose(0, 3, 2, 1) for r in rows]
    down = np.concatenate([at[f + "sd_w"].T, at[f + "ed_w"].transpose(0, 2, 1).reshape(E * EI, D)]).reshape(ITEMS, ITEM, D)
    laid.update({
        "wqk": np.stack(by_head, axis=2), "wv": at[f + "wv"], "wo": at[f + "wo"],
        "gate": at[f + "gate_w"].T, "wgu": np.stack(by_item, axis=2), "wd": down,
    })
    laid = {k: np.ascontiguousarray(v) for k, v in laid.items()}
    nc = bacc.Bacc("TRN2", target_bir_lowering=False, num_devices=1)
    io = {k: nc.dram_tensor("in_" + k, v.shape, mybir.dt.from_np(v.dtype), kind="ExternalInput").ap() for k, v in laid.items()}
    out = nc.dram_tensor("out", (B, S, D), F32, kind="ExternalOutput").ap()
    program(nc, io, out)
    return run(nc, [{"in_" + k: v for k, v in laid.items()}], core_ids=[0]).results[0]["out"]
```

```python
import concourse.bass as bass
from concourse import mybir
from contextlib import ExitStack

F32 = mybir.dt.float32
BF16 = mybir.dt.bfloat16
I32 = mybir.dt.int32
ALU = mybir.AluOpType
ACT = mybir.ActivationFunctionType
AX = mybir.AxisListType

P = 128
B, S, D = 4, 512, 256
DC = D // P
TB = S // P
NT = B * TB
MH, MD, MN = 8, 128, 256
NC = MN // P
STEPS = 3
LN_EPS = 1e-5
NEWTON = 5
ACT_HEADS = 4
DVE_HEADS = MH - ACT_HEADS
H, HD = 16, 128
RMS_EPS = 1e-6
E, TOPK, EI = 16, 6, 176
ITEM = 2 * EI
CHUNKS = (P, P, ITEM - 2 * P)
NCH = len(CHUNKS)
ITEMS = 1 + E // 2
GUARD = 3e38
DVE_STEPS = 75


class Tally:

    def __init__(self, per_body=0, before=0):
        self.per_body, self.before, self.n = per_body, before, 0

    def more(self):
        self.n += 1
        return self.n

    def value(self, i, n):
        return i * self.per_body + (self.before + n) if self.per_body else self.before + n

    def check(self):
        assert self.n == self.per_body, (self.n, self.per_body)


def inverse_root(dve, y, arg, half, term, step_done, steps, i=0):
    dve.tensor_scalar(half.bitcast(I32), arg.bitcast(I32), 1, None, ALU.arith_shift_right).then_inc(step_done, 1)
    dve.wait_ge(step_done, steps.value(i, steps.more()))
    dve.tensor_scalar(y.bitcast(I32), half.bitcast(I32), -1.0, float(0x5F3759DF), ALU.mult, ALU.add).then_inc(step_done, 1)
    dve.wait_ge(step_done, steps.value(i, steps.more()))
    dve.tensor_scalar(half, arg, -0.5, None, ALU.mult).then_inc(step_done, 1)
    dve.wait_ge(step_done, steps.value(i, steps.more()))
    for _ in range(4):
        dve.tensor_tensor(term, half, y, ALU.mult).then_inc(step_done, 1)
        dve.wait_ge(step_done, steps.value(i, steps.more()))
        dve.tensor_tensor(term, term, y, ALU.mult).then_inc(step_done, 1)
        dve.wait_ge(step_done, steps.value(i, steps.more()))
        dve.scalar_tensor_tensor(y, term, 1.5, y, ALU.add, ALU.mult).then_inc(step_done, 1)
        dve.wait_ge(step_done, steps.value(i, steps.more()))


def setup(nc, io, ps, x_all, fold, stats, consts):
    ctx = ExitStack()
    with ctx:
        tile = lambda n, s, d=F32: ctx.enter_context(nc.sbuf_tensor(n, s, d))
        sem = lambda n: ctx.enter_context(nc.semaphore(n))
        memory = tile("memory", [P, NC, MD])
        memory_n = tile("memory_n", [P, NC, MD])
        memory_nT = tile("memory_nT", [P, MN])
        wq = tile("wq_m", [P, MH, D])
        wkT = tile("wkT", [P, MH * P])
        wvT = tile("wvT", [P, MH * P])
        woT = tile("woT", [P, MH, D])
        g_mem = tile("g_mem", [P, 1])
        b_mem = tile("b_mem", [P, 1])
        half_beta = tile("half_beta", [P, MH])
        kT = tile("kT_m", [P, 2, MN])
        vT = tile("vT_m", [P, 2, MN])
        bn = tile("bn_setup", [P, NT + NC, 6])
        mv = tile("mv_setup", [P, NT + NC, 2])
        arg = tile("arg_setup", [P, NT + NC])
        tmp = [tile(f"tmp_setup{k}", [P, NT + NC]) for k in range(2)]
        ident, mask_bias, ident_bf, mask_bf = consts

        memory_in, small_in, kv_w_in, q_w_in, o_w_in = (sem(n) for n in ("memory_in", "small_in", "kv_w_in", "q_w_in", "o_w_in"))
        tokens_in = [sem(f"tokens_in{b}") for b in range(B)]
        const_step, stats_done, root_done, memory_done = (sem(n) for n in ("const_step", "stats_done", "root_done", "memory_done"))
        memT_done, memT_ready, beta_ready = sem("memT_done"), sem("memT_ready"), sem("beta_ready")
        kv_done, fold_done = sem("kv_done"), sem("fold_done")
        kT_ready, vT_ready, g_saved, ap_saved = (sem(n) for n in ("kT_ready", "vT_ready", "g_saved", "ap_saved"))
        block = ctx.enter_context(nc.Block())

        @block.sync
        def _(sp):
            sp.dma_start(memory[:, :, :], io["memory"].rearrange("(c p) d -> p c d", p=P)).then_inc(memory_in, 16)
            for dst, name in ((g_mem, "g_mem"), (b_mem, "b_mem")):
                sp.dma_start(dst[:, :], io[name].rearrange("(p a) -> p a", a=1)).then_inc(small_in, 16)
            sp.dma_start(half_beta[:, :], io["log_beta"].rearrange("(a h) -> a h", a=1).to_broadcast([P, MH])).then_inc(small_in, 16)
            sp.dma_start(stats["gains"][:, :, :], io["gains"]).then_inc(small_in, 16)
            sp.dma_start(wkT[:, :], io["wkT"]).then_inc(kv_w_in, 16)
            sp.dma_start(wvT[:, :], io["wvT"]).then_inc(kv_w_in, 16)
            sp.dma_start(wq[:, :, :], io["wq_m"].rearrange("(h p) d -> p h d", p=P)).then_inc(q_w_in, 16)
            sp.dma_start(woT[:, :, :], io["woT"].rearrange("(h p) d -> p h d", p=P)).then_inc(o_w_in, 16)

        @block.gpsimd
        def _(pool):
            pool.memset(ident[:, :], 0.0).then_inc(const_step, 1)
            pool.memset(mask_bias[:, :], 0.0).then_inc(const_step, 1)
            pool.wait_ge(const_step, 2)
            pool.affine_select(out=ident[:, :], in_=ident[:, :], compare_op=ALU.not_equal, fill=1.0,
                               base=0, pattern=[[-1, P]], channel_multiplier=1).then_inc(const_step, 1)
            pool.affine_select(out=mask_bias[:, :], in_=mask_bias[:, :], compare_op=ALU.is_ge, fill=-1e30,
                               base=0, pattern=[[-1, P]], channel_multiplier=1).then_inc(const_step, 1)
            pool.wait_ge(const_step, 4)
            pool.tensor_copy(ident_bf[:, :], ident[:, :]).then_inc(const_step, 1)
            pool.tensor_copy(mask_bf[:, :], mask_bias[:, :]).then_inc(const_step, 1)

        @block.scalar
        def _(act):
            for b in range(B):
                act.dma_start(x_all[:, b * TB:(b + 1) * TB, :],
                              io["hidden"][b].rearrange("(t p) d -> p t d", p=P)).then_inc(tokens_in[b], 16)
            act.wait_ge(small_in, 4 * 16)
            act.activation(half_beta[:, :], half_beta[:, :], ACT.Exp).then_inc(beta_ready, 1)
            act.wait_ge(beta_ready, 1)
            act.activation(half_beta[:, :], half_beta[:, :], ACT.Copy, scale=0.5).then_inc(beta_ready, 1)
            act.wait_ge(memT_done, 1)
            act.activation(memory_nT[:, :], ps[0][:, 0:MN], ACT.Identity, bias=b_mem[:, :], scale=g_mem[:, :]).then_inc(memT_ready, 1)
            act.wait_ge(beta_ready, 2)

            def save_k(h):
                act.wait_ge(kv_done, h + 1)
                if h >= 2:
                    act.wait_ge(fold_done, h - 1)
                act.activation(kT[:, h % 2, :], ps[h % 2][:, 0:MN], ACT.Copy, scale=half_beta[:, h:h + 1]).then_inc(kT_ready, 1)

            save_k(0)
            for h in range(MH):
                if h + 1 < MH:
                    save_k(h + 1)
                act.wait_ge(fold_done, h + 1)
                act.activation(fold["G"][:, h, :, :], ps[4 + h % 2][:, :].rearrange("p (c n) -> p c n", c=NC), ACT.Copy).then_inc(g_saved, 1)

        @block.vector
        def _(dve):
            dve.wait_ge(memory_in, 16)
            for c in range(NC):
                dve.bn_stats(bn[:, NT + c, :], memory[:, c, :]).then_inc(stats_done, 1)
            for b in range(B):
                dve.wait_ge(tokens_in[b], 16)
                for t in range(b * TB, (b + 1) * TB):
                    dve.bn_stats(bn[:, t, :], x_all[:, t, :]).then_inc(stats_done, 1)
            dve.wait_ge(stats_done, NT + NC)
            for t in range(NT + NC):
                dve.bn_aggr(mv[:, t, :], bn[:, t, :]).then_inc(stats_done, 1)
            dve.wait_ge(stats_done, 2 * (NT + NC))
            dve.tensor_scalar(arg[:, 0:NT], mv[:, 0:NT, 1], 1.0 + LN_EPS, LN_EPS * LN_EPS, ALU.mult, ALU.add).then_inc(root_done, 1)
            dve.tensor_scalar(arg[:, NT:NT + NC], mv[:, NT:NT + NC, 1], LN_EPS, None, ALU.add).then_inc(root_done, 1)
            dve.wait_ge(root_done, 2)
            inverse_root(dve, stats["scale"][:, :], arg[:, :], tmp[0][:, :], tmp[1][:, :], root_done, Tally(before=2))
            dve.tensor_copy(stats["mean"][:, :], mv[:, 0:NT, 0])
            for c in range(NC):
                dve.tensor_scalar(memory_n[:, c, :], memory[:, c, :], mv[:, NT + c, 0:1], stats["scale"][:, NT + c:NT + c + 1],
                                  ALU.subtract, ALU.mult).then_inc(memory_done, 1)

            def save_v(h):
                dve.wait_ge(kT_ready, h + 1)
                if h >= 2:
                    dve.wait_ge(fold_done, h - 1)
                dve.tensor_copy(vT[:, h % 2, :], ps[h % 2][:, MN:2 * MN]).then_inc(vT_ready, 1)

            save_v(0)
            for h in range(MH):
                if h + 1 < MH:
                    save_v(h + 1)
                dve.wait_ge(fold_done, h + 1)
                dve.tensor_copy(fold["A"][:, h, :, :], ps[2 + h % 2][:, :].rearrange("p (c n) -> p c n", c=DC)).then_inc(ap_saved, 1)
                dve.tensor_copy(fold["O"][:, h, :, :], ps[6 + h % 2][:, :].rearrange("p (c n) -> p c n", c=NC)).then_inc(ap_saved, 1)

        @block.tensor
        def _(pe):
            pe.wait_ge(const_step, 3)
            for c in range(NC):
                pe.wait_ge(memory_done, c + 1)
                last = pe.transpose(ps[0][:, c * P:(c + 1) * P], memory_n[:, c, :], ident[:, :])
            last.then_inc(memT_done, 1)
            pe.wait_ge(memT_ready, 1)
            pe.wait_ge(kv_w_in, 32)

            def keys_values(h):
                if h >= 2:
                    pe.wait_ge(kT_ready, h - 1)
                    pe.wait_ge(vT_ready, h - 1)
                pe.matmul(ps[h % 2][:, 0:MN], wkT[:, h * P:(h + 1) * P], memory_nT[:, :], start=True, stop=True)
                pe.matmul(ps[h % 2][:, MN:2 * MN], wvT[:, h * P:(h + 1) * P], memory_nT[:, :], start=True, stop=True).then_inc(kv_done, 1)

            keys_values(0)
            pe.wait_ge(q_w_in, 16)
            pe.wait_ge(o_w_in, 16)
            for h in range(MH):
                if h + 1 < MH:
                    keys_values(h + 1)
                pe.wait_ge(kT_ready, h + 1)
                pe.wait_ge(vT_ready, h + 1)
                if h >= 2:
                    pe.wait_ge(ap_saved, 2 * (h - 1))
                    pe.wait_ge(g_saved, h - 1)
                k, v = kT[:, h % 2, :], vT[:, h % 2, :]
                for c in range(DC):
                    pe.matmul(ps[2 + h % 2][:, c * MN:(c + 1) * MN], wq[:, h, c * P:(c + 1) * P], k, start=True, stop=True)
                for c in range(NC):
                    pe.matmul(ps[4 + h % 2][:, c * MN:(c + 1) * MN], v[:, c * P:(c + 1) * P], k, start=True, stop=True)
                for c in range(NC):
                    last = pe.matmul(ps[6 + h % 2][:, c * D:(c + 1) * D], v[:, c * P:(c + 1) * P], woT[:, h, :], start=True, stop=True)
                last.then_inc(fold_done, 1)


class Shared:
    pass


def shared(nc, tile, sem):
    m = Shared()
    m.y = tile("y", [P, TB, D])
    m.tT = tile("tT", [P, DC, S])
    m.cwT = tile("cwT", [E, S])
    m.cw_dram = nc.dram_tensor("cw_dram", (E, S), F32, kind="Internal").ap()
    m.xn_ready, m.xnT_done, m.hT_ready = sem("xn_ready"), sem("xnT_done"), sem("hT_ready")
    m.mem_scores_done, m.mem_max_ready, m.R_ready = sem("mem_scores_done"), sem("mem_max_ready"), sem("R_ready")
    m.tau_ready, m.act_sums, m.r_final = sem("tau_ready"), sem("act_sums"), sem("r_final")
    m.rT_done, m.wT_ready, m.out_done, m.x_ready = sem("rT_done"), sem("wT_ready"), sem("out_done"), sem("x_ready")
    m.relu_done, m.stats_done, m.small_done, m.max_done = sem("relu_done"), sem("mem_stats_done"), sem("small_done"), sem("max_done")
    m.act_relu = sem("act_relu")
    m.wqkv_in, m.wo_in, m.gate_in, m.cw_stored = [sem("wqkv_in0"), sem("wqkv_in1")], sem("wo_in"), sem("gate_in"), sem("cw_stored")
    m.dve_step, m.norm_ready, m.normT_done, m.normT_ready = sem("dve_step"), sem("norm_ready"), sem("normT_done"), sem("normT_ready")
    m.qkv_done, m.qk_saved, m.v_saved = sem("qkv_done"), sem("qk_saved"), sem("v_saved")
    m.scores_done, m.max_ready, m.exp_done = sem("scores_done"), sem("max_ready"), sem("exp_done")
    m.rinv_ready, m.prob_ready = sem("rinv_ready"), sem("prob_ready")
    m.pT_done, m.pT_act_saved, m.pT_dve_saved = sem("pT_done"), sem("pT_act_saved"), sem("pT_dve_saved")
    m.o_done, m.o_saved, m.ao_done = sem("o_done"), sem("o_saved"), sem("ao_done")
    m.gate_done, m.shifted_ready, m.e_ready = sem("gate_done"), sem("shifted_ready"), sem("e_ready")
    m.cw_ready, m.cwT_done, m.cwT_ready = sem("cw_ready"), sem("cwT_done"), sem("cwT_ready")
    m.wgu_in, m.wd_in, m.cwB_in = ([sem(f"{n}{e}") for e in range(2)] for n in ("wgu_in", "wd_in", "cwB_in"))
    m.gu_done, m.silu_done, m.weighted_ready, m.hidden_ready = sem("gu_done"), sem("silu_done"), sem("weighted_ready"), sem("hidden_ready")
    m.down_done, m.result_ready, m.out_stored = sem("down_done"), sem("result_ready"), sem("out_stored")
    return m


def credits(nc, m):
    with nc.Block() as block:
        @block.tensor
        def _(pe):
            pe.sem_inc(m.qkv_done, 6)

        @block.scalar
        def _(act):
            act.sem_inc(m.R_ready, 2)
            act.sem_inc(m.exp_done, TB)
            act.sem_inc(m.pT_act_saved, 1)
            act.sem_inc(m.o_saved, 2)

        @block.vector
        def _(dve):
            dve.sem_inc(m.v_saved, 1)
            dve.sem_inc(m.pT_dve_saved, 1)
            dve.sem_inc(m.hidden_ready, 2)


class Experts:

    def __init__(self, nc, ctx, m, ps, io, out, b, banks):
        tile = lambda n, s, d=F32: ctx.enter_context(nc.sbuf_tensor(n, s, d))
        self.m, self.ps, self.io, self.out, self.b = m, ps, io, out, b
        self.banks = banks
        self.lag = 1 if banks[0] == banks[1] else 2
        self.wgu = tile(f"wgu_{self.lag}", [P, 2, 2, DC, ITEM])
        self.wd = tile(f"wd_{self.lag}", [P, 2, NCH, D])
        self.cwB = tile(f"cwB_{self.lag}", [P, 2, NCH, S])
        self.act_g = tile(f"act_g_{self.lag}", [P, 2, S])
        self.hidden = tile(f"hidden_{self.lag}", [P, 2, S])

    def load_weights(self, sp, idx, e):
        for lo, hi, c, w in ((0, P, 0, 0), (0, EI - P, 1, 0), (EI - P, P, 1, 1), (0, CHUNKS[2], 2, 1)):
            row = self.m.cw_dram[bass.ds(idx * 4 + (2 * e - 2 + w), 1), :]
            sp.dma_start(self.cwB[lo:hi, e, c, :], row.to_broadcast([hi - lo, S])).then_inc(self.m.cwB_in[e], 16)

    def load_gu(self, sp, idx, e):
        sp.dma_start(self.wgu[:, e, :, :, :], self.io["wgu"][idx * 2 + e]).then_inc(self.m.wgu_in[e], 16)

    def load_d(self, sp, idx, e):
        rows = self.io["wd"][idx * 2 + e]
        sp.dma_start(self.wd[:, e, 0:2, :], rows[0:2 * P, :].rearrange("(c p) n -> p c n", p=P)).then_inc(self.m.wd_in[e], 16)
        sp.dma_start(self.wd[0:CHUNKS[2], e, 2, :], rows[2 * P:ITEM, :]).then_inc(self.m.wd_in[e], 16)

    def sync(self, sp):
        m, b = self.m, self.b
        for e in range(2):
            self.load_gu(sp, 0, e)
            self.load_d(sp, 0, e)
        self.load_weights(sp, 0, 1)
        self.load_weights(sp, 1, 0)

        def item(idx, e):
            n = lambda k: b * (ITEMS * NCH) + (idx * (2 * NCH) + (NCH * e + k))
            sp.wait_ge(m.gu_done, n(-NCH))
            self.load_gu(sp, idx, e)
            sp.wait_ge(m.gu_done, n(-1))
            self.load_d(sp, idx, e)

        def weights(idx, e):
            sp.wait_ge(m.weighted_ready, b * (NCH * (ITEMS - 1)) + (idx * (2 * NCH) + NCH * (e - 2)))
            self.load_weights(sp, idx, e)

        item(1, 0)
        with sp.Fori(1, (ITEMS - 1) // 2) as i:
            item(i, 1)
            weights(i, 1)
            item(i + 1, 0)
            weights(i + 1, 0)
        sp.wait_ge(m.result_ready, b * TB + TB)
        sp.dma_start(self.out[b].rearrange("(t p) d -> p t d", p=P), m.y[:, :, :]).then_inc(m.out_stored, 16)

    def pool(self, pool):
        m, b = self.m, self.b
        with pool.Fori(0, (ITEMS - 1) // 2) as i:
            for e in (1, 0):
                pool.wait_ge(m.cwB_in[e], b * (64 * (ITEMS // 2)) + (i * 64 + 64))
                for c, rows in enumerate(CHUNKS):
                    k = NCH * (2 - e) + c
                    pool.wait_ge(m.silu_done, b * (ITEMS * NCH) + (i * (2 * NCH) + k + 1))
                    pool.tensor_tensor(self.act_g[0:rows, k % 2, :], self.act_g[0:rows, k % 2, :], self.cwB[0:rows, e, c, :], ALU.mult) \
                        .then_inc(m.weighted_ready, 1)

    def gate_up(self, pe, n, c, e, idx, par):
        m, b = self.m, self.b
        if c == 0:
            pe.wait_ge(m.wgu_in[e], b * (16 * (5 - e)) + (idx * 16 + 16))
        pe.wait_ge(m.hidden_ready, b * (ITEMS * NCH) + (n + (3 - self.lag)))
        rows = CHUNKS[c]
        for which in range(2):
            for k in range(DC):
                last = pe.matmul(self.ps[self.banks[par][which]][0:rows, :], self.wgu[:, e, which, k, c * P:c * P + rows], m.tT[:, k, :],
                                 start=(k == 0), stop=(k == DC - 1))
        last.then_inc(m.gu_done, 1)

    def down(self, pe, n, c, e, idx, par, start=False, stop=False):
        m, b = self.m, self.b
        if c == 0:
            pe.wait_ge(m.wd_in[e], b * (32 * (5 - e)) + (idx * 32 + 32))
        pe.wait_ge(m.hidden_ready, b * (ITEMS * NCH) + (n + 3))
        rows = CHUNKS[c]
        for t in range(TB):
            last = pe.matmul(self.ps[4 + t // 2][:, (t % 2) * D:(t % 2 + 1) * D], self.hidden[0:rows, par, t * P:(t + 1) * P],
                             self.wd[0:rows, e, c, :], start=start and t % 2 == 0, stop=stop and t % 2 == 1)
        if stop:
            last.then_inc(m.down_done, 1)

    def silu(self, act, n, c, par):
        m, b, rows = self.m, self.b, CHUNKS[c]
        act.wait_ge(m.gu_done, b * (ITEMS * NCH) + (n + 1))
        act.activation(self.act_g[0:rows, par, :], self.ps[self.banks[par][0]][0:rows, :], ACT.Silu).then_inc(m.silu_done, 1)

    def hide(self, dve, n, c, par, routed):
        m, b, rows = self.m, self.b, CHUNKS[c]
        if routed:
            dve.wait_ge(m.weighted_ready, b * (NCH * (ITEMS - 1)) + (n - NCH + 1))
        else:
            dve.wait_ge(m.silu_done, b * (ITEMS * NCH) + (n + 1))
        dve.tensor_tensor(self.hidden[0:rows, par, :], self.act_g[0:rows, par, :], self.ps[self.banks[par][1]][0:rows, :], ALU.mult) \
           .then_inc(m.hidden_ready, 1)

    def result(self, dve):
        m, b = self.m, self.b
        dve.wait_ge(m.down_done, b + 1)
        for t in range(TB):
            dve.tensor_tensor(m.y[:, t, :], m.y[:, t, :], self.ps[4 + t // 2][:, (t % 2) * D:(t % 2 + 1) * D], ALU.add) \
               .then_inc(m.result_ready, 1)


def experts_alone(nc, m, ps, io, out, b):
    with ExitStack() as ctx:
        x = Experts(nc, ctx, m, ps, io, out, b, ((6, 7), (0, 1)))
        block = ctx.enter_context(nc.Block())
        PAIRS = (ITEMS - 1) // 2

        @block.sync
        def _(sp):
            x.sync(sp)
            sp.wait_ge(m.out_stored, 16 * B)

        @block.gpsimd
        def _(pool):
            x.pool(pool)

        @block.tensor
        def _(pe):
            for c in range(NCH):
                x.gate_up(pe, c, c, 0, 0, c % 2)
                if c:
                    x.down(pe, c - 1, c - 1, 0, 0, (c - 1) % 2, start=(c == 1))
            with pe.Fori(0, PAIRS) as i:
                for k in range(2 * NCH):
                    item, c = divmod(k, NCH)
                    x.gate_up(pe, i * (2 * NCH) + (NCH + k), c, 1 - item, i + item, (NCH + k) % 2)
                    before, c = divmod(k - 1, NCH)
                    x.down(pe, i * (2 * NCH) + (NCH + k - 1), c, (1 - before) % 2, i + max(before, 0), (NCH + k - 1) % 2)
            x.down(pe, ITEMS * NCH - 1, NCH - 1, 0, 4, 0, stop=True)

        @block.scalar
        def _(act):
            for c in range(NCH):
                x.silu(act, c, c, c % 2)
            with act.Fori(0, PAIRS) as i:
                for k in range(2 * NCH):
                    x.silu(act, i * (2 * NCH) + (NCH + k), k % NCH, (NCH + k) % 2)

        @block.vector
        def _(dve):
            for c in range(NCH):
                x.hide(dve, c, c, c % 2, False)
            with dve.Fori(0, PAIRS) as i:
                for k in range(2 * NCH):
                    x.hide(dve, i * (2 * NCH) + (NCH + k), k % NCH, (NCH + k) % 2, True)
            x.result(dve)


def memory_attention(nc, m, io, out, ps, x_all, fold, stats, consts, b, beside):
    PAIRS = ((0, 1), (2, 3))
    ctx = ExitStack()
    with ctx:
        tile = lambda n, s, d=F32: ctx.enter_context(nc.sbuf_tensor(f"{n}_{beside}", s, d))
        xn = tile("xn", [P, TB, D])
        hT = tile("hT_m", [P, TB, DC, P])
        R = tile("R", [P, TB, MH, MN])
        r = tile("r", [P, 2, DVE_HEADS, MN])
        r_act = tile("r_act", [P, 2, ACT_HEADS, MN])
        wT = tile("wT", [P, TB, MH, NC, P])
        mx = tile("mx", [P, TB, MH])
        one_less_max = tile("one_less_max", [P, TB, MH])
        neg_tau = tile("neg_tau", [P, TB, MH])
        bn = tile("bn", [P, TB, MH, 6])
        squares = tile("squares", [P, TB, MH, 2])
        s1 = tile("s1", [P, TB, MH])
        s2 = tile("s2", [P, TB, MH])
        den = tile("den", [P, TB, MH])
        num = tile("num", [P, TB, MH])
        ident = consts[0]

        experts = Experts(nc, ctx, m, ps, io, out, b - 1, ((6, 7), (6, 7))) if beside else None
        block = ctx.enter_context(nc.Block())
        NS = STEPS * TB
        nth = lambda s, t: s * TB + t
        HALVES = {k: ((k - 1) // 2, (k - 1) % 2) for k in range(1, 5)}
        score_bank = lambda s, t, u: (0, 1, 6, 7)[u // 2] if nth(s, t) < 2 else (u // 2) % 2
        tick = lambda s, pair, k: (s * 2 + pair[0] // 2) * NEWTON + k

        if beside:
            @block.sync
            def _(sp):
                experts.sync(sp)

            @block.gpsimd
            def _(pool):
                experts.pool(pool)

        @block.tensor
        def _(pe):
            def scores(t, s, half):
                if s == 0:
                    pe.wait_ge(m.hT_ready, b * TB + (t + 1))
                else:
                    pe.wait_ge(m.wT_ready, b * (NS * 4) + (4 * nth(s - 1, t) + 4))
                for u in range(4 * half, 4 * half + 4):
                    bank, at = ps[score_bank(s, t, u)], (u % 2) * MN
                    if u % 2 == 0 and nth(s, t) == 1:
                        pe.wait_ge(m.R_ready, b * (NS * 4) + (2 + u // 2 + 1))
                    elif u % 2 == 0:
                        pe.wait_ge(m.R_ready, b * (NS * 4) + (4 * nth(s, t) + u // 2 + 1))
                    for c in range(NC):
                        lhsT, rhs = (hT[:, t, c, :], fold["A"][:, u, c, :]) if s == 0 else (wT[:, t, u, c, :], fold["G"][:, u, c, :])
                        last = pe.matmul(bank[:, at:at + MN], lhsT, rhs, start=(c == 0), stop=(c == NC - 1))
                    if u % 2:
                        last.then_inc(m.mem_scores_done, 1)

            def transpose_r(t, s):
                n = nth(s, t)
                pe.wait_ge(m.r_final, b * NS + (n + 1))
                for u in range(MH):
                    bank, at = ps[2 + (u // 2) % 2], (u % 2) * MN
                    if u % 2 == 0:
                        if n == 0 and u < 4:
                            pe.wait_ge(m.hT_ready, b * TB + TB)
                        elif s == STEPS - 1 and t == 2 and u < 4:
                            pe.wait_ge(m.x_ready, b * TB + 2)
                        else:
                            pe.wait_ge(m.wT_ready, b * (NS * 4) + (4 * n + u // 2 - 1))
                    for c in range(NC):
                        last = pe.transpose(bank[:, at + c * P:at + (c + 1) * P], R[:, t, u, c * P:(c + 1) * P], ident[:, :])
                    if u % 2:
                        last.then_inc(m.rT_done, 1)

            def project(t):
                pe.wait_ge(m.wT_ready, b * (NS * 4) + (4 * nth(STEPS - 1, t - t % 2 + 1) + 4))
                for u in range(MH):
                    for c in range(NC):
                        last = pe.matmul(ps[2 + t % 2][:, 0:D], wT[:, t, u, c, :], fold["O"][:, u, c, :],
                                         start=(u == 0 and c == 0), stop=(u == MH - 1 and c == NC - 1))
                last.then_inc(m.out_done, 1)

            def chunk(n):
                if beside and n == 0:
                    pe.wait_ge(m.R_ready, b * (NS * 4) + (2 + 2 * 4))
                if beside and n < ITEMS * NCH:
                    j, c = divmod(n, NCH)
                    experts.gate_up(pe, n, c, j % 2, j // 2, n % 2)
                if beside and 1 <= n <= ITEMS * NCH:
                    j, c = divmod(n - 1, NCH)
                    experts.down(pe, n - 1, c, j % 2, j // 2, (n - 1) % 2, start=(n == 1), stop=(n == ITEMS * NCH))

            for t in range(TB):
                pe.wait_ge(m.xn_ready, b * TB + (t + 1))
                if t >= 2:
                    pe.wait_ge(m.hT_ready, b * TB + (t - 1))
                for c in range(DC):
                    last = pe.transpose(ps[2 + t % 2][:, c * P:(c + 1) * P], xn[:, t, c * P:(c + 1) * P], ident[:, :])
                last.then_inc(m.xnT_done, 1)
            for t in PAIRS[0]:
                for half in range(2):
                    scores(t, 0, half)
            for s in range(STEPS):
                for pair, other in (PAIRS, PAIRS[::-1]):
                    coming = s if pair == PAIRS[0] else s + 1
                    last_s = s - 1 if pair == PAIRS[0] else s
                    if last_s >= 0:
                        for t in other:
                            transpose_r(t, last_s)
                    chunk(tick(s, pair, 0))
                    for k in range(1, NEWTON):
                        i, half = HALVES[k]
                        if coming < STEPS:
                            scores(other[i], coming, half)
                        chunk(tick(s, pair, k))
                        if coming == STEPS and k == NEWTON - 2:
                            for t in other:
                                project(t)
            for t in PAIRS[1]:
                transpose_r(t, STEPS - 1)
            for t in PAIRS[1]:
                project(t)

        @block.scalar
        def _(act):
            relus = Tally(per_body=STEPS * TB * (NEWTON - 1) * ACT_HEADS)

            def save_scores(t, s, half):
                act.wait_ge(m.mem_max_ready, b * (NS * 2) + (2 * nth(s, t) + half + 1))
                for u in range(4 * half, 4 * half + 4):
                    last = act.activation(R[:, t, u, :], ps[score_bank(s, t, u)][:, (u % 2) * MN:(u % 2 + 1) * MN], ACT.Relu,
                                          bias=one_less_max[:, t, u:u + 1])
                    if u % 2:
                        last.then_inc(m.R_ready, 1)

            def share(k, i, pair, s):
                t = pair[i]
                act.wait_ge(m.tau_ready, b * (NS * NEWTON) + (nth(s, pair[0]) * NEWTON + 2 * (k - 1) + i + 1))
                for j in range(ACT_HEADS):
                    u = DVE_HEADS + j
                    act.activation(r_act[:, i, j, :], R[:, t, u, :], ACT.Relu, bias=neg_tau[:, t, u:u + 1],
                                   accum_out=s1[:, t, u:u + 1]).then_inc(m.act_relu, 1)
                    relus.more()
                for j in range(ACT_HEADS):
                    u = DVE_HEADS + j
                    act.wait_ge(m.act_relu, relus.value(b, relus.n - ACT_HEADS + j + 1))
                    last = act.activation(r_act[:, i, j, :], r_act[:, i, j, :], ACT.Square, accum_out=s2[:, t, u:u + 1])
                last.then_inc(m.act_sums, 1)

            def save_weights(t, s):
                for u in range(0, MH, 2):
                    act.wait_ge(m.rT_done, b * (NS * 4) + (4 * nth(s, t) + u // 2 + 1))
                    act.activation(wT[:, t, u:u + 2, :, :], ps[2 + (u // 2) % 2][:, :], ACT.Square).then_inc(m.wT_ready, 1)

            def chunk(n):
                if beside and 0 <= n < ITEMS * NCH:
                    experts.silu(act, n, n % NCH, n % 2)

            for t in range(TB):
                act.wait_ge(m.xnT_done, b * TB + (t + 1))
                for c in range(DC):
                    last = act.activation(hT[:, t, c, :], ps[2 + t % 2][:, c * P:(c + 1) * P], ACT.Identity,
                                          bias=stats["gains"][:, 1, c:c + 1], scale=stats["gains"][:, 0, c:c + 1])
                last.then_inc(m.hT_ready, 1)
            for t in PAIRS[0]:
                for half in range(2):
                    save_scores(t, 0, half)
            for s in range(STEPS):
                for pair, other in (PAIRS, PAIRS[::-1]):
                    coming = s if pair == PAIRS[0] else s + 1
                    last_s = s - 1 if pair == PAIRS[0] else s
                    chunk(tick(s, pair, 0) - 1)
                    if last_s >= 0:
                        for t in other:
                            save_weights(t, last_s)
                    for k in range(1, NEWTON):
                        chunk(tick(s, pair, k) - 1)
                        share(k, 0, pair, s)
                        share(k, 1, pair, s)
                        i, half = HALVES[k]
                        if coming < STEPS:
                            save_scores(other[i], coming, half)
            for t in PAIRS[1]:
                save_weights(t, STEPS - 1)
            relus.check()

        @block.vector
        def _(dve):
            relu_n = Tally(per_body=NS * (NEWTON - 1) * DVE_HEADS)
            stats_n = Tally(per_body=NS * (MH + (NEWTON - 1) * DVE_HEADS))
            small_n = Tally(per_body=NS * (8 + (NEWTON - 1) * 9))
            max_n = Tally(per_body=NS * 4)
            for t in range(TB):
                dve.tensor_scalar(xn[:, t, :], x_all[:, b * TB + t, :], stats["mean"][:, bass.ds(b * TB + t, 1)],
                                  stats["scale"][:, bass.ds(b * TB + t, 1)], ALU.subtract, ALU.mult).then_inc(m.xn_ready, 1)

            def maxima(t, s, half):
                for j in (2 * half, 2 * half + 1):
                    dve.wait_ge(m.mem_scores_done, b * (NS * 4) + (4 * nth(s, t) + j + 1))
                    dve.tensor_reduce(mx[:, t, 2 * j:2 * j + 2], ps[score_bank(s, t, 2 * j)][:, :].rearrange("p (u n) -> p u n", u=2),
                                                   op=ALU.max, axis=AX.X).then_inc(m.max_done, 1)
                    max_n.more()
                dve.wait_ge(m.max_done, max_n.value(b, max_n.n))
                heads = slice(4 * half, 4 * half + 4)
                dve.tensor_scalar(one_less_max[:, t, heads], mx[:, t, heads], -1.0, 1.0, ALU.mult, ALU.add).then_inc(m.mem_max_ready, 1)

            sums_end = {}
            small_at = {}

            def taus(t, k, s):
                return b * (NS * NEWTON) + (nth(s, t - t % 2) * NEWTON + 2 * k + t % 2 + 1)

            def update(t, k, s, i):
                w = MH if k == 0 else DVE_HEADS
                bnv = bn[:, t, 0:w, :].rearrange("p u (e q) -> p u e q", e=2)
                if i == 0:
                    dve.wait_ge(m.stats_done, stats_n.value(b, sums_end[t]))
                    dve.tensor_tensor(squares[:, t, 0:w, :], bnv[:, :, :, 1], bnv[:, :, :, 1], ALU.mult).then_inc(m.small_done, 1)
                    small_at[t] = small_n.more()
                elif i == 1:
                    dve.tensor_tensor(s1[:, t, 0:w], bnv[:, :, 0, 1], bnv[:, :, 1, 1], ALU.add).then_inc(m.small_done, 1)
                    small_n.more()
                    dve.wait_ge(m.small_done, small_n.value(b, small_at[t]))
                    dve.scalar_tensor_tensor(squares[:, t, 0:w, :], squares[:, t, 0:w, :], MN / 2.0,
                                                                          bnv[:, :, :, 2], ALU.mult, ALU.add).then_inc(m.small_done, 1)
                    small_at[t] = small_n.more()
                elif i == 2:
                    dve.wait_ge(m.small_done, small_n.value(b, small_at[t]))
                    dve.tensor_tensor(s2[:, t, 0:w], squares[:, t, 0:w, 0], squares[:, t, 0:w, 1], ALU.add).then_inc(m.small_done, 1)
                    small_at[t] = small_n.more()
                elif i == 3:
                    if k > 0:
                        dve.wait_ge(m.act_sums, b * (NS * (NEWTON - 1)) + (nth(s, t - t % 2) * (NEWTON - 1) + 2 * (k - 1) + t % 2 + 1))
                        dve.tensor_scalar(s1[:, t, w:MH], s1[:, t, w:MH], 2.0 / MN, None, ALU.mult).then_inc(m.small_done, 1)
                        small_at[t] = small_n.more()
                elif i == 4:
                    dve.wait_ge(m.small_done, small_n.value(b, small_at[t]))
                    dve.scalar_tensor_tensor(den[:, t, :], s2[:, t, :], 3.0, s1[:, t, :], ALU.add, ALU.mult).then_inc(m.small_done, 1)
                    small_at[t] = small_n.more()
                    dve.tensor_tensor(num[:, t, :], s2[:, t, :], s2[:, t, :], ALU.mult).then_inc(m.small_done, 1)
                    small_n.more()
                elif i == 5:
                    dve.wait_ge(m.small_done, small_n.value(b, small_at[t]))
                    dve.reciprocal(den[:, t, :], den[:, t, :]).then_inc(m.small_done, 1)
                    small_at[t] = small_n.more()
                elif i == 6:
                    dve.wait_ge(m.small_done, small_n.value(b, small_at[t]))
                    dve.scalar_tensor_tensor(num[:, t, :], num[:, t, :], -1.0, den[:, t, :], ALU.add, ALU.mult).then_inc(m.small_done, 1)
                    small_at[t] = small_n.more()
                elif i == 7:
                    dve.wait_ge(m.small_done, small_n.value(b, small_at[t]))
                    if k == 0:
                        dve.tensor_scalar(neg_tau[:, t, :], num[:, t, :], -2.0 / MN, None, ALU.mult).then_inc(m.tau_ready, 1)
                    else:
                        dve.scalar_tensor_tensor(neg_tau[:, t, :], num[:, t, :], -2.0 / MN, neg_tau[:, t, :],
                                                 ALU.mult, ALU.add).then_inc(m.tau_ready, 1)

            def first_sweep(t, s, between):
                for u in range(MH):
                    dve.wait_ge(m.R_ready, b * (NS * 4) + (2 + 4 * nth(s, t) + u // 2 + 1))
                    dve.bn_stats(bn[:, t, u, :], R[:, t, u, :]).then_inc(m.stats_done, 1)
                    n = stats_n.more()
                    if between:
                        update(*between, u)
                sums_end[t] = n

            def sweep(t, k, s, between):
                dve.wait_ge(m.tau_ready, taus(t, k - 1, s))
                first = relu_n.n
                part = 0
                for u in range(DVE_HEADS + 1):
                    if u < DVE_HEADS:
                        dve.tensor_scalar(r[:, t % 2, u, :], R[:, t, u, :], neg_tau[:, t, u:u + 1], 0.0, ALU.add, ALU.max).then_inc(m.relu_done, 1)
                        relu_n.more()
                        if part < 8:
                            update(*between, part)
                            part += 1
                    if u >= 1:
                        dve.wait_ge(m.relu_done, relu_n.value(b, first + u))
                        dve.bn_stats(bn[:, t, u - 1, :], r[:, t % 2, u - 1, :]).then_inc(m.stats_done, 1)
                        sums_end[t] = stats_n.more()
                        if part < 8:
                            update(*between, part)
                            part += 1

            def final(t, s, between):
                dve.wait_ge(m.tau_ready, taus(t, NEWTON - 1, s))
                for u in range(MH):
                    last = dve.tensor_scalar(R[:, t, u, :], R[:, t, u, :], neg_tau[:, t, u:u + 1], 0.0, ALU.add, ALU.max)
                    if between:
                        update(*between, u)
                last.then_inc(m.r_final, 1)

            def chunk(n):
                if beside and 0 <= n < ITEMS * NCH:
                    experts.hide(dve, n, n % NCH, n % 2, n >= NCH)

            def output(pair):
                for t in pair:
                    dve.wait_ge(m.out_done, b * TB + (t + 1))
                    dve.tensor_tensor(x_all[:, b * TB + t, :], x_all[:, b * TB + t, :], ps[2 + t % 2][:, 0:D], ALU.add).then_inc(m.x_ready, 1)

            for t in PAIRS[0]:
                for half in range(2):
                    maxima(t, 0, half)
            for s in range(STEPS):
                for pair, other in (PAIRS, PAIRS[::-1]):
                    coming = s if pair == PAIRS[0] else s + 1
                    a, z = pair
                    first_sweep(a, s, None)
                    chunk(tick(s, pair, 0) - 1)
                    first_sweep(z, s, (a, 0, s))
                    for k in range(1, NEWTON):
                        i, half = HALVES[k]
                        sweep(a, k, s, (z, k - 1, s))
                        chunk(tick(s, pair, k) - 1)
                        sweep(z, k, s, (a, k, s))
                        if coming < STEPS:
                            maxima(other[i], coming, half)
                        if coming == STEPS and k == NEWTON - 1:
                            output(other)
                    final(a, s, (z, NEWTON - 1, s))
                    final(z, s, None)
            if beside:
                experts.result(dve)
            output(PAIRS[1])
            for tally in (relu_n, stats_n, small_n, max_n):
                tally.check()


def causal_attention(nc, m, io, ps, x_all, stats, consts, b, where):
    ctx = ExitStack()
    with ctx:
        tile = lambda n, s, d=F32: ctx.enter_context(nc.sbuf_tensor(f"{n}_{where}", s, d))
        ident, _, ident_bf, mask_bf = consts
        wo = tile("wo", [P, H, D])
        gate = tile("gate", [P, DC, E])
        wqkv = tile("wqkv", [P, 2, 3, DC, HD])
        hn = tile("hn", [P, TB, D])
        hT = tile("hT", [P, DC, S])
        qT = tile("qT", [P, S])
        kT = tile("kT", [P, S])
        v = tile("v", [P, 2, TB, HD])
        prob = tile("prob", [P, TB, S])
        probT = tile("probT", [P, TB, S])
        oT = tile("oT", [P, H, S])
        bn = tile("bn_d", [P, 2 * TB, 6])
        mv = tile("mv_d", [P, 2 * TB, 2])
        arg, root, half, term = (tile(n, [P, 2 * TB]) for n in ("arg", "root", "half", "term"))
        nmax, rowsum, rinv = tile("nmax", [P, TB]), tile("rowsum", [P, TB]), tile("rinv", [P, TB])
        logits = tile("logits", [P, TB, E + 2])
        marked = tile("marked", [P, TB, E + 2])
        top = tile("top", [P, TB, 8])
        cw = tile("cw", [P, TB, E])
        cw_sum = tile("cw_sum", [P, TB])
        block = ctx.enter_context(nc.Block())
        T_GROUPS = ((6, (0,)), (7, (1, 3)), (6, (2,)))

        @block.sync
        def _(sp):
            sp.dma_start(gate[:, :, :], io["gate"].rearrange("(c p) n -> p c n", p=P)).then_inc(m.gate_in, 16)
            with sp.Fori(0, H // 2) as i:
                for e in range(2):
                    sp.wait_ge(m.qkv_done, b * (3 * H) + (i * 6 + (3 * e + 3)))
                    sp.dma_start(wqkv[:, e, :, :, :], io["wqkv"][i * 2 + e]).then_inc(m.wqkv_in[e], 16)
            sp.wait_ge(m.cwT_ready, b + 1)
            sp.dma_start(m.cw_dram, m.cwT[:, :]).then_inc(m.cw_stored, 16)
            sp.wait_ge(m.cw_stored, b * 16 + 16)
            sp.nop(nofuse=True)

        @block.gpsimd
        def _(pool):
            with pool.Fori(0, H) as h:
                pool.wait_ge(m.rinv_ready, b * H + (h + 1))
                pool.nop(nofuse=True)
                for t in range(TB):
                    w = (t + 1) * P
                    pool.tensor_scalar(prob[:, t, 0:w], prob[:, t, 0:w], rinv[:, t:t + 1], 1.0, ALU.mult, ALU.mult).then_inc(m.prob_ready, 1)

        @block.tensor
        def _(pe):
            def transpose_norm(b, part):
                for t in range(TB):
                    pe.wait_ge(m.norm_ready, b * (2 * TB) + (part * TB + t + 1))
                    for c in range(DC):
                        ins = pe.transpose(ps[4 + c][:, t * P:(t + 1) * P], hn[:, t, c * P:(c + 1) * P], ident[:, :])
                        if t == TB - 1:
                            ins.then_inc(m.normT_done, 1)

            def qkv(b, h, e, idx):
                g = b * H + h
                pe.wait_ge(m.wqkv_in[e], b * (8 * H) + (idx * 16 + 16))
                pe.wait_ge(m.v_saved, g + 1)
                for which in range(2):
                    if which == 1:
                        pe.wait_ge(m.o_saved, g + 1)
                    for c in range(DC):
                        last = pe.matmul(ps[4 + which][:, :], wqkv[:, e, which, c, :], hT[:, c, :], start=(c == 0), stop=(c == DC - 1))
                    last.then_inc(m.qkv_done, 1)
                pe.wait_ge(m.qk_saved, g * 2 + 1)
                for t in range(TB):
                    for c in range(DC):
                        last = pe.matmul(ps[4][:, t * HD:(t + 1) * HD], hT[:, c, t * P:(t + 1) * P], wqkv[:, e, 2, c, :],
                                         start=(c == 0), stop=(c == DC - 1))
                last.then_inc(m.qkv_done, 1)

            def scores(b, h):
                g = b * H + h
                pe.wait_ge(m.qk_saved, g * 2 + 2)
                for t in range(TB):
                    pe.wait_ge(m.exp_done, g * TB + (t + 1))
                    pe.matmul(ps[t][:, 0:(t + 1) * P], qT[:, t * P:(t + 1) * P], kT[:, 0:(t + 1) * P], start=True, stop=False)
                    pe.matmul(ps[t][:, t * P:(t + 1) * P], ident_bf[:, :], mask_bf[:, :], start=False, stop=True).then_inc(m.scores_done, 1)

            def transpose_prob(b, h):
                g = b * H + h
                pe.wait_ge(m.prob_ready, g * TB + TB)
                for k, (bank, tiles) in enumerate(T_GROUPS):
                    if k == 0:
                        pe.wait_ge(m.pT_act_saved, g * 2 + 1)
                    elif k == 1:
                        pe.wait_ge(m.pT_dve_saved, g + 1)
                    else:
                        pe.wait_ge(m.pT_act_saved, g * 2 + 2)
                    at = 0
                    for j in tiles:
                        for t in range(j, TB):
                            last = pe.transpose(ps[bank][:, at:at + P], prob[:, t, j * P:(j + 1) * P], ident[:, :])
                            at += P
                    last.then_inc(m.pT_done, 1)

            def attend(b, h, e):
                g = b * H + h
                pe.wait_ge(m.v_saved, g + 2)
                pe.wait_ge(m.pT_act_saved, g * 2 + 3)
                pe.wait_ge(m.pT_dve_saved, g + 2)
                for j, (row, at) in enumerate(((0, 0), (1, 0), (2, 0), (1, 3 * P))):
                    last = pe.matmul(ps[5][:, j * P:S], v[:, e, j, :], probT[:, row, at:at + S - j * P], start=(j == 0), stop=(j == TB - 1))
                last.then_inc(m.o_done, 1)

            def head(b, h, e, idx, first=False):
                qkv(b, h, e, idx)
                if not first:
                    transpose_prob(b, h - 1)
                scores(b, h)
                if not first:
                    attend(b, h - 1, 1 - e)

            transpose_norm(b, 0)
            pe.wait_ge(m.normT_ready, b * (2 * DC) + DC)
            head(b, 0, 0, 0, first=True)
            with pe.Fori(0, H // 2 - 1) as i:
                head(b, i * 2 + 1, 1, i)
                head(b, i * 2 + 2, 0, i + 1)
            head(b, H - 1, 1, H // 2 - 1)
            transpose_prob(b, H - 1)
            attend(b, H - 1, 1)
            pe.wait_ge(m.wo_in, b * 16 + 16)
            pe.wait_ge(m.exp_done, b * (H * TB) + (H * TB + TB))
            pe.wait_ge(m.o_saved, b * H + (H + 2))
            for t in range(TB):
                for h in range(H):
                    last = pe.matmul(ps[t][:, 0:D], oT[:, h, t * P:(t + 1) * P], wo[:, h, :], start=(h == 0), stop=(h == H - 1))
                last.then_inc(m.ao_done, 1)
            transpose_norm(b, 1)
            pe.wait_ge(m.normT_ready, b * (2 * DC) + 2 * DC)
            pe.wait_ge(m.gate_in, b * 16 + 16)
            for t in range(TB):
                for c in range(DC):
                    last = pe.matmul(ps[6][:, t * E:(t + 1) * E], m.tT[:, c, t * P:(t + 1) * P], gate[:, c, :], start=(c == 0), stop=(c == DC - 1))
            last.then_inc(m.gate_done, 1)
            for t in range(TB):
                pe.wait_ge(m.cw_ready, b + 1)
                last = pe.transpose(ps[7][0:E, t * P:(t + 1) * P], cw[:, t, :], ident[:, :])
            last.then_inc(m.cwT_done, 1)

        @block.scalar
        def _(act):
            act.dma_start(wo[:, :, :], io["wo"].rearrange("(h p) d -> p h d", p=P)).then_inc(m.wo_in, 16)

            def save_norm(b, part, dst, gain):
                for c in range(DC):
                    act.wait_ge(m.normT_done, b * (2 * DC) + (part * DC + c + 1))
                    act.activation(dst[:, c, :], ps[4 + c][:, :], ACT.Copy, scale=stats["gains"][:, gain, c:c + 1]).then_inc(m.normT_ready, 1)

            def save_prob(b, h):
                g = b * H + h
                act.wait_ge(m.pT_done, g * 3 + 1)
                act.activation(probT[:, 0, :], ps[6][:, :], ACT.Copy).then_inc(m.pT_act_saved, 1)
                act.wait_ge(m.pT_done, g * 3 + 3)
                act.activation(probT[:, 2, 0:2 * P], ps[6][:, 0:2 * P], ACT.Copy).then_inc(m.pT_act_saved, 1)

            def save_o(b, h):
                act.wait_ge(m.o_done, b * H + (h + 1))
                act.activation(oT[:, h, :], ps[5][:, :], ACT.Copy).then_inc(m.o_saved, 1)

            def head(b, h, first=False):
                g = b * H + h
                for which, (dst, scale) in enumerate(((qT, HD ** -0.5), (kT, 1.0))):
                    act.wait_ge(m.qkv_done, g * 3 + (6 + which + 1))
                    act.activation(dst[:, :], ps[4 + which][:, :], ACT.Copy, scale=scale).then_inc(m.qk_saved, 1)
                if not first:
                    save_prob(b, h - 1)
                for t in range(TB):
                    w = (t + 1) * P
                    act.wait_ge(m.max_ready, g * TB + (t + 1))
                    act.activation(prob[:, t, 0:w], ps[t][:, 0:w], ACT.Exp, bias=nmax[:, t:t + 1], accum_out=rowsum[:, t:t + 1]).then_inc(m.exp_done, 1)
                if not first:
                    save_o(b, h - 1)

            save_norm(b, 0, hT, 2)
            head(b, 0, first=True)
            with act.Fori(0, H - 1) as i:
                head(b, i + 1)
            save_prob(b, H - 1)
            save_o(b, H - 1)
            save_norm(b, 1, m.tT, 3)
            act.wait_ge(m.shifted_ready, b + 1)
            act.activation(cw[:, :, :], logits[:, :, 0:E], ACT.Exp).then_inc(m.e_ready, 1)

        @block.vector
        def _(dve):
            steps = Tally(per_body=DVE_STEPS)
            dve.memset(logits[:, :, E:E + 2], GUARD).then_inc(m.dve_step, 1)
            steps.more()

            def head(b, h, e, first=False):
                g = b * H + h
                dve.wait_ge(m.qkv_done, g * 3 + (6 + 3))
                dve.tensor_copy(v[:, e, :, :], ps[4][:, :].rearrange("p (t d) -> p t d", t=TB)).then_inc(m.v_saved, 1)
                if not first:
                    save_prob(b, h - 1)
                for t in range(TB):
                    dve.wait_ge(m.scores_done, g * TB + (t + 1))
                    dve.tensor_reduce(nmax[:, t:t + 1], ps[t][:, 0:(t + 1) * P], op=ALU.max, axis=AX.X, negate=True).then_inc(m.max_ready, 1)
                dve.wait_ge(m.exp_done, g * TB + 2 * TB)
                dve.reciprocal(rinv[:, :], rowsum[:, :]).then_inc(m.rinv_ready, 1)

            def save_prob(b, h):
                dve.wait_ge(m.pT_done, (b * H + h) * 3 + 2)
                dve.tensor_copy(probT[:, 1, :], ps[7][:, :]).then_inc(m.pT_dve_saved, 1)


            for t in range(TB):
                dve.bn_stats(bn[:, t, :], x_all[:, b * TB + t, :]).then_inc(m.dve_step, 1)
                steps.more()
            dve.wait_ge(m.dve_step, steps.value(b, steps.n))
            dve.nop(nofuse=True)
            for t in range(TB):
                dve.bn_aggr(mv[:, t, :], bn[:, t, :]).then_inc(m.dve_step, 1)
                steps.more()
            dve.wait_ge(m.dve_step, steps.value(b, steps.n))
            dve.tensor_scalar(arg[:, 0:TB], mv[:, 0:TB, 1], LN_EPS, None, ALU.add).then_inc(m.dve_step, 1)
            steps.more()
            dve.tensor_scalar(arg[:, TB:2 * TB], mv[:, 0:TB, 1], 1.0 + RMS_EPS, RMS_EPS * LN_EPS, ALU.mult, ALU.add).then_inc(m.dve_step, 1)
            steps.more()
            dve.wait_ge(m.dve_step, steps.value(b, steps.n))
            inverse_root(dve, root[:, :], arg[:, :], half[:, :], term[:, :], m.dve_step, steps, b)
            for t in range(TB):
                dve.tensor_scalar(hn[:, t, :], x_all[:, b * TB + t, :], mv[:, t, 0:1], root[:, TB + t:TB + t + 1],
                                  ALU.subtract, ALU.mult).then_inc(m.norm_ready, 1)
            if not (isinstance(b, int) and b == 0):
                dve.wait_ge(m.out_stored, b * 16)
                dve.nop(nofuse=True)
            for t in range(TB):
                dve.tensor_scalar(m.y[:, t, :], x_all[:, b * TB + t, :], mv[:, t, 0:1], root[:, t:t + 1], ALU.subtract, ALU.mult).then_inc(m.dve_step, 1)
                steps.more()
            y_at = steps.n

            head(b, 0, 0, first=True)
            with dve.Fori(0, H // 2 - 1) as i:
                head(b, i * 2 + 1, 1)
                head(b, i * 2 + 2, 0)
            head(b, H - 1, 1)
            save_prob(b, H - 1)

            dve.wait_ge(m.dve_step, steps.value(b, y_at))
            for t in range(TB):
                dve.wait_ge(m.ao_done, b * TB + (t + 1))
                dve.tensor_tensor(m.y[:, t, :], m.y[:, t, :], ps[t][:, 0:D], ALU.add).then_inc(m.dve_step, 1)
                steps.more()
            for t in range(TB):
                dve.wait_ge(m.dve_step, steps.value(b, y_at + t + 1))
                dve.bn_stats(bn[:, TB + t, :], m.y[:, t, :]).then_inc(m.dve_step, 1)
                steps.more()
            dve.wait_ge(m.dve_step, steps.value(b, steps.n))
            dve.nop(nofuse=True)
            for t in range(TB):
                dve.bn_aggr(mv[:, TB + t, :], bn[:, TB + t, :]).then_inc(m.dve_step, 1)
                steps.more()
            dve.wait_ge(m.dve_step, steps.value(b, steps.n))
            dve.tensor_tensor(arg[:, 0:TB], mv[:, TB:2 * TB, 0], mv[:, TB:2 * TB, 0], ALU.mult).then_inc(m.dve_step, 1)
            steps.more()
            dve.wait_ge(m.dve_step, steps.value(b, steps.n))
            dve.scalar_tensor_tensor(arg[:, 0:TB], arg[:, 0:TB], RMS_EPS, mv[:, TB:2 * TB, 1], ALU.add, ALU.add).then_inc(m.dve_step, 1)
            steps.more()
            dve.wait_ge(m.dve_step, steps.value(b, steps.n))
            inverse_root(dve, root[:, 0:TB], arg[:, 0:TB], half[:, 0:TB], term[:, 0:TB], m.dve_step, steps, b)
            for t in range(TB):
                dve.tensor_scalar(hn[:, t, :], m.y[:, t, :], root[:, t:t + 1], None, ALU.mult).then_inc(m.norm_ready, 1)
            for t in range(TB):
                dve.tensor_tensor(m.y[:, t, :], m.y[:, t, :], x_all[:, b * TB + t, :], ALU.add).then_inc(m.dve_step, 1)
                steps.more()

            dve.wait_ge(m.gate_done, b + 1)
            dve.tensor_copy(logits[:, :, 0:E], ps[6][:, 0:TB * E].rearrange("p (t e) -> p t e", t=TB)).then_inc(m.dve_step, 1)
            steps.more()
            dve.wait_ge(m.dve_step, steps.value(b, steps.n))
            dve.nop(nofuse=True)
            for t in range(TB):
                dve.max(top[:, t, :], logits[:, t, :]).then_inc(m.dve_step, 1)
                steps.more()
            dve.wait_ge(m.dve_step, steps.value(b, steps.n))
            dve.nop(nofuse=True)
            for t in range(TB):
                dve.match_replace(marked[:, t, :], top[:, t, :], logits[:, t, :], -GUARD).then_inc(m.dve_step, 1)
                steps.more()
            dve.wait_ge(m.dve_step, steps.value(b, steps.n))
            dve.tensor_tensor(logits[:, :, 0:E], logits[:, :, 0:E], top[:, :, 2:3].to_broadcast([P, TB, E]), ALU.subtract).then_inc(m.shifted_ready, 1)
            dve.wait_ge(m.e_ready, b + 1)
            dve.scalar_tensor_tensor(cw[:, :, :], marked[:, :, 0:E], -GUARD, cw[:, :, :], ALU.is_le, ALU.mult).then_inc(m.dve_step, 1)
            steps.more()
            dve.wait_ge(m.dve_step, steps.value(b, steps.n))
            dve.tensor_reduce(cw_sum[:, :], cw[:, :, :], op=ALU.add, axis=AX.X).then_inc(m.dve_step, 1)
            steps.more()
            dve.wait_ge(m.dve_step, steps.value(b, steps.n))
            dve.reciprocal(cw_sum[:, :], cw_sum[:, :]).then_inc(m.dve_step, 1)
            steps.more()
            dve.wait_ge(m.dve_step, steps.value(b, steps.n))
            dve.tensor_tensor(cw[:, :, :], cw[:, :, :], cw_sum[:, :].rearrange("p (t a) -> p t a", a=1).to_broadcast([P, TB, E]), ALU.mult).then_inc(m.cw_ready, 1)

            dve.wait_ge(m.cwT_done, b + 1)
            dve.tensor_copy(m.cwT[:, :], ps[7][0:E, :]).then_inc(m.cwT_ready, 1)
            steps.check()


def program(nc, io, out):
    ctx = ExitStack()
    with ctx:
        tile = lambda n, s, d=F32: ctx.enter_context(nc.sbuf_tensor(n, s, d))
        sem = lambda n: ctx.enter_context(nc.semaphore(n))
        ps = [ctx.enter_context(nc.psum_tensor(f"bank{k}", [P, 512], F32)) for k in range(8)]
        x_all = tile("x_all", [P, NT, D])
        consts = (tile("ident", [P, P]), tile("mask_bias", [P, P]), tile("ident_bf", [P, P], BF16), tile("mask_bf", [P, P], BF16))
        stats = {"mean": tile("mean", [P, NT]), "scale": tile("scale", [P, NT + NC]), "gains": tile("gains", [P, 4, DC])}
        fold = {"A": tile("fold_A", [P, MH, DC, MN]), "G": tile("fold_G", [P, MH, NC, MN]), "O": tile("fold_O", [P, MH, NC, D])}
        m = shared(nc, tile, sem)
        setup(nc, io, ps, x_all, fold, stats, consts)
        credits(nc, m)
        memory_attention(nc, m, io, out, ps, x_all, fold, stats, consts, 0, beside=False)
        causal_attention(nc, m, io, ps, x_all, stats, consts, 0, "first")
        with nc.Fori(0, B - 1) as i:
            b = i + 1
            memory_attention(nc, m, io, out, ps, x_all, fold, stats, consts, b, beside=True)
            causal_attention(nc, m, io, ps, x_all, stats, consts, b, "rest")
        experts_alone(nc, m, ps, io, out, B - 1)


def kernel(**inputs):
    import numpy as np
    import concourse.bacc as bacc
    from concourse.bass_utils import run_bass_kernel_spmd as run

    at = {k: np.asarray(v) for k, v in inputs.items()}
    a, f = "L0_attn_", "L0_ffn_"
    laid = {
        "hidden": at[a + "hidden"], "memory": at[a + "memory"],
        "wq_m": at[a + "Wq"], "wkT": at[a + "Wk"].T, "wvT": at[a + "Wv"].T, "woT": at[a + "Wo"].T,
        "log_beta": at[a + "log_beta"], "g_mem": at[a + "g_mem"], "b_mem": at[a + "b_mem"],
        "gains": np.stack([at[n].reshape(DC, P).T for n in (a + "g_state", a + "b_state", f + "ln1_w", f + "ln2_w")], axis=1),
    }
    by_head = [at[f + n].reshape(DC, P, H, HD).transpose(2, 1, 0, 3) for n in ("wq", "wk", "wv")]
    rows = [np.concatenate([at[f + s_w], at[f + e_w].reshape(E * EI, D)]) for s_w, e_w in (("sg_w", "eg_w"), ("su_w", "eu_w"))]
    by_item = [r.reshape(ITEMS, ITEM, DC, P).transpose(0, 3, 2, 1) for r in rows]
    down = np.concatenate([at[f + "sd_w"].T, at[f + "ed_w"].transpose(0, 2, 1).reshape(E * EI, D)]).reshape(ITEMS, ITEM, D)
    laid.update({
        "wqkv": np.stack(by_head, axis=2), "wo": at[f + "wo"],
        "gate": at[f + "gate_w"].T, "wgu": np.stack(by_item, axis=2), "wd": down,
    })
    laid = {k: np.ascontiguousarray(v) for k, v in laid.items()}
    nc = bacc.Bacc("TRN2", target_bir_lowering=False, num_devices=1)
    io = {k: nc.dram_tensor("in_" + k, v.shape, mybir.dt.from_np(v.dtype), kind="ExternalInput").ap() for k, v in laid.items()}
    out = nc.dram_tensor("out", (B, S, D), F32, kind="ExternalOutput").ap()
    program(nc, io, out)
    return run(nc, [{"in_" + k: v for k, v in laid.items()}], core_ids=[0]).results[0]["out"]
```

```python
import concourse.bass as bass
from concourse import mybir
from contextlib import ExitStack

F32 = mybir.dt.float32
F32R = mybir.dt.float32r
BF16 = mybir.dt.bfloat16
I32 = mybir.dt.int32
ALU = mybir.AluOpType
ACT = mybir.ActivationFunctionType
AX = mybir.AxisListType

P = 128
B, S, D = 4, 512, 256
DC = D // P
TB = S // P
NT = B * TB
MH, MD, MN = 8, 128, 256
NC = MN // P
STEPS = 3
LN_EPS = 1e-5
NEWTON = 5
ACT_HEADS = 4
DVE_HEADS = MH - ACT_HEADS
H, HD = 16, 128
RMS_EPS = 1e-6
E, TOPK, EI = 16, 6, 176
ITEM = 2 * EI
CHUNKS = (P, P, ITEM - 2 * P)
NCH = len(CHUNKS)
ITEMS = 1 + E // 2
SPLIT = 4097.0
GUARD = 3e38
DVE_STEPS = 33
ROUTER_STEPS = 42


class Tally:

    def __init__(self, per_body=0, before=0):
        self.per_body, self.before, self.n = per_body, before, 0

    def more(self):
        self.n += 1
        return self.n

    def value(self, i, n):
        return i * self.per_body + (self.before + n) if self.per_body else self.before + n

    def check(self):
        assert self.n == self.per_body, (self.n, self.per_body)


def inverse_root(dve, y, arg, half, term, step_done, steps, i=0):
    dve.tensor_scalar(half.bitcast(I32), arg.bitcast(I32), 1, None, ALU.arith_shift_right).then_inc(step_done, 1)
    dve.wait_ge(step_done, steps.value(i, steps.more()))
    dve.tensor_scalar(y.bitcast(I32), half.bitcast(I32), -1.0, float(0x5F3759DF), ALU.mult, ALU.add).then_inc(step_done, 1)
    dve.wait_ge(step_done, steps.value(i, steps.more()))
    dve.tensor_scalar(half, arg, -0.5, None, ALU.mult).then_inc(step_done, 1)
    dve.wait_ge(step_done, steps.value(i, steps.more()))
    for _ in range(4):
        dve.tensor_tensor(term, half, y, ALU.mult).then_inc(step_done, 1)
        dve.wait_ge(step_done, steps.value(i, steps.more()))
        dve.tensor_tensor(term, term, y, ALU.mult).then_inc(step_done, 1)
        dve.wait_ge(step_done, steps.value(i, steps.more()))
        dve.scalar_tensor_tensor(y, term, 1.5, y, ALU.add, ALU.mult).then_inc(step_done, 1)
        dve.wait_ge(step_done, steps.value(i, steps.more()))


def setup(nc, io, ps, x_all, fold, stats, consts):
    ctx = ExitStack()
    with ctx:
        tile = lambda n, s, d=F32: ctx.enter_context(nc.sbuf_tensor(n, s, d))
        sem = lambda n: ctx.enter_context(nc.semaphore(n))
        memory = tile("memory", [P, NC, MD])
        memory_n = tile("memory_n", [P, NC, MD])
        memory_nT = tile("memory_nT", [P, MN])
        wq = tile("wq_m", [P, MH, D])
        wkT = tile("wkT", [P, MH * P])
        wvT = tile("wvT", [P, MH * P])
        woT = tile("woT", [P, MH, D])
        g_mem = tile("g_mem", [P, 1])
        b_mem = tile("b_mem", [P, 1])
        half_beta = tile("half_beta", [P, MH])
        kT = tile("kT_m", [P, 2, MN])
        vT = tile("vT_m", [P, 2, MN])
        bn = tile("bn_setup", [P, NT + NC, 6])
        mv = tile("mv_setup", [P, NT + NC, 2])
        arg = tile("arg_setup", [P, NT + NC])
        tmp = [tile(f"tmp_setup{k}", [P, NT + NC]) for k in range(2)]
        ident, mask_bias, ident_bf, mask_bf = consts

        memory_in, small_in, kv_w_in, q_w_in, o_w_in = (sem(n) for n in ("memory_in", "small_in", "kv_w_in", "q_w_in", "o_w_in"))
        tokens_in = [sem(f"tokens_in{b}") for b in range(B)]
        const_step, stats_done, root_done, memory_done = (sem(n) for n in ("const_step", "stats_done", "root_done", "memory_done"))
        memT_done, memT_ready, beta_ready = sem("memT_done"), sem("memT_ready"), sem("beta_ready")
        kv_done, fold_done = sem("kv_done"), sem("fold_done")
        kT_ready, vT_ready, g_saved, ap_saved = (sem(n) for n in ("kT_ready", "vT_ready", "g_saved", "ap_saved"))
        block = ctx.enter_context(nc.Block())

        @block.sync
        def _(sp):
            sp.dma_start(memory[:, :, :], io["memory"].rearrange("(c p) d -> p c d", p=P)).then_inc(memory_in, 16)
            for dst, name in ((g_mem, "g_mem"), (b_mem, "b_mem")):
                sp.dma_start(dst[:, :], io[name].rearrange("(p a) -> p a", a=1)).then_inc(small_in, 16)
            sp.dma_start(half_beta[:, :], io["log_beta"].rearrange("(a h) -> a h", a=1).to_broadcast([P, MH])).then_inc(small_in, 16)
            sp.dma_start(stats["gains"][:, :, :], io["gains"]).then_inc(small_in, 16)
            sp.dma_start(wkT[:, :], io["wkT"]).then_inc(kv_w_in, 16)
            sp.dma_start(wvT[:, :], io["wvT"]).then_inc(kv_w_in, 16)
            sp.dma_start(wq[:, :, :], io["wq_m"].rearrange("(h p) d -> p h d", p=P)).then_inc(q_w_in, 16)
            sp.dma_start(woT[:, :, :], io["woT"].rearrange("(h p) d -> p h d", p=P)).then_inc(o_w_in, 16)

        @block.gpsimd
        def _(pool):
            pool.memset(ident[:, :], 0.0).then_inc(const_step, 1)
            pool.memset(mask_bias[:, :], 0.0).then_inc(const_step, 1)
            pool.wait_ge(const_step, 2)
            pool.affine_select(out=ident[:, :], in_=ident[:, :], compare_op=ALU.not_equal, fill=1.0,
                               base=0, pattern=[[-1, P]], channel_multiplier=1).then_inc(const_step, 1)
            pool.affine_select(out=mask_bias[:, :], in_=mask_bias[:, :], compare_op=ALU.is_ge, fill=-1e30,
                               base=0, pattern=[[-1, P]], channel_multiplier=1).then_inc(const_step, 1)
            pool.wait_ge(const_step, 4)
            pool.tensor_copy(ident_bf[:, :], ident[:, :]).then_inc(const_step, 1)
            pool.tensor_copy(mask_bf[:, :], mask_bias[:, :]).then_inc(const_step, 1)

        @block.scalar
        def _(act):
            for b in range(B):
                act.dma_start(x_all[:, b * TB:(b + 1) * TB, :],
                              io["hidden"][b].rearrange("(t p) d -> p t d", p=P)).then_inc(tokens_in[b], 16)
            act.wait_ge(small_in, 4 * 16)
            act.activation(half_beta[:, :], half_beta[:, :], ACT.Exp).then_inc(beta_ready, 1)
            act.wait_ge(beta_ready, 1)
            act.activation(half_beta[:, :], half_beta[:, :], ACT.Copy, scale=0.5).then_inc(beta_ready, 1)
            act.wait_ge(memT_done, 1)
            act.activation(memory_nT[:, :], ps[0][:, 0:MN], ACT.Identity, bias=b_mem[:, :], scale=g_mem[:, :]).then_inc(memT_ready, 1)
            act.wait_ge(beta_ready, 2)

            def save_k(h):
                act.wait_ge(kv_done, h + 1)
                if h >= 2:
                    act.wait_ge(fold_done, h - 1)
                act.activation(kT[:, h % 2, :], ps[h % 2][:, 0:MN], ACT.Copy, scale=half_beta[:, h:h + 1]).then_inc(kT_ready, 1)

            save_k(0)
            for h in range(MH):
                if h + 1 < MH:
                    save_k(h + 1)
                act.wait_ge(fold_done, h + 1)
                act.activation(fold["G"][:, h, :, :], ps[4 + h % 2][:, :].rearrange("p (c n) -> p c n", c=NC), ACT.Copy).then_inc(g_saved, 1)

        @block.vector
        def _(dve):
            dve.wait_ge(memory_in, 16)
            for c in range(NC):
                dve.bn_stats(bn[:, NT + c, :], memory[:, c, :]).then_inc(stats_done, 1)
            for b in range(B):
                dve.wait_ge(tokens_in[b], 16)
                for t in range(b * TB, (b + 1) * TB):
                    dve.bn_stats(bn[:, t, :], x_all[:, t, :]).then_inc(stats_done, 1)
            dve.wait_ge(stats_done, NT + NC)
            for t in range(NT + NC):
                dve.bn_aggr(mv[:, t, :], bn[:, t, :]).then_inc(stats_done, 1)
            dve.wait_ge(stats_done, 2 * (NT + NC))
            dve.tensor_scalar(arg[:, 0:NT], mv[:, 0:NT, 1], 1.0 + LN_EPS, LN_EPS * LN_EPS, ALU.mult, ALU.add).then_inc(root_done, 1)
            dve.tensor_scalar(arg[:, NT:NT + NC], mv[:, NT:NT + NC, 1], LN_EPS, None, ALU.add).then_inc(root_done, 1)
            dve.wait_ge(root_done, 2)
            inverse_root(dve, stats["scale"][:, :], arg[:, :], tmp[0][:, :], tmp[1][:, :], root_done, Tally(before=2))
            dve.tensor_copy(stats["mean"][:, :], mv[:, 0:NT, 0])
            for c in range(NC):
                dve.tensor_scalar(memory_n[:, c, :], memory[:, c, :], mv[:, NT + c, 0:1], stats["scale"][:, NT + c:NT + c + 1],
                                  ALU.subtract, ALU.mult).then_inc(memory_done, 1)

            def save_v(h):
                dve.wait_ge(kT_ready, h + 1)
                if h >= 2:
                    dve.wait_ge(fold_done, h - 1)
                dve.tensor_copy(vT[:, h % 2, :], ps[h % 2][:, MN:2 * MN]).then_inc(vT_ready, 1)

            save_v(0)
            for h in range(MH):
                if h + 1 < MH:
                    save_v(h + 1)
                dve.wait_ge(fold_done, h + 1)
                dve.tensor_copy(fold["A"][:, h, :, :], ps[2 + h % 2][:, :].rearrange("p (c n) -> p c n", c=DC)).then_inc(ap_saved, 1)
                dve.tensor_copy(fold["O"][:, h, :, :], ps[6 + h % 2][:, :].rearrange("p (c n) -> p c n", c=NC)).then_inc(ap_saved, 1)

        @block.tensor
        def _(pe):
            pe.wait_ge(const_step, 3)
            for c in range(NC):
                pe.wait_ge(memory_done, c + 1)
                last = pe.transpose(ps[0][:, c * P:(c + 1) * P], memory_n[:, c, :], ident[:, :])
            last.then_inc(memT_done, 1)
            pe.wait_ge(memT_ready, 1)
            pe.wait_ge(kv_w_in, 32)

            def keys_values(h):
                if h >= 2:
                    pe.wait_ge(kT_ready, h - 1)
                    pe.wait_ge(vT_ready, h - 1)
                pe.matmul(ps[h % 2][:, 0:MN], wkT[:, h * P:(h + 1) * P], memory_nT[:, :], start=True, stop=True)
                pe.matmul(ps[h % 2][:, MN:2 * MN], wvT[:, h * P:(h + 1) * P], memory_nT[:, :], start=True, stop=True).then_inc(kv_done, 1)

            keys_values(0)
            pe.wait_ge(q_w_in, 16)
            pe.wait_ge(o_w_in, 16)
            for h in range(MH):
                if h + 1 < MH:
                    keys_values(h + 1)
                pe.wait_ge(kT_ready, h + 1)
                pe.wait_ge(vT_ready, h + 1)
                if h >= 2:
                    pe.wait_ge(ap_saved, 2 * (h - 1))
                    pe.wait_ge(g_saved, h - 1)
                k, v = kT[:, h % 2, :], vT[:, h % 2, :]
                for c in range(DC):
                    pe.matmul(ps[2 + h % 2][:, c * MN:(c + 1) * MN], wq[:, h, c * P:(c + 1) * P], k, start=True, stop=True)
                for c in range(NC):
                    pe.matmul(ps[4 + h % 2][:, c * MN:(c + 1) * MN], v[:, c * P:(c + 1) * P], k, start=True, stop=True)
                for c in range(NC):
                    last = pe.matmul(ps[6 + h % 2][:, c * D:(c + 1) * D], v[:, c * P:(c + 1) * P], woT[:, h, :], start=True, stop=True)
                last.then_inc(fold_done, 1)


class Shared:
    pass


def shared(nc, tile, sem):
    m = Shared()
    m.y = tile("y", [P, TB, D])
    m.tT = tile("tT", [P, DC, S])
    m.cwT = tile("cwT", [E, S])
    m.cw_dram = nc.dram_tensor("cw_dram", (E, S), F32, kind="Internal").ap()
    m.xn_ready, m.xnT_done, m.hT_ready = sem("xn_ready"), sem("xnT_done"), sem("hT_ready")
    m.mem_scores_done, m.mem_max_ready, m.R_ready = sem("mem_scores_done"), sem("mem_max_ready"), sem("R_ready")
    m.tau_ready, m.act_sums, m.r_final = sem("tau_ready"), sem("act_sums"), sem("r_final")
    m.rT_done, m.wT_ready, m.out_done, m.x_ready = sem("rT_done"), sem("wT_ready"), sem("out_done"), sem("x_ready")
    m.relu_done, m.stats_done, m.small_done, m.max_done = sem("relu_done"), sem("mem_stats_done"), sem("small_done"), sem("max_done")
    m.act_relu, m.router_step = sem("act_relu"), sem("router_step")
    m.wqkv_in, m.wo_in, m.gate_in, m.cw_stored = [sem("wqkv_in0"), sem("wqkv_in1")], sem("wo_in"), sem("gate_in"), sem("cw_stored")
    m.dve_step, m.norm_ready, m.normT_done, m.normT_ready = sem("dve_step"), sem("norm_ready"), sem("normT_done"), sem("normT_ready")
    m.qkv_done, m.qk_saved, m.v_saved = sem("qkv_done"), sem("qk_saved"), sem("v_saved")
    m.scores_done, m.max_ready, m.exp_done = sem("scores_done"), sem("max_ready"), sem("exp_done")
    m.w_mid_ready = sem("w_mid_ready")
    m.w_hi_ready, m.w_lo_ready, m.hT_split = sem("w_hi_ready"), sem("w_lo_ready"), sem("hT_split")
    m.rinv_ready, m.prob_ready = sem("rinv_ready"), sem("prob_ready")
    m.pT_done, m.pT_act_saved, m.pT_dve_saved = sem("pT_done"), sem("pT_act_saved"), sem("pT_dve_saved")
    m.o_done, m.o_saved, m.ao_done = sem("o_done"), sem("o_saved"), sem("ao_done")
    m.gate_done, m.shifted_ready, m.e_ready = sem("gate_done"), sem("shifted_ready"), sem("e_ready")
    m.cw_ready, m.cwT_done, m.cwT_ready = sem("cw_ready"), sem("cwT_done"), sem("cwT_ready")
    m.wgu_in, m.wd_in, m.cwB_in = ([sem(f"{n}{e}") for e in range(2)] for n in ("wgu_in", "wd_in", "cwB_in"))
    m.gu_done, m.silu_done, m.weighted_ready, m.hidden_ready = sem("gu_done"), sem("silu_done"), sem("weighted_ready"), sem("hidden_ready")
    m.down_done, m.result_ready, m.out_stored = sem("down_done"), sem("result_ready"), sem("out_stored")
    return m


def credits(nc, m):
    with nc.Block() as block:
        @block.tensor
        def _(pe):
            pe.sem_inc(m.qkv_done, 6)

        @block.scalar
        def _(act):
            act.sem_inc(m.R_ready, 2)
            act.sem_inc(m.exp_done, TB)
            act.sem_inc(m.pT_act_saved, 1)
            act.sem_inc(m.o_saved, 2)

        @block.vector
        def _(dve):
            dve.sem_inc(m.v_saved, 1)
            dve.sem_inc(m.pT_dve_saved, 1)
            dve.sem_inc(m.hidden_ready, 2)


class Experts:

    def __init__(self, nc, ctx, m, ps, io, out, b, banks):
        tile = lambda n, s, d=F32: ctx.enter_context(nc.sbuf_tensor(n, s, d))
        self.m, self.ps, self.io, self.out, self.b = m, ps, io, out, b
        self.banks = banks
        self.lag = 1 if banks[0] == banks[1] else 2
        self.wgu = tile(f"wgu_{self.lag}", [P, 2, 2, DC, ITEM])
        self.wd = tile(f"wd_{self.lag}", [P, 2, NCH, D])
        self.cwB = tile(f"cwB_{self.lag}", [P, 2, NCH, S])
        self.act_g = tile(f"act_g_{self.lag}", [P, 2, S])
        self.hidden = tile(f"hidden_{self.lag}", [P, 2, S])

    def load_weights(self, sp, idx, e):
        for lo, hi, c, w in ((0, P, 0, 0), (0, EI - P, 1, 0), (EI - P, P, 1, 1), (0, CHUNKS[2], 2, 1)):
            row = self.m.cw_dram[bass.ds(idx * 4 + (2 * e - 2 + w), 1), :]
            sp.dma_start(self.cwB[lo:hi, e, c, :], row.to_broadcast([hi - lo, S])).then_inc(self.m.cwB_in[e], 16)

    def load_gu(self, sp, idx, e):
        sp.dma_start(self.wgu[:, e, :, :, :], self.io["wgu"][idx * 2 + e]).then_inc(self.m.wgu_in[e], 16)

    def load_d(self, sp, idx, e):
        rows = self.io["wd"][idx * 2 + e]
        sp.dma_start(self.wd[:, e, 0:2, :], rows[0:2 * P, :].rearrange("(c p) n -> p c n", p=P)).then_inc(self.m.wd_in[e], 16)
        sp.dma_start(self.wd[0:CHUNKS[2], e, 2, :], rows[2 * P:ITEM, :]).then_inc(self.m.wd_in[e], 16)

    def sync(self, sp, router):
        m, b = self.m, self.b
        router.load_gate(sp)
        for e in range(2):
            self.load_gu(sp, 0, e)
            self.load_d(sp, 0, e)
        router.store_weights(sp)
        self.load_weights(sp, 0, 1)
        self.load_weights(sp, 1, 0)

        def item(idx, e):
            n = lambda k: b * (ITEMS * NCH) + (idx * (2 * NCH) + (NCH * e + k))
            sp.wait_ge(m.gu_done, n(-NCH))
            self.load_gu(sp, idx, e)
            sp.wait_ge(m.gu_done, n(-1))
            self.load_d(sp, idx, e)

        def weights(idx, e):
            sp.wait_ge(m.weighted_ready, b * (NCH * (ITEMS - 1)) + (idx * (2 * NCH) + NCH * (e - 2)))
            self.load_weights(sp, idx, e)

        item(1, 0)
        with sp.Fori(1, (ITEMS - 1) // 2) as i:
            item(i, 1)
            weights(i, 1)
            item(i + 1, 0)
            weights(i + 1, 0)
        sp.wait_ge(m.result_ready, b * TB + TB)
        sp.dma_start(self.out[b].rearrange("(t p) d -> p t d", p=P), m.y[:, :, :]).then_inc(m.out_stored, 16)

    def pool(self, pool):
        m, b = self.m, self.b
        with pool.Fori(0, (ITEMS - 1) // 2) as i:
            for e in (1, 0):
                pool.wait_ge(m.cwB_in[e], b * (64 * (ITEMS // 2)) + (i * 64 + 64))
                for c, rows in enumerate(CHUNKS):
                    k = NCH * (2 - e) + c
                    pool.wait_ge(m.silu_done, b * (ITEMS * NCH) + (i * (2 * NCH) + k + 1))
                    pool.tensor_tensor(self.act_g[0:rows, k % 2, :], self.act_g[0:rows, k % 2, :], self.cwB[0:rows, e, c, :], ALU.mult) \
                        .then_inc(m.weighted_ready, 1)

    def gate_up(self, pe, n, c, e, idx, par):
        m, b = self.m, self.b
        if c == 0:
            pe.wait_ge(m.wgu_in[e], b * (16 * (5 - e)) + (idx * 16 + 16))
        pe.wait_ge(m.hidden_ready, b * (ITEMS * NCH) + (n + (3 - self.lag)))
        rows = CHUNKS[c]
        for which in range(2):
            for k in range(DC):
                last = pe.matmul(self.ps[self.banks[par][which]][0:rows, :], self.wgu[:, e, which, k, c * P:c * P + rows], m.tT[:, k, :],
                                 start=(k == 0), stop=(k == DC - 1))
        last.then_inc(m.gu_done, 1)

    def down(self, pe, n, c, e, idx, par, start=False, stop=False):
        m, b = self.m, self.b
        if c == 0:
            pe.wait_ge(m.wd_in[e], b * (32 * (5 - e)) + (idx * 32 + 32))
        pe.wait_ge(m.hidden_ready, b * (ITEMS * NCH) + (n + 3))
        rows = CHUNKS[c]
        for t in range(TB):
            last = pe.matmul(self.ps[4 + t // 2][:, (t % 2) * D:(t % 2 + 1) * D], self.hidden[0:rows, par, t * P:(t + 1) * P],
                             self.wd[0:rows, e, c, :], start=start and t % 2 == 0, stop=stop and t % 2 == 1)
        if stop:
            last.then_inc(m.down_done, 1)

    def silu(self, act, n, c, par):
        m, b, rows = self.m, self.b, CHUNKS[c]
        act.wait_ge(m.gu_done, b * (ITEMS * NCH) + (n + 1))
        act.activation(self.act_g[0:rows, par, :], self.ps[self.banks[par][0]][0:rows, :], ACT.Silu).then_inc(m.silu_done, 1)

    def hide(self, dve, n, c, par, routed):
        m, b, rows = self.m, self.b, CHUNKS[c]
        if routed:
            dve.wait_ge(m.weighted_ready, b * (NCH * (ITEMS - 1)) + (n - NCH + 1))
        else:
            dve.wait_ge(m.silu_done, b * (ITEMS * NCH) + (n + 1))
        dve.tensor_tensor(self.hidden[0:rows, par, :], self.act_g[0:rows, par, :], self.ps[self.banks[par][1]][0:rows, :], ALU.mult) \
           .then_inc(m.hidden_ready, 1)

    def result(self, dve):
        m, b = self.m, self.b
        dve.wait_ge(m.down_done, b + 1)
        for t in range(TB):
            dve.tensor_tensor(m.y[:, t, :], m.y[:, t, :], self.ps[4 + t // 2][:, (t % 2) * D:(t % 2 + 1) * D], ALU.add) \
               .then_inc(m.result_ready, 1)


class Router:

    def __init__(self, nc, ctx, m, ps, io, x_all, stats, hn, b, where):
        tile = lambda n, s, d=F32: ctx.enter_context(nc.sbuf_tensor(f"{n}_{where}", s, d))
        self.m, self.ps, self.io, self.b = m, ps, io, b
        self.x_all, self.stats, self.hn = x_all, stats, hn
        self.bn, self.mv = tile("bn_y", [P, TB, 6]), tile("mv_y", [P, TB, 2])
        self.arg, self.root, self.half, self.term = (tile(n, [P, TB]) for n in ("arg_y", "root_y", "half_y", "term_y"))
        self.gate = tile("gate", [P, DC, E])
        self.logits = tile("logits", [P, TB, E + 2])
        self.marked = tile("marked", [P, TB, E + 2])
        self.top = tile("top", [P, TB, 8])
        self.cw = tile("cw", [P, TB, E])
        self.cw_sum = tile("cw_sum", [P, TB])

    def load_gate(self, sp):
        sp.dma_start(self.gate[:, :, :], self.io["gate"].rearrange("(c p) n -> p c n", p=P)).then_inc(self.m.gate_in, 16)

    def store_weights(self, sp):
        m, b = self.m, self.b
        sp.wait_ge(m.cwT_ready, b + 1)
        sp.dma_start(m.cw_dram, m.cwT[:, :]).then_inc(m.cw_stored, 16)
        sp.wait_ge(m.cw_stored, b * 16 + 16)
        sp.nop(nofuse=True)

    def normalise_tokens(self, dve):
        m, b, bn, mv, arg, root = self.m, self.b, self.bn, self.mv, self.arg, self.root
        self.steps = steps = Tally(per_body=ROUTER_STEPS)
        for t in range(TB):
            dve.bn_stats(bn[:, t, :], m.y[:, t, :]).then_inc(m.router_step, 1)
            steps.more()
        dve.wait_ge(m.router_step, steps.value(b, steps.n))
        dve.nop(nofuse=True)
        for t in range(TB):
            dve.bn_aggr(mv[:, t, :], bn[:, t, :]).then_inc(m.router_step, 1)
            steps.more()
        dve.wait_ge(m.router_step, steps.value(b, steps.n))
        dve.tensor_tensor(arg[:, :], mv[:, :, 0], mv[:, :, 0], ALU.mult).then_inc(m.router_step, 1)
        steps.more()
        dve.wait_ge(m.router_step, steps.value(b, steps.n))
        dve.scalar_tensor_tensor(arg[:, :], arg[:, :], RMS_EPS, mv[:, :, 1], ALU.add, ALU.add).then_inc(m.router_step, 1)
        steps.more()
        dve.wait_ge(m.router_step, steps.value(b, steps.n))
        inverse_root(dve, root[:, :], arg[:, :], self.half[:, :], self.term[:, :], m.router_step, steps, b)
        for t in range(TB):
            dve.tensor_scalar(self.hn[t][0], m.y[:, t, :].rearrange("p (c n) -> p c n", c=DC), root[:, t:t + 1], None, ALU.mult) \
               .then_inc(m.norm_ready, 1)
        for t in range(TB):
            dve.tensor_tensor(m.y[:, t, :], m.y[:, t, :], self.x_all[:, b * TB + t, :], ALU.add).then_inc(m.router_step, 1)
            steps.more()

    def transpose_tokens(self, pe, ident):
        m, b = self.m, self.b
        for t in range(TB):
            pe.wait_ge(m.norm_ready, b * (2 * TB) + (TB + t + 1))
            for c in range(DC):
                last = pe.transpose(self.ps[4 + c][:, t * P:(t + 1) * P], self.hn[t][1][c], ident[:, :])
        last.then_inc(m.normT_done, DC)

    def keep_tokens(self, act):
        m, b = self.m, self.b
        for c in range(DC):
            act.wait_ge(m.normT_done, b * (2 * DC) + 2 * DC)
            act.activation(m.tT[:, c, :], self.ps[4 + c][:, :], ACT.Copy, scale=self.stats["gains"][:, 3, c:c + 1]).then_inc(m.normT_ready, 1)

    def products(self, pe):
        m, b = self.m, self.b
        pe.wait_ge(m.normT_ready, b * (2 * DC) + 2 * DC)
        pe.wait_ge(m.gate_in, b * 16 + 16)
        for t in range(TB):
            for c in range(DC):
                last = pe.matmul(self.ps[2][:, t * E:(t + 1) * E], m.tT[:, c, t * P:(t + 1) * P], self.gate[:, c, :],
                                 start=(c == 0), stop=(c == DC - 1))
        last.then_inc(m.gate_done, 1)

    def transpose(self, pe, ident):
        m, b = self.m, self.b
        pe.wait_ge(m.cw_ready, b + 1)
        for t in range(TB):
            last = pe.transpose(self.ps[3][0:E, t * P:(t + 1) * P], self.cw[:, t, :], ident[:, :])
        last.then_inc(m.cwT_done, 1)

    def exponentials(self, act):
        act.wait_ge(self.m.shifted_ready, self.b + 1)
        act.activation(self.cw[:, :, :], self.logits[:, :, 0:E], ACT.Exp).then_inc(self.m.e_ready, 1)

    def select(self, dve):
        m, b, steps = self.m, self.b, self.steps
        dve.memset(self.logits[:, :, E:E + 2], GUARD).then_inc(m.router_step, 1)
        steps.more()
        dve.wait_ge(m.gate_done, b + 1)
        dve.tensor_copy(self.logits[:, :, 0:E], self.ps[2][:, 0:TB * E].rearrange("p (t e) -> p t e", t=TB)).then_inc(m.router_step, 1)
        steps.more()
        dve.wait_ge(m.router_step, steps.value(b, steps.n))
        dve.nop(nofuse=True)
        for t in range(TB):
            dve.max(self.top[:, t, :], self.logits[:, t, :]).then_inc(m.router_step, 1)
            steps.more()
        dve.wait_ge(m.router_step, steps.value(b, steps.n))
        dve.nop(nofuse=True)
        for t in range(TB):
            dve.match_replace(self.marked[:, t, :], self.top[:, t, :], self.logits[:, t, :], -GUARD).then_inc(m.router_step, 1)
            steps.more()
        dve.wait_ge(m.router_step, steps.value(b, steps.n))
        dve.tensor_tensor(self.logits[:, :, 0:E], self.logits[:, :, 0:E], self.top[:, :, 2:3].to_broadcast([P, TB, E]),
                          ALU.subtract).then_inc(m.shifted_ready, 1)

    def normalise(self, dve):
        m, b, steps, cw, cw_sum = self.m, self.b, self.steps, self.cw, self.cw_sum
        dve.wait_ge(m.e_ready, b + 1)
        dve.scalar_tensor_tensor(cw[:, :, :], self.marked[:, :, 0:E], -GUARD, cw[:, :, :], ALU.is_le, ALU.mult).then_inc(m.router_step, 1)
        steps.more()
        dve.wait_ge(m.router_step, steps.value(b, steps.n))
        dve.tensor_reduce(cw_sum[:, :], cw[:, :, :], op=ALU.add, axis=AX.X).then_inc(m.router_step, 1)
        steps.more()
        dve.wait_ge(m.router_step, steps.value(b, steps.n))
        dve.reciprocal(cw_sum[:, :], cw_sum[:, :]).then_inc(m.router_step, 1)
        steps.more()
        dve.wait_ge(m.router_step, steps.value(b, steps.n))
        dve.tensor_tensor(cw[:, :, :], cw[:, :, :], cw_sum[:, :].rearrange("p (t a) -> p t a", a=1).to_broadcast([P, TB, E]), ALU.mult) \
           .then_inc(m.cw_ready, 1)
        steps.check()

    def keep_transposed(self, dve):
        m, b = self.m, self.b
        dve.wait_ge(m.cwT_done, b + 1)
        dve.tensor_copy(m.cwT[:, :], self.ps[3][0:E, :]).then_inc(m.cwT_ready, 1)


def experts_alone(nc, m, ps, io, out, x_all, stats, consts, b):
    with ExitStack() as ctx:
        x = Experts(nc, ctx, m, ps, io, out, b, ((6, 7), (0, 1)))
        hn = ctx.enter_context(nc.sbuf_tensor("hn_alone", [P, TB, DC, P], F32))
        parts = [(hn[:, t, :, :], [hn[:, t, c, :] for c in range(DC)]) for t in range(TB)]
        router = Router(nc, ctx, m, ps, io, x_all, stats, parts, b, "alone")
        block = ctx.enter_context(nc.Block())
        PAIRS = (ITEMS - 1) // 2

        @block.sync
        def _(sp):
            x.sync(sp, router)
            sp.wait_ge(m.out_stored, 16 * B)

        @block.gpsimd
        def _(pool):
            x.pool(pool)

        @block.tensor
        def _(pe):
            router.transpose_tokens(pe, consts[0])
            router.products(pe)
            for c in range(NCH):
                x.gate_up(pe, c, c, 0, 0, c % 2)
                if c:
                    x.down(pe, c - 1, c - 1, 0, 0, (c - 1) % 2, start=(c == 1))
                if c == 1:
                    router.transpose(pe, consts[0])
            with pe.Fori(0, PAIRS) as i:
                for k in range(2 * NCH):
                    item, c = divmod(k, NCH)
                    x.gate_up(pe, i * (2 * NCH) + (NCH + k), c, 1 - item, i + item, (NCH + k) % 2)
                    before, c = divmod(k - 1, NCH)
                    x.down(pe, i * (2 * NCH) + (NCH + k - 1), c, (1 - before) % 2, i + max(before, 0), (NCH + k - 1) % 2)
            x.down(pe, ITEMS * NCH - 1, NCH - 1, 0, 4, 0, stop=True)

        @block.scalar
        def _(act):
            router.keep_tokens(act)
            for c in range(NCH):
                x.silu(act, c, c, c % 2)
                if c == 0:
                    router.exponentials(act)
            with act.Fori(0, PAIRS) as i:
                for k in range(2 * NCH):
                    x.silu(act, i * (2 * NCH) + (NCH + k), k % NCH, (NCH + k) % 2)

        @block.vector
        def _(dve):
            router.normalise_tokens(dve)
            router.select(dve)
            for c in range(NCH):
                x.hide(dve, c, c, c % 2, False)
                if c == 0:
                    router.normalise(dve)
                if c == 1:
                    router.keep_transposed(dve)
            with dve.Fori(0, PAIRS) as i:
                for k in range(2 * NCH):
                    x.hide(dve, i * (2 * NCH) + (NCH + k), k % NCH, (NCH + k) % 2, True)
            x.result(dve)


def memory_attention(nc, m, io, out, ps, x_all, fold, stats, consts, b, beside):
    PAIRS = ((0, 1), (2, 3))
    ctx = ExitStack()
    with ctx:
        tile = lambda n, s, d=F32: ctx.enter_context(nc.sbuf_tensor(f"{n}_{beside}", s, d))
        xn = tile("xn", [P, TB, D])
        hT = tile("hT_m", [P, TB, DC, P])
        R = tile("R", [P, TB, MH, MN])
        r = tile("r", [P, 2, DVE_HEADS, MN])
        r_act = tile("r_act", [P, 2, ACT_HEADS, MN])
        wT = tile("wT", [P, TB, MH, NC, P])
        mx = tile("mx", [P, TB, MH])
        one_less_max = tile("one_less_max", [P, TB, MH])
        neg_tau = tile("neg_tau", [P, TB, MH])
        bn = tile("bn", [P, TB, MH, 6])
        halves = tile("halves", [P, TB, MH, 2, 2])
        sums = tile("sums", [P, TB, MH, 2])
        den = tile("den", [P, TB, MH])
        num = tile("num", [P, TB, MH])
        ident = consts[0]

        parts = [(wT[:, TB - 1, t, :, :], [wT[:, TB - 1, t, c, :] for c in range(DC)]) for t in range(TB)]
        router = Router(nc, ctx, m, ps, io, x_all, stats, parts, b - 1, "beside") if beside else None
        experts = Experts(nc, ctx, m, ps, io, out, b - 1, ((6, 7), (6, 7))) if beside else None
        block = ctx.enter_context(nc.Block())
        NS = STEPS * TB
        nth = lambda s, t: s * TB + t
        HALVES = {k: ((k - 1) // 2, (k - 1) % 2) for k in range(1, 5)}
        score_bank = lambda s, t, u: (0, 1, 6, 7)[u // 2] if nth(s, t) < 2 else (u // 2) % 2
        tick = lambda s, pair, k: (s * 2 + pair[0] // 2) * NEWTON + k

        if beside:
            @block.sync
            def _(sp):
                experts.sync(sp, router)

            @block.gpsimd
            def _(pool):
                experts.pool(pool)

        @block.tensor
        def _(pe):
            def scores(t, s, half):
                if s == 0:
                    pe.wait_ge(m.hT_ready, b * TB + (t + 1))
                else:
                    pe.wait_ge(m.wT_ready, b * (NS * 4) + (4 * nth(s - 1, t) + 4))
                for u in range(4 * half, 4 * half + 4):
                    bank, at = ps[score_bank(s, t, u)], (u % 2) * MN
                    if nth(s, t) == 0:
                        pass
                    elif u % 2 == 0 and nth(s, t) == 1:
                        pe.wait_ge(m.R_ready, b * (NS * 4) + (2 + u // 2 + 1))
                    elif u % 2 == 0:
                        pe.wait_ge(m.R_ready, b * (NS * 4) + (4 * nth(s, t) + u // 2 + 1))
                    for c in range(NC):
                        lhsT, rhs = (hT[:, t, c, :], fold["A"][:, u, c, :]) if s == 0 else (wT[:, t, u, c, :], fold["G"][:, u, c, :])
                        last = pe.matmul(bank[:, at:at + MN], lhsT, rhs, start=(c == 0), stop=(c == NC - 1))
                    if u % 2:
                        last.then_inc(m.mem_scores_done, 1)

            def transpose_r(t, s):
                n = nth(s, t)
                pe.wait_ge(m.r_final, b * NS + (n + 1))
                for u in range(MH):
                    bank, at = ps[2 + (u // 2) % 2], (u % 2) * MN
                    if u % 2 == 0:
                        if n == 0 and u < 4:
                            pe.wait_ge(m.hT_ready, b * TB + TB)
                            if beside:
                                pe.wait_ge(m.cwT_ready, b)
                        elif s == STEPS - 1 and t == 2 and u < 4:
                            pe.wait_ge(m.x_ready, b * TB + 2)
                        else:
                            pe.wait_ge(m.wT_ready, b * (NS * 4) + (4 * n + u // 2 - 1))
                    for c in range(NC):
                        last = pe.transpose(bank[:, at + c * P:at + (c + 1) * P], R[:, t, u, c * P:(c + 1) * P], ident[:, :])
                    if u % 2:
                        last.then_inc(m.rT_done, 1)

            def project(t):
                pe.wait_ge(m.wT_ready, b * (NS * 4) + (4 * nth(STEPS - 1, t - t % 2 + 1) + 4))
                for u in range(MH):
                    for c in range(NC):
                        last = pe.matmul(ps[2 + t % 2][:, 0:D], wT[:, t, u, c, :], fold["O"][:, u, c, :],
                                         start=(u == 0 and c == 0), stop=(u == MH - 1 and c == NC - 1))
                last.then_inc(m.out_done, 1)

            def chunk(n):
                if beside and n == 0:
                    pe.wait_ge(m.R_ready, b * (NS * 4) + (2 + 2 * 4))
                if beside and n < ITEMS * NCH:
                    j, c = divmod(n, NCH)
                    experts.gate_up(pe, n, c, j % 2, j // 2, n % 2)
                if beside and 1 <= n <= ITEMS * NCH:
                    j, c = divmod(n - 1, NCH)
                    experts.down(pe, n - 1, c, j % 2, j // 2, (n - 1) % 2, start=(n == 1), stop=(n == ITEMS * NCH))

            for t in range(TB):
                pe.wait_ge(m.xn_ready, b * TB + (t + 1))
                if t >= 2:
                    pe.wait_ge(m.hT_ready, b * TB + (t - 1))
                for c in range(DC):
                    last = pe.transpose(ps[2 + t % 2][:, c * P:(c + 1) * P], xn[:, t, c * P:(c + 1) * P], ident[:, :])
                last.then_inc(m.xnT_done, 1)
            for t in PAIRS[0]:
                for half in range(2):
                    scores(t, 0, half)
                    if beside and (t, half) == (0, 1):
                        router.transpose_tokens(pe, ident)
                    if beside and (t, half) == (1, 0):
                        pe.wait_ge(m.hT_ready, b * TB + TB)
                        router.products(pe)
            if beside:
                router.transpose(pe, ident)
            for s in range(STEPS):
                for pair, other in (PAIRS, PAIRS[::-1]):
                    coming = s if pair == PAIRS[0] else s + 1
                    last_s = s - 1 if pair == PAIRS[0] else s
                    if last_s >= 0:
                        for t in other:
                            transpose_r(t, last_s)
                    chunk(tick(s, pair, 0))
                    for k in range(1, NEWTON):
                        i, half = HALVES[k]
                        if coming < STEPS:
                            scores(other[i], coming, half)
                        chunk(tick(s, pair, k))
                        if coming == STEPS and k == NEWTON - 2:
                            for t in other:
                                project(t)
            for t in PAIRS[1]:
                transpose_r(t, STEPS - 1)
            for t in PAIRS[1]:
                project(t)

        @block.scalar
        def _(act):
            relus = Tally(per_body=STEPS * TB * (NEWTON - 1) * ACT_HEADS)

            def save_scores(t, s, half):
                act.wait_ge(m.mem_max_ready, b * (NS * 2) + (2 * nth(s, t) + half + 1))
                for u in range(4 * half, 4 * half + 4):
                    last = act.activation(R[:, t, u, :], ps[score_bank(s, t, u)][:, (u % 2) * MN:(u % 2 + 1) * MN], ACT.Relu,
                                          bias=one_less_max[:, t, u:u + 1])
                    if u % 2:
                        last.then_inc(m.R_ready, 1)

            def share(k, i, pair, s):
                t = pair[i]
                act.wait_ge(m.tau_ready, b * (NS * NEWTON) + (nth(s, pair[0]) * NEWTON + 2 * (k - 1) + i + 1))
                for j in range(ACT_HEADS):
                    u = DVE_HEADS + j
                    act.activation(r_act[:, i, j, :], R[:, t, u, :], ACT.Relu, bias=neg_tau[:, t, u:u + 1],
                                   accum_out=sums[:, t, u, 0:1]).then_inc(m.act_relu, 1)
                    relus.more()
                for j in range(ACT_HEADS):
                    u = DVE_HEADS + j
                    act.wait_ge(m.act_relu, relus.value(b, relus.n - ACT_HEADS + j + 1))
                    last = act.activation(r_act[:, i, j, :], r_act[:, i, j, :], ACT.Square, accum_out=sums[:, t, u, 1:2])
                last.then_inc(m.act_sums, 1)

            def save_weights(t, s):
                for u in range(0, MH, 2):
                    act.wait_ge(m.rT_done, b * (NS * 4) + (4 * nth(s, t) + u // 2 + 1))
                    act.activation(wT[:, t, u:u + 2, :, :], ps[2 + (u // 2) % 2][:, :], ACT.Square).then_inc(m.wT_ready, 1)

            def chunk(n):
                if beside and 0 <= n < ITEMS * NCH:
                    experts.silu(act, n, n % NCH, n % 2)

            for t in range(TB):
                act.wait_ge(m.xnT_done, b * TB + (t + 1))
                for c in range(DC):
                    last = act.activation(hT[:, t, c, :], ps[2 + t % 2][:, c * P:(c + 1) * P], ACT.Identity,
                                          bias=stats["gains"][:, 1, c:c + 1], scale=stats["gains"][:, 0, c:c + 1])
                last.then_inc(m.hT_ready, 1)
            for t in PAIRS[0]:
                for half in range(2):
                    save_scores(t, 0, half)
                    if beside and (t, half) == (0, 1):
                        router.keep_tokens(act)
                    if beside and (t, half) == (1, 0):
                        router.exponentials(act)
            for s in range(STEPS):
                for pair, other in (PAIRS, PAIRS[::-1]):
                    coming = s if pair == PAIRS[0] else s + 1
                    last_s = s - 1 if pair == PAIRS[0] else s
                    chunk(tick(s, pair, 0) - 1)
                    if last_s >= 0:
                        for t in other:
                            save_weights(t, last_s)
                    for k in range(1, NEWTON):
                        chunk(tick(s, pair, k) - 1)
                        share(k, 0, pair, s)
                        share(k, 1, pair, s)
                        i, half = HALVES[k]
                        if coming < STEPS:
                            save_scores(other[i], coming, half)
            for t in PAIRS[1]:
                save_weights(t, STEPS - 1)
            relus.check()

        @block.vector
        def _(dve):
            relu_n = Tally(per_body=NS * (NEWTON - 1) * DVE_HEADS)
            stats_n = Tally(per_body=NS * (MH + (NEWTON - 1) * DVE_HEADS))
            small_n = Tally(per_body=NS * NEWTON * 8)
            max_n = Tally(per_body=NS * 4)
            for t in range(TB):
                dve.tensor_scalar(xn[:, t, :], x_all[:, b * TB + t, :], stats["mean"][:, bass.ds(b * TB + t, 1)],
                                  stats["scale"][:, bass.ds(b * TB + t, 1)], ALU.subtract, ALU.mult).then_inc(m.xn_ready, 1)
            if beside:
                router.normalise_tokens(dve)

            def maxima(t, s, half):
                for j in (2 * half, 2 * half + 1):
                    dve.wait_ge(m.mem_scores_done, b * (NS * 4) + (4 * nth(s, t) + j + 1))
                    dve.tensor_reduce(mx[:, t, 2 * j:2 * j + 2], ps[score_bank(s, t, 2 * j)][:, :].rearrange("p (u n) -> p u n", u=2),
                                                   op=ALU.max, axis=AX.X).then_inc(m.max_done, 1)
                    max_n.more()
                dve.wait_ge(m.max_done, max_n.value(b, max_n.n))
                heads = slice(4 * half, 4 * half + 4)
                dve.tensor_scalar(one_less_max[:, t, heads], mx[:, t, heads], -1.0, 1.0, ALU.mult, ALU.add).then_inc(m.mem_max_ready, 1)

            sums_end = {}
            small_at = {}

            def taus(t, k, s):
                return b * (NS * NEWTON) + (nth(s, t - t % 2) * NEWTON + 2 * k + t % 2 + 1)

            def update(t, k, s, i):
                w = MH if k == 0 else DVE_HEADS
                bnv = bn[:, t, 0:w, :].rearrange("p u (e q) -> p u e q", e=2)
                if i == 0:
                    dve.wait_ge(m.stats_done, stats_n.value(b, sums_end[t]))
                    dve.tensor_tensor(halves[:, t, 0:w, 1, :], bnv[:, :, :, 1], bnv[:, :, :, 1], ALU.mult).then_inc(m.small_done, 1)
                    small_at[t] = small_n.more()
                elif i == 1:
                    dve.tensor_scalar(halves[:, t, 0:w, 0, :], bnv[:, :, :, 1], MN / 2.0, None, ALU.mult).then_inc(m.small_done, 1)
                    small_n.more()
                    dve.wait_ge(m.small_done, small_n.value(b, small_at[t]))
                    dve.scalar_tensor_tensor(halves[:, t, 0:w, 1, :], halves[:, t, 0:w, 1, :], MN / 2.0,
                                             bnv[:, :, :, 2], ALU.mult, ALU.add).then_inc(m.small_done, 1)
                    small_at[t] = small_n.more()
                elif i == 2:
                    dve.wait_ge(m.small_done, small_n.value(b, small_at[t]))
                    dve.tensor_tensor(sums[:, t, 0:w, :], halves[:, t, 0:w, :, 0], halves[:, t, 0:w, :, 1], ALU.add).then_inc(m.small_done, 1)
                    small_at[t] = small_n.more()
                elif i == 4:
                    dve.wait_ge(m.small_done, small_n.value(b, small_at[t]))
                    if k > 0:
                        dve.wait_ge(m.act_sums, b * (NS * (NEWTON - 1)) + (nth(s, t - t % 2) * (NEWTON - 1) + 2 * (k - 1) + t % 2 + 1))
                    dve.scalar_tensor_tensor(den[:, t, :], sums[:, t, :, 1], 3.0, sums[:, t, :, 0], ALU.add, ALU.mult).then_inc(m.small_done, 1)
                    small_at[t] = small_n.more()
                    dve.tensor_tensor(num[:, t, :], sums[:, t, :, 1], sums[:, t, :, 1], ALU.mult).then_inc(m.small_done, 1)
                    small_n.more()
                elif i == 5:
                    dve.wait_ge(m.small_done, small_n.value(b, small_at[t]))
                    dve.reciprocal(den[:, t, :], den[:, t, :]).then_inc(m.small_done, 1)
                    small_at[t] = small_n.more()
                elif i == 6:
                    dve.wait_ge(m.small_done, small_n.value(b, small_at[t]))
                    dve.scalar_tensor_tensor(num[:, t, :], num[:, t, :], -1.0, den[:, t, :], ALU.add, ALU.mult).then_inc(m.small_done, 1)
                    small_at[t] = small_n.more()
                elif i == 7:
                    dve.wait_ge(m.small_done, small_n.value(b, small_at[t]))
                    if k == 0:
                        dve.tensor_scalar(neg_tau[:, t, :], num[:, t, :], -1.0, None, ALU.mult).then_inc(m.tau_ready, 1)
                    else:
                        dve.tensor_tensor(neg_tau[:, t, :], neg_tau[:, t, :], num[:, t, :], ALU.subtract).then_inc(m.tau_ready, 1)

            def chunk(n):
                if beside and 0 <= n < ITEMS * NCH:
                    experts.hide(dve, n, n % NCH, n % 2, n >= NCH)

            def first_sweep(t, s, between):
                for u in range(MH):
                    dve.wait_ge(m.R_ready, b * (NS * 4) + (2 + 4 * nth(s, t) + u // 2 + 1))
                    dve.bn_stats(bn[:, t, u, :], R[:, t, u, :]).then_inc(m.stats_done, 1)
                    n = stats_n.more()
                    if between:
                        update(*between, u)
                sums_end[t] = n

            def sweep(t, k, s, between, n_chunk=-1):
                dve.wait_ge(m.tau_ready, taus(t, k - 1, s))
                first = relu_n.n
                part = 0
                for u in range(DVE_HEADS + 1):
                    if u < DVE_HEADS:
                        dve.tensor_scalar(r[:, t % 2, u, :], R[:, t, u, :], neg_tau[:, t, u:u + 1], 0.0, ALU.add, ALU.max).then_inc(m.relu_done, 1)
                        relu_n.more()
                        if u == 0:
                            chunk(n_chunk)
                        if part < 8:
                            update(*between, part)
                            part += 1
                    if u >= 1:
                        dve.wait_ge(m.relu_done, relu_n.value(b, first + u))
                        dve.bn_stats(bn[:, t, u - 1, :], r[:, t % 2, u - 1, :]).then_inc(m.stats_done, 1)
                        sums_end[t] = stats_n.more()
                        if part < 8:
                            update(*between, part)
                            part += 1

            def final(t, s, between):
                dve.wait_ge(m.tau_ready, taus(t, NEWTON - 1, s))
                for u in range(MH):
                    last = dve.tensor_scalar(R[:, t, u, :], R[:, t, u, :], neg_tau[:, t, u:u + 1], 0.0, ALU.add, ALU.max)
                    if between:
                        update(*between, u)
                last.then_inc(m.r_final, 1)

            def output(pair):
                for t in pair:
                    dve.wait_ge(m.out_done, b * TB + (t + 1))
                    dve.tensor_tensor(x_all[:, b * TB + t, :], x_all[:, b * TB + t, :], ps[2 + t % 2][:, 0:D], ALU.add).then_inc(m.x_ready, 1)

            for t in PAIRS[0]:
                for half in range(2):
                    maxima(t, 0, half)
                    if beside and (t, half) == (1, 0):
                        router.select(dve)
            if beside:
                router.normalise(dve)
                router.keep_transposed(dve)
            for s in range(STEPS):
                for pair, other in (PAIRS, PAIRS[::-1]):
                    coming = s if pair == PAIRS[0] else s + 1
                    a, z = pair
                    first_sweep(a, s, None)
                    chunk(tick(s, pair, 0) - 1)
                    first_sweep(z, s, (a, 0, s))
                    for k in range(1, NEWTON):
                        i, half = HALVES[k]
                        sweep(a, k, s, (z, k - 1, s))
                        sweep(z, k, s, (a, k, s), tick(s, pair, k) - 1)
                        if coming < STEPS:
                            maxima(other[i], coming, half)
                        if coming == STEPS and k == NEWTON - 1:
                            output(other)
                    final(a, s, (z, NEWTON - 1, s))
                    final(z, s, None)
            if beside:
                experts.result(dve)
            output(PAIRS[1])
            for tally in (relu_n, stats_n, small_n, max_n):
                tally.check()


def causal_attention(nc, m, io, ps, x_all, stats, consts, b, where):
    ctx = ExitStack()
    with ctx:
        tile = lambda n, s, d=F32: ctx.enter_context(nc.sbuf_tensor(f"{n}_{where}", s, d))
        ident, _, ident_bf, mask_bf = consts
        wo = tile("wo", [P, H, D])
        wqkv = tile("wqkv", [P, 2, 3, DC, HD])
        w_hi, w_lo = tile("w_hi", [P, 2, 2, DC, HD], F32R), tile("w_lo", [P, 2, 2, DC, HD], F32R)
        hT_hi, hT_lo = tile("hT_hi", [P, DC, S], F32R), tile("hT_lo", [P, DC, S], F32R)
        w_mid, hT_mid = tile("w_mid", [P, 2, DC, HD]), tile("hT_mid", [P, DC, S])
        hn = tile("hn", [P, TB, D])
        hT = tile("hT", [P, DC, S])
        qT = tile("qT", [P, S])
        kT = tile("kT", [P, S])
        v = tile("v", [P, 2, TB, HD])
        prob = tile("prob", [P, TB, S])
        probT = tile("probT", [P, TB, S])
        oT = tile("oT", [P, H, S])
        bn = tile("bn_d", [P, TB, 6])
        mv = tile("mv_d", [P, TB, 2])
        arg, root, half, term = (tile(n, [P, 2 * TB]) for n in ("arg", "root", "half", "term"))
        nmax, rowsum, rinv = tile("nmax", [P, TB]), tile("rowsum", [P, TB]), tile("rinv", [P, TB])
        block = ctx.enter_context(nc.Block())
        T_GROUPS = ((6, (0,)), (7, (1, 3)), (6, (2,)))

        @block.sync
        def _(sp):
            with sp.Fori(0, H // 2) as i:
                for e in range(2):
                    sp.wait_ge(m.qkv_done, b * (3 * H) + (i * 6 + (3 * e + 3)))
                    sp.dma_start(wqkv[:, e, :, :, :], io["wqkv"][i * 2 + e]).then_inc(m.wqkv_in[e], 16)

        @block.gpsimd
        def _(pool):
            def scale(h):
                pool.wait_ge(m.rinv_ready, b * H + (h + 1))
                pool.nop(nofuse=True)
                for t in range(TB):
                    w = (t + 1) * P
                    pool.tensor_scalar(prob[:, t, 0:w], prob[:, t, 0:w], rinv[:, t:t + 1], 1.0, ALU.mult, ALU.mult).then_inc(m.prob_ready, 1)

            def rest(h, e):
                pool.wait_ge(m.w_hi_ready, b * (H - 1) + h)
                pool.tensor_tensor(w_lo[:, e, :, :, :], wqkv[:, e, 0:2, :, :], w_hi[:, e, :, :, :].bitcast(F32), ALU.subtract).then_inc(m.w_lo_ready, 1)

            rest(1, 1)
            with pool.Fori(0, H // 2 - 1) as i:
                for e in range(2):
                    scale(i * 2 + e)
                    rest(i * 2 + (e + 2), e)
            scale(H - 2)
            scale(H - 1)

        @block.tensor
        def _(pe):
            def transpose_norm(b):
                for t in range(TB):
                    pe.wait_ge(m.norm_ready, b * (2 * TB) + (t + 1))
                    for c in range(DC):
                        ins = pe.transpose(ps[4 + c][:, t * P:(t + 1) * P], hn[:, t, c * P:(c + 1) * P], ident[:, :])
                        if t == TB - 1:
                            ins.then_inc(m.normT_done, 1)

            def qkv(b, h, e, idx, whole):
                g = b * H + h
                if not whole:
                    pe.wait_ge(m.w_lo_ready, b * (H - 1) + h)
                    pe.wait_ge(m.hT_split, 3 * b + 3)
                pe.wait_ge(m.wqkv_in[e], b * (8 * H) + (idx * 16 + 16))
                pe.wait_ge(m.v_saved, g + 1)
                for which in range(2):
                    if which == 1:
                        pe.wait_ge(m.o_saved, g + 1)
                    if whole:
                        parts = ((wqkv, hT),)
                    else:
                        parts = ((w_hi, hT_hi), (w_hi, hT_lo), (w_lo, hT_hi))
                    for k, (w_part, h_part) in enumerate(parts):
                        for c in range(DC):
                            last = pe.matmul(ps[4 + which][:, :], w_part[:, e, which, c, :], h_part[:, c, :],
                                             start=(k == 0 and c == 0), stop=(k == len(parts) - 1 and c == DC - 1))
                    last.then_inc(m.qkv_done, 1)
                pe.wait_ge(m.qk_saved, g * 2 + 1)
                for t in range(TB):
                    for c in range(DC):
                        last = pe.matmul(ps[4][:, t * HD:(t + 1) * HD], hT[:, c, t * P:(t + 1) * P], wqkv[:, e, 2, c, :],
                                         start=(c == 0), stop=(c == DC - 1))
                last.then_inc(m.qkv_done, 1)

            def scores(b, h):
                g = b * H + h
                pe.wait_ge(m.qk_saved, g * 2 + 2)
                for t in range(TB):
                    pe.wait_ge(m.exp_done, g * TB + (t + 1))
                    pe.matmul(ps[t][:, 0:(t + 1) * P], qT[:, t * P:(t + 1) * P], kT[:, 0:(t + 1) * P], start=True, stop=False)
                    pe.matmul(ps[t][:, t * P:(t + 1) * P], ident_bf[:, :], mask_bf[:, :], start=False, stop=True).then_inc(m.scores_done, 1)

            def transpose_prob(b, h):
                g = b * H + h
                pe.wait_ge(m.prob_ready, g * TB + TB)
                for k, (bank, tiles) in enumerate(T_GROUPS):
                    if k == 0:
                        pe.wait_ge(m.pT_act_saved, g * 2 + 1)
                    elif k == 1:
                        pe.wait_ge(m.pT_dve_saved, g + 1)
                    else:
                        pe.wait_ge(m.pT_act_saved, g * 2 + 2)
                    at = 0
                    for j in tiles:
                        for t in range(j, TB):
                            last = pe.transpose(ps[bank][:, at:at + P], prob[:, t, j * P:(j + 1) * P], ident[:, :])
                            at += P
                    last.then_inc(m.pT_done, 1)

            def attend(b, h, e):
                g = b * H + h
                pe.wait_ge(m.v_saved, g + 2)
                pe.wait_ge(m.pT_act_saved, g * 2 + 3)
                pe.wait_ge(m.pT_dve_saved, g + 2)
                for j, (row, at) in enumerate(((0, 0), (1, 0), (2, 0), (1, 3 * P))):
                    last = pe.matmul(ps[5][:, j * P:S], v[:, e, j, :], probT[:, row, at:at + S - j * P], start=(j == 0), stop=(j == TB - 1))
                last.then_inc(m.o_done, 1)

            def head(b, h, e, idx, first=False):
                qkv(b, h, e, idx, whole=first)
                if not first:
                    transpose_prob(b, h - 1)
                scores(b, h)
                if not first:
                    attend(b, h - 1, 1 - e)

            transpose_norm(b)
            pe.wait_ge(m.normT_ready, b * (2 * DC) + DC)
            head(b, 0, 0, 0, first=True)
            with pe.Fori(0, H // 2 - 1) as i:
                head(b, i * 2 + 1, 1, i)
                head(b, i * 2 + 2, 0, i + 1)
            head(b, H - 1, 1, H // 2 - 1)
            transpose_prob(b, H - 1)
            attend(b, H - 1, 1)
            pe.wait_ge(m.wo_in, b * 16 + 16)
            pe.wait_ge(m.exp_done, b * (H * TB) + (H * TB + TB))
            pe.wait_ge(m.o_saved, b * H + (H + 2))
            for t in range(TB):
                for h in range(H):
                    last = pe.matmul(ps[t][:, 0:D], oT[:, h, t * P:(t + 1) * P], wo[:, h, :], start=(h == 0), stop=(h == H - 1))
                last.then_inc(m.ao_done, 1)
        @block.scalar
        def _(act):
            act.dma_start(wo[:, :, :], io["wo"].rearrange("(h p) d -> p h d", p=P)).then_inc(m.wo_in, 16)

            def save_norm(b):
                for c in range(DC):
                    act.wait_ge(m.normT_done, b * (2 * DC) + (c + 1))
                    act.activation(hT[:, c, :], ps[4 + c][:, :], ACT.Copy, scale=stats["gains"][:, 2, c:c + 1]).then_inc(m.normT_ready, 1)

            def save_prob(b, h):
                g = b * H + h
                act.wait_ge(m.pT_done, g * 3 + 1)
                act.activation(probT[:, 0, :], ps[6][:, :], ACT.Copy).then_inc(m.pT_act_saved, 1)
                act.wait_ge(m.pT_done, g * 3 + 3)
                act.activation(probT[:, 2, 0:2 * P], ps[6][:, 0:2 * P], ACT.Copy).then_inc(m.pT_act_saved, 1)

            def save_o(b, h):
                act.wait_ge(m.o_done, b * H + (h + 1))
                act.activation(oT[:, h, :], ps[5][:, :], ACT.Copy).then_inc(m.o_saved, 1)

            def head(b, h, first=False):
                g = b * H + h
                for which, (dst, scale) in enumerate(((qT, HD ** -0.5), (kT, 1.0))):
                    act.wait_ge(m.qkv_done, g * 3 + (6 + which + 1))
                    act.activation(dst[:, :], ps[4 + which][:, :], ACT.Copy, scale=scale).then_inc(m.qk_saved, 1)
                if not first:
                    save_prob(b, h - 1)
                for t in range(TB):
                    w = (t + 1) * P
                    act.wait_ge(m.max_ready, g * TB + (t + 1))
                    act.activation(prob[:, t, 0:w], ps[t][:, 0:w], ACT.Exp, bias=nmax[:, t:t + 1], accum_out=rowsum[:, t:t + 1]).then_inc(m.exp_done, 1)
                if not first:
                    save_o(b, h - 1)

            save_norm(b)
            head(b, 0, first=True)
            with act.Fori(0, H - 1) as i:
                head(b, i + 1)
            save_prob(b, H - 1)
            save_o(b, H - 1)

        @block.vector
        def _(dve):
            steps = Tally(per_body=DVE_STEPS)

            def head(b, h, e, next_idx=None, first=False, last=False):
                g = b * H + h
                dve.wait_ge(m.qkv_done, g * 3 + (6 + 3))
                dve.tensor_copy(v[:, e, :, :], ps[4][:, :].rearrange("p (t d) -> p t d", t=TB)).then_inc(m.v_saved, 1)
                if not first:
                    save_prob(b, h - 1)
                for t in range(TB):
                    dve.wait_ge(m.scores_done, g * TB + (t + 1))
                    dve.tensor_reduce(nmax[:, t:t + 1], ps[t][:, 0:(t + 1) * P], op=ALU.max, axis=AX.X, negate=True).then_inc(m.max_ready, 1)
                dve.wait_ge(m.exp_done, g * TB + 2 * TB)
                dve.reciprocal(rinv[:, :], rowsum[:, :]).then_inc(m.rinv_ready, 1)
                if not last:
                    split(b, h + 2, e, next_idx)

            def split(b, h, e, idx, first=False):
                dve.wait_ge(m.wqkv_in[e], b * (8 * H) + (idx * 16 + 16))
                if not first:
                    dve.wait_ge(m.w_hi_ready, b * (H - 1) + (h - 1))
                dve.scalar_tensor_tensor(w_mid[:, :, :, :], wqkv[:, e, 0:2, :, :], SPLIT, wqkv[:, e, 0:2, :, :], ALU.mult, ALU.subtract) \
                   .then_inc(m.w_mid_ready, 1)
                dve.wait_ge(m.w_mid_ready, b * (H - 1) + h)
                dve.scalar_tensor_tensor(w_hi[:, e, :, :, :], wqkv[:, e, 0:2, :, :], SPLIT, w_mid[:, :, :, :], ALU.mult, ALU.subtract) \
                   .then_inc(m.w_hi_ready, 1)

            def save_prob(b, h):
                dve.wait_ge(m.pT_done, (b * H + h) * 3 + 2)
                dve.tensor_copy(probT[:, 1, :], ps[7][:, :]).then_inc(m.pT_dve_saved, 1)

            for t in range(TB):
                dve.bn_stats(bn[:, t, :], x_all[:, b * TB + t, :]).then_inc(m.dve_step, 1)
                steps.more()
            dve.wait_ge(m.dve_step, steps.value(b, steps.n))
            dve.nop(nofuse=True)
            for t in range(TB):
                dve.bn_aggr(mv[:, t, :], bn[:, t, :]).then_inc(m.dve_step, 1)
                steps.more()
            dve.wait_ge(m.dve_step, steps.value(b, steps.n))
            dve.tensor_scalar(arg[:, 0:TB], mv[:, 0:TB, 1], LN_EPS, None, ALU.add).then_inc(m.dve_step, 1)
            steps.more()
            dve.tensor_scalar(arg[:, TB:2 * TB], mv[:, 0:TB, 1], 1.0 + RMS_EPS, RMS_EPS * LN_EPS, ALU.mult, ALU.add).then_inc(m.dve_step, 1)
            steps.more()
            dve.wait_ge(m.dve_step, steps.value(b, steps.n))
            inverse_root(dve, root[:, :], arg[:, :], half[:, :], term[:, :], m.dve_step, steps, b)
            for t in range(TB):
                dve.tensor_scalar(hn[:, t, :], x_all[:, b * TB + t, :], mv[:, t, 0:1], root[:, TB + t:TB + t + 1],
                                  ALU.subtract, ALU.mult).then_inc(m.norm_ready, 1)
            if not (isinstance(b, int) and b == 0):
                dve.wait_ge(m.out_stored, b * 16)
                dve.nop(nofuse=True)
            for t in range(TB):
                dve.tensor_scalar(m.y[:, t, :], x_all[:, b * TB + t, :], mv[:, t, 0:1], root[:, t:t + 1],
                                  ALU.subtract, ALU.mult).then_inc(m.dve_step, 1)
                steps.more()
            y_at = steps.n

            dve.wait_ge(m.normT_ready, b * (2 * DC) + DC)
            dve.scalar_tensor_tensor(hT_mid[:, :, :], hT[:, :, :], SPLIT, hT[:, :, :], ALU.mult, ALU.subtract).then_inc(m.hT_split, 1)
            dve.wait_ge(m.hT_split, 3 * b + 1)
            dve.scalar_tensor_tensor(hT_hi[:, :, :], hT[:, :, :], SPLIT, hT_mid[:, :, :], ALU.mult, ALU.subtract).then_inc(m.hT_split, 1)
            dve.wait_ge(m.hT_split, 3 * b + 2)
            dve.tensor_tensor(hT_lo[:, :, :], hT[:, :, :], hT_hi[:, :, :].bitcast(F32), ALU.subtract).then_inc(m.hT_split, 1)
            split(b, 1, 1, 0, first=True)
            head(b, 0, 0, 1, first=True)
            with dve.Fori(0, H // 2 - 2) as i:
                head(b, i * 2 + 1, 1, i + 1)
                head(b, i * 2 + 2, 0, i + 2)
            head(b, H - 3, 1, H // 2 - 1)
            head(b, H - 2, 0, last=True)
            head(b, H - 1, 1, last=True)
            save_prob(b, H - 1)

            dve.wait_ge(m.dve_step, steps.value(b, y_at))
            for t in range(TB):
                dve.wait_ge(m.ao_done, b * TB + (t + 1))
                dve.tensor_tensor(m.y[:, t, :], m.y[:, t, :], ps[t][:, 0:D], ALU.add).then_inc(m.dve_step, 1)
                steps.more()
            steps.check()


def program(nc, io, out):
    ctx = ExitStack()
    with ctx:
        tile = lambda n, s, d=F32: ctx.enter_context(nc.sbuf_tensor(n, s, d))
        sem = lambda n: ctx.enter_context(nc.semaphore(n))
        ps = [ctx.enter_context(nc.psum_tensor(f"bank{k}", [P, 512], F32)) for k in range(8)]
        x_all = tile("x_all", [P, NT, D])
        consts = (tile("ident", [P, P]), tile("mask_bias", [P, P]), tile("ident_bf", [P, P], BF16), tile("mask_bf", [P, P], BF16))
        stats = {"mean": tile("mean", [P, NT]), "scale": tile("scale", [P, NT + NC]), "gains": tile("gains", [P, 4, DC])}
        fold = {"A": tile("fold_A", [P, MH, DC, MN]), "G": tile("fold_G", [P, MH, NC, MN]), "O": tile("fold_O", [P, MH, NC, D])}
        m = shared(nc, tile, sem)
        setup(nc, io, ps, x_all, fold, stats, consts)
        credits(nc, m)
        memory_attention(nc, m, io, out, ps, x_all, fold, stats, consts, 0, beside=False)
        causal_attention(nc, m, io, ps, x_all, stats, consts, 0, "first")
        with nc.Fori(0, B - 1) as i:
            b = i + 1
            memory_attention(nc, m, io, out, ps, x_all, fold, stats, consts, b, beside=True)
            causal_attention(nc, m, io, ps, x_all, stats, consts, b, "rest")
        experts_alone(nc, m, ps, io, out, x_all, stats, consts, B - 1)


def kernel(**inputs):
    import numpy as np
    import concourse.bacc as bacc
    from concourse.bass_utils import run_bass_kernel_spmd as run

    at = {k: np.asarray(v) for k, v in inputs.items()}
    a, f = "L0_attn_", "L0_ffn_"
    laid = {
        "hidden": at[a + "hidden"], "memory": at[a + "memory"],
        "wq_m": at[a + "Wq"], "wkT": at[a + "Wk"].T, "wvT": at[a + "Wv"].T, "woT": at[a + "Wo"].T,
        "log_beta": at[a + "log_beta"], "g_mem": at[a + "g_mem"], "b_mem": at[a + "b_mem"],
        "gains": np.stack([at[n].reshape(DC, P).T for n in (a + "g_state", a + "b_state", f + "ln1_w", f + "ln2_w")], axis=1),
    }
    by_head = [at[f + n].reshape(DC, P, H, HD).transpose(2, 1, 0, 3) for n in ("wq", "wk", "wv")]
    rows = [np.concatenate([at[f + s_w], at[f + e_w].reshape(E * EI, D)]) for s_w, e_w in (("sg_w", "eg_w"), ("su_w", "eu_w"))]
    by_item = [r.reshape(ITEMS, ITEM, DC, P).transpose(0, 3, 2, 1) for r in rows]
    down = np.concatenate([at[f + "sd_w"].T, at[f + "ed_w"].transpose(0, 2, 1).reshape(E * EI, D)]).reshape(ITEMS, ITEM, D)
    laid.update({
        "wqkv": np.stack(by_head, axis=2), "wo": at[f + "wo"],
        "gate": at[f + "gate_w"].T, "wgu": np.stack(by_item, axis=2), "wd": down,
    })
    laid = {k: np.ascontiguousarray(v) for k, v in laid.items()}
    nc = bacc.Bacc("TRN2", target_bir_lowering=False, num_devices=1)
    io = {k: nc.dram_tensor("in_" + k, v.shape, mybir.dt.from_np(v.dtype), kind="ExternalInput").ap() for k, v in laid.items()}
    out = nc.dram_tensor("out", (B, S, D), F32, kind="ExternalOutput").ap()
    program(nc, io, out)
    return run(nc, [{"in_" + k: v for k, v in laid.items()}], core_ids=[0]).results[0]["out"]
```
